# Optimizing a Trainium2 kernel written in Bass

```python
import numpy as np
import jax
import jax.numpy as jnp

def _softmax(x, axis=-1):
    return jax.nn.softmax(x, axis=axis)

def _gelu(x):
    return jax.nn.gelu(x, approximate=True)

def _silu(x):
    return jax.nn.silu(x)

def _sigmoid(x):
    return jax.nn.sigmoid(x)

def _layernorm(x, axis=-1, eps=1e-05):
    m = jnp.mean(x, axis=axis, keepdims=True)
    v = jnp.var(x, axis=axis, keepdims=True)
    return (x - m) / jnp.sqrt(v + eps)

def _scatter_add(tgt, idx, src, axis=0):
    return tgt.at[idx].add(src)

def _segment_sum(src, seg, n):
    return jax.ops.segment_sum(src, seg, n)
kernel_name = 'mk_flamingo_gated_d2_seqx_r2_4098f0'

def setup_inputs(seed: int=0):
    np.random.seed(seed)
    _w = jnp.asarray

    def _rec_inputs():
        import jax
        import jax.numpy as jnp
        _rk = jax.random.key(seed)
        x = -0.0002928 + 1 * jax.random.normal(jax.random.fold_in(_rk, 1), (8, 100, 512), jnp.float32)
        _lenS = 100 - jax.random.randint(jax.random.fold_in(_rk, 7), (8,), 0, max(1, 100 // 4) + 1, jnp.int32)
        _lenS2 = 722 - jax.random.randint(jax.random.fold_in(_rk, 8), (8,), 0, max(1, 722 // 4) + 1, jnp.int32)
        _ctx_1024P = jax.random.normal(jax.random.fold_in(_rk, 11), (8, 16, 512), jnp.float32)
        _ctx_1024c = jax.random.dirichlet(jax.random.fold_in(_rk, 511), 0.3 * jnp.ones((16,), jnp.float32), (8, 722))
        _ctx_1024t = jnp.einsum('bsk,bkd->bsd', _ctx_1024c, _ctx_1024P)
        _ctx_1024t = _ctx_1024t * jax.lax.rsqrt(jnp.mean(jnp.square(_ctx_1024t)) + 1e-12) * 0.953939
        ctx_1024 = -1.39393e-06 + 0.999914 * (_ctx_1024t + 0.3 * jax.random.normal(jax.random.fold_in(_rk, 611), (8, 722, 512), jnp.float32))
        _validS = jnp.arange(100)[None, :] < _lenS[:, None]
        _validS2 = jnp.arange(722)[None, :] < _lenS2[:, None]
        _causal = jnp.tril(jnp.ones((100, 100), dtype=bool))
        mask_Bx1xSxS2_ik0 = jnp.where(jnp.broadcast_to(_validS2[:, None, None, :], (8, 1, 100, 722)), 0, 1).astype(jnp.int32)
        _g = jax.random.normal(jax.random.fold_in(_rk, 9001), (2, 2), jnp.float32)
        _g = jnp.sign(_g) * jnp.maximum(jnp.abs(_g), 1.0) + (_g == 0) * 1.0
        g_xattn = _g[0]
        g_ffn = _g[1]
        return (x, ctx_1024, mask_Bx1xSxS2_ik0, g_xattn, g_ffn)
    x, ctx_1024, mask_Bx1xSxS2_ik0, g_xattn, g_ffn = _rec_inputs()

    def _L0_xattn_setup():
        import jax, jax.numpy as jnp
        import numpy as np
        D_MODEL = 512
        H = 16
        D_K = D_MODEL // H
        B = 2
        S = 1024

        def _split_heads(x):
            b, s, _ = x.shape
            return x.reshape(b, s, H, D_K).transpose(0, 2, 1, 3)
        key = jax.random.key(seed)
        ks = jax.random.split(key, 11)
        scale = 1.0 / np.sqrt(D_MODEL)
        inp = {'query': jax.random.normal(ks[0], (B, S, D_MODEL), jnp.float32), 'key_in': jax.random.normal(ks[1], (B, S, D_MODEL), jnp.float32), 'value': jax.random.normal(ks[2], (B, S, D_MODEL), jnp.float32), 'mask': jnp.tril(jnp.ones((S, S), jnp.int32))[None, None, :, :].repeat(B, axis=0), 'w_q': jax.random.normal(ks[3], (D_MODEL, D_MODEL), jnp.float32) * scale, 'b_q': jax.random.normal(ks[4], (D_MODEL,), jnp.float32) * 0.01, 'w_k': jax.random.normal(ks[5], (D_MODEL, D_MODEL), jnp.float32) * scale, 'b_k': jax.random.normal(ks[6], (D_MODEL,), jnp.float32) * 0.01, 'w_v': jax.random.normal(ks[7], (D_MODEL, D_MODEL), jnp.float32) * scale, 'b_v': jax.random.normal(ks[8], (D_MODEL,), jnp.float32) * 0.01, 'w_out': jax.random.normal(ks[9], (D_MODEL, D_MODEL), jnp.float32) * scale, 'b_out': jax.random.normal(ks[10], (D_MODEL,), jnp.float32) * 0.01}
        return inp
    _L0_xattn_all = _L0_xattn_setup()
    _L0_xattn_in = {k: v for k, v in _L0_xattn_all.items() if k in ('w_q', 'b_q', 'w_k', 'b_k', 'w_v', 'b_v', 'w_out', 'b_out')}
    del _L0_xattn_all

    def _L0_ffn_setup():
        import jax, jax.numpy as jnp
        import numpy as np
        TOP_K = 8
        CAPACITY = 256

        def _silu(x):
            return x * jax.nn.sigmoid(x)
        key = jax.random.key(seed)
        ks = jax.random.split(key, 7)
        B, S, H, E, I, Is = (2, 512, 512, 64, 256, 1024)
        s = 0.05
        return {'hidden_states': jax.random.normal(ks[0], (B, S, H), jnp.float32), 'gate_w': jax.random.normal(ks[1], (H, E), jnp.float32) * s, 'shared_gate_w': jax.random.normal(ks[2], (H, 1), jnp.float32) * s, 'shared_gate_up_w': jax.random.normal(ks[3], (H, 2 * Is), jnp.float32) * s, 'shared_down_w': jax.random.normal(ks[4], (Is, H), jnp.float32) * s, 'expert_gate_up_w': jax.random.normal(ks[5], (E, H, 2 * I), jnp.float32) * s, 'expert_down_w': jax.random.normal(ks[6], (E, I, H), jnp.float32) * s}
    _L0_ffn_all = _L0_ffn_setup()
    _L0_ffn_in = {k: v for k, v in _L0_ffn_all.items() if k in ('gate_w', 'shared_gate_w', 'shared_gate_up_w', 'shared_down_w', 'expert_gate_up_w', 'expert_down_w')}
    del _L0_ffn_all

    def _L1_xattn_setup():
        import jax, jax.numpy as jnp
        import numpy as np
        H = 16

        def _split_heads(x):
            B, S, D = x.shape
            return x.reshape(B, S, H, D // H).transpose(0, 2, 1, 3)
        key = jax.random.key(seed)
        ks = jax.random.split(key, 6)
        B, Q, K, D = (2, 1024, 1024, 512)
        s = 0.02
        return {'query_tokens': jax.random.normal(ks[0], (B, Q, D), jnp.float32), 'key_value_tokens': jax.random.normal(ks[1], (B, K, D), jnp.float32), 'Wq': jax.random.normal(ks[2], (D, D), jnp.float32) * s, 'bq': jnp.zeros((D,), jnp.float32), 'Wk': jax.random.normal(ks[3], (D, D), jnp.float32) * s, 'bk': jnp.zeros((D,), jnp.float32), 'Wv': jax.random.normal(ks[4], (D, D), jnp.float32) * s, 'bv': jnp.zeros((D,), jnp.float32), 'Wo': jax.random.normal(ks[5], (D, D), jnp.float32) * s, 'bo': jnp.zeros((D,), jnp.float32)}
    _L1_xattn_all = _L1_xattn_setup()
    _L1_xattn_in = {k: v for k, v in _L1_xattn_all.items() if k in ('Wq', 'bq', 'Wk', 'bk', 'Wv', 'bv', 'Wo', 'bo')}
    del _L1_xattn_all

    def _L1_ffn_setup():
        import jax, jax.numpy as jnp
        import numpy as np
        TOP_K = 2

        def _mlp(x, w1, b1, w2, b2):
            h = jax.nn.gelu(jnp.einsum('bsd,di->bsi', x, w1) + b1)
            return jnp.einsum('bsi,id->bsd', h, w2) + b2
        key = jax.random.key(seed)
        ks = jax.random.split(key, 8)
        B, S, D, I, E = (2, 1024, 512, 2048, 8)
        s_in = 1.0 / np.sqrt(D)
        s_mid = 1.0 / np.sqrt(I)
        return {'x': jax.random.normal(ks[0], (B, S, D), jnp.float32), 'gate_w': jax.random.normal(ks[1], (D, E), jnp.float32) * s_in, 'gate_b': jnp.zeros((E,), jnp.float32), 'sh_w1': jax.random.normal(ks[2], (D, I), jnp.float32) * s_in, 'sh_b1': jnp.zeros((I,), jnp.float32), 'sh_w2': jax.random.normal(ks[3], (I, D), jnp.float32) * s_mid, 'sh_b2': jnp.zeros((D,), jnp.float32), 'ew1': jax.random.normal(ks[4], (E, D, I), jnp.float32) * s_in, 'eb1': jnp.zeros((E, I), jnp.float32), 'ew2': jax.random.normal(ks[5], (E, I, D), jnp.float32) * s_mid, 'eb2': jnp.zeros((E, D), jnp.float32)}
    _L1_ffn_all = _L1_ffn_setup()
    _L1_ffn_in = {k: v for k, v in _L1_ffn_all.items() if k in ('gate_w', 'gate_b', 'sh_w1', 'sh_b1', 'sh_w2', 'sh_b2', 'ew1', 'eb1', 'ew2', 'eb2')}
    del _L1_ffn_all
    return {'x': x, 'ctx_1024': ctx_1024, 'mask_Bx1xSxS2_ik0': mask_Bx1xSxS2_ik0, 'g_xattn': g_xattn, 'g_ffn': g_ffn, 'L0_xattn_w_q': _L0_xattn_in['w_q'], 'L0_xattn_b_q': _L0_xattn_in['b_q'], 'L0_xattn_w_k': _L0_xattn_in['w_k'], 'L0_xattn_b_k': _L0_xattn_in['b_k'], 'L0_xattn_w_v': _L0_xattn_in['w_v'], 'L0_xattn_b_v': _L0_xattn_in['b_v'], 'L0_xattn_w_out': _L0_xattn_in['w_out'], 'L0_xattn_b_out': _L0_xattn_in['b_out'], 'L0_ffn_gate_w': _L0_ffn_in['gate_w'], 'L0_ffn_shared_gate_w': _L0_ffn_in['shared_gate_w'], 'L0_ffn_shared_gate_up_w': _L0_ffn_in['shared_gate_up_w'], 'L0_ffn_shared_down_w': _L0_ffn_in['shared_down_w'], 'L0_ffn_expert_gate_up_w': _L0_ffn_in['expert_gate_up_w'], 'L0_ffn_expert_down_w': _L0_ffn_in['expert_down_w'], 'L1_xattn_Wq': _L1_xattn_in['Wq'], 'L1_xattn_bq': _L1_xattn_in['bq'], 'L1_xattn_Wk': _L1_xattn_in['Wk'], 'L1_xattn_bk': _L1_xattn_in['bk'], 'L1_xattn_Wv': _L1_xattn_in['Wv'], 'L1_xattn_bv': _L1_xattn_in['bv'], 'L1_xattn_Wo': _L1_xattn_in['Wo'], 'L1_xattn_bo': _L1_xattn_in['bo'], 'L1_ffn_gate_w': _L1_ffn_in['gate_w'], 'L1_ffn_gate_b': _L1_ffn_in['gate_b'], 'L1_ffn_sh_w1': _L1_ffn_in['sh_w1'], 'L1_ffn_sh_b1': _L1_ffn_in['sh_b1'], 'L1_ffn_sh_w2': _L1_ffn_in['sh_w2'], 'L1_ffn_sh_b2': _L1_ffn_in['sh_b2'], 'L1_ffn_ew1': _L1_ffn_in['ew1'], 'L1_ffn_eb1': _L1_ffn_in['eb1'], 'L1_ffn_ew2': _L1_ffn_in['ew2'], 'L1_ffn_eb2': _L1_ffn_in['eb2']}

def reference(x, ctx_1024, mask_Bx1xSxS2_ik0, g_xattn, g_ffn, L0_xattn_w_q, L0_xattn_b_q, L0_xattn_w_k, L0_xattn_b_k, L0_xattn_w_v, L0_xattn_b_v, L0_xattn_w_out, L0_xattn_b_out, L0_ffn_gate_w, L0_ffn_shared_gate_w, L0_ffn_shared_gate_up_w, L0_ffn_shared_down_w, L0_ffn_expert_gate_up_w, L0_ffn_expert_down_w, L1_xattn_Wq, L1_xattn_bq, L1_xattn_Wk, L1_xattn_bk, L1_xattn_Wv, L1_xattn_bv, L1_xattn_Wo, L1_xattn_bo, L1_ffn_gate_w, L1_ffn_gate_b, L1_ffn_sh_w1, L1_ffn_sh_b1, L1_ffn_sh_w2, L1_ffn_sh_b2, L1_ffn_ew1, L1_ffn_eb1, L1_ffn_ew2, L1_ffn_eb2):
    import jax
    import jax.numpy as jnp

    def _L0_xattn_ref(query, key_in, value, mask, w_q, b_q, w_k, b_k, w_v, b_v, w_out, b_out):
        import jax, jax.numpy as jnp
        import numpy as np
        D_MODEL = 512
        H = 16
        D_K = D_MODEL // H
        B = 2
        S = 1024

        def _split_heads(x):
            b, s, _ = x.shape
            return x.reshape(b, s, H, D_K).transpose(0, 2, 1, 3)
        q = _split_heads(query @ w_q.T + b_q)
        k = _split_heads(key_in @ w_k.T + b_k)
        v = _split_heads(value @ w_v.T + b_v)
        scores = jnp.einsum('bhqd,bhkd->bhqk', q, k) / jnp.sqrt(jnp.float32(D_K))
        scores = jnp.where(mask == 0, jnp.float32(-1000000000.0), scores)
        attn = jax.nn.softmax(scores, axis=-1)
        out = jnp.einsum('bhqk,bhkd->bhqd', attn, v)
        out = out.transpose(0, 2, 1, 3).reshape(query.shape[0], -1, D_MODEL)
        return out @ w_out.T + b_out

    def _L0_ffn_ref(hidden_states, gate_w, shared_gate_w, shared_gate_up_w, shared_down_w, expert_gate_up_w, expert_down_w):
        import jax, jax.numpy as jnp
        import numpy as np
        TOP_K = 8
        CAPACITY = 256

        def _silu(x):
            return x * jax.nn.sigmoid(x)
        B, S, H = hidden_states.shape
        x = hidden_states.reshape(-1, H)
        T = x.shape[0]
        E = gate_w.shape[1]
        Is = shared_gate_up_w.shape[1] // 2
        I = expert_gate_up_w.shape[2] // 2
        gu = x @ shared_gate_up_w
        shared = _silu(gu[:, :Is]) * gu[:, Is:] @ shared_down_w
        shared = shared * jax.nn.sigmoid(x @ shared_gate_w)
        logits = x @ gate_w
        probs = jax.nn.softmax(logits.astype(jnp.float32), axis=-1)
        w, idx = jax.lax.top_k(probs, TOP_K)
        w = (w / jnp.sum(w, axis=-1, keepdims=True)).astype(x.dtype)
        e_flat = idx.reshape(-1)
        w_flat = w.reshape(-1)
        A = e_flat.shape[0]
        tok = jnp.arange(A) // TOP_K
        onehot = jax.nn.one_hot(e_flat, E, dtype=jnp.int32)
        pos = jnp.take_along_axis(jnp.cumsum(onehot, axis=0) - 1, e_flat[:, None], axis=1)[:, 0]
        slot = jnp.minimum(pos, CAPACITY)
        buf = jnp.zeros((E, CAPACITY + 1, H), x.dtype).at[e_flat, slot].set(x[tok])
        gu_e = jnp.einsum('ech,ehf->ecf', buf, expert_gate_up_w)
        act = _silu(gu_e[..., :I]) * gu_e[..., I:]
        out_e = jnp.einsum('eci,eih->ech', act, expert_down_w)
        y = out_e[e_flat, slot] * w_flat[:, None]
        y = jnp.where((pos < CAPACITY)[:, None], y, jnp.zeros_like(y))
        y = y.reshape(T, TOP_K, H).sum(axis=1)
        return (y + shared).reshape(B, S, H)

    def _L1_xattn_ref(query_tokens, key_value_tokens, Wq, bq, Wk, bk, Wv, bv, Wo, bo):
        import jax, jax.numpy as jnp
        import numpy as np
        H = 16

        def _split_heads(x):
            B, S, D = x.shape
            return x.reshape(B, S, H, D // H).transpose(0, 2, 1, 3)
        q = _split_heads(query_tokens @ Wq + bq)
        k = _split_heads(key_value_tokens @ Wk + bk)
        v = _split_heads(key_value_tokens @ Wv + bv)
        hd = q.shape[-1]
        scores = jnp.einsum('bhqd,bhkd->bhqk', q, k) / jnp.sqrt(jnp.asarray(hd, q.dtype))
        probs = jax.nn.softmax(scores, axis=-1)
        ctx = jnp.einsum('bhqk,bhkd->bhqd', probs, v)
        B, _, Q, _ = ctx.shape
        ctx = ctx.transpose(0, 2, 1, 3).reshape(B, Q, H * hd)
        return ctx @ Wo + bo

    def _L1_ffn_ref(x, gate_w, gate_b, sh_w1, sh_b1, sh_w2, sh_b2, ew1, eb1, ew2, eb2):
        import jax, jax.numpy as jnp
        import numpy as np
        TOP_K = 2

        def _mlp(x, w1, b1, w2, b2):
            h = jax.nn.gelu(jnp.einsum('bsd,di->bsi', x, w1) + b1)
            return jnp.einsum('bsi,id->bsd', h, w2) + b2
        E = ew1.shape[0]
        router_probs = jax.nn.softmax(jnp.einsum('bsd,de->bse', x, gate_w) + gate_b, axis=-1)
        expert_values, expert_indices = jax.lax.top_k(router_probs, k=TOP_K)
        expert_values = expert_values / (jnp.sum(expert_values, axis=-1, keepdims=True) + 1e-09)
        h = jax.nn.gelu(jnp.einsum('bsd,edi->bsei', x, ew1) + eb1)
        all_outputs = jnp.einsum('bsei,eid->bsed', h, ew2) + eb2
        one_hot = jax.nn.one_hot(expert_indices, E, dtype=x.dtype)
        weights_E = (one_hot * expert_values[..., None]).sum(axis=2)
        moe_out = jnp.einsum('bse,bsed->bsd', weights_E, all_outputs)
        return x + _mlp(x, sh_w1, sh_b1, sh_w2, sh_b2) + moe_out
    x = x + jnp.tanh(g_xattn[0]) * _L0_xattn_ref(_layernorm(x, axis=-1), ctx_1024, ctx_1024, mask_Bx1xSxS2_ik0, L0_xattn_w_q, L0_xattn_b_q, L0_xattn_w_k, L0_xattn_b_k, L0_xattn_w_v, L0_xattn_b_v, L0_xattn_w_out, L0_xattn_b_out)
    x = x + jnp.tanh(g_ffn[0]) * _L0_ffn_ref(_layernorm(x, axis=-1), L0_ffn_gate_w, L0_ffn_shared_gate_w, L0_ffn_shared_gate_up_w, L0_ffn_shared_down_w, L0_ffn_expert_gate_up_w, L0_ffn_expert_down_w)
    x = x + jnp.tanh(g_xattn[1]) * _L1_xattn_ref(_layernorm(x, axis=-1), ctx_1024, L1_xattn_Wq, L1_xattn_bq, L1_xattn_Wk, L1_xattn_bk, L1_xattn_Wv, L1_xattn_bv, L1_xattn_Wo, L1_xattn_bo)
    x = x + jnp.tanh(g_ffn[1]) * _L1_ffn_ref(_layernorm(x, axis=-1), L1_ffn_gate_w, L1_ffn_gate_b, L1_ffn_sh_w1, L1_ffn_sh_b1, L1_ffn_sh_w2, L1_ffn_sh_b2, L1_ffn_ew1, L1_ffn_eb1, L1_ffn_ew2, L1_ffn_eb2)
    return x

_drawn_inputs = setup_inputs


def setup_inputs(seed=0):
    import zlib

    import numpy as np

    out = dict(_drawn_inputs(seed))
    spreads = {'g_ffn': (-1.0, 0.2),
     'L1_xattn_bq': (0.0, 1.292),
     'L1_xattn_bk': (0.0, 2.0),
     'L1_xattn_bv': (0.0, 0.1),
     'L1_xattn_bo': (0.0, 0.1),
     'L1_ffn_gate_b': (0.0, 0.1),
     'L1_ffn_sh_b1': (0.0, 0.1),
     'L1_ffn_sh_b2': (0.0, 0.1),
     'L1_ffn_eb1': (0.0, 0.1),
     'L1_ffn_eb2': (0.0, 0.1)}
    factors = {'L0_xattn_b_k': 64.0, 'L0_xattn_b_q': 3.09}
    for name, (base, spread) in spreads.items():
        noise = np.random.default_rng([zlib.crc32(name.encode()), seed]).standard_normal(out[name].shape)
        drawn = base * np.exp(spread * noise) if base else spread * noise
        out[name] = jnp.asarray(drawn.astype(out[name].dtype))
    for name, factor in factors.items():
        out[name] = (out[name] * factor).astype(out[name].dtype)
    return out
```

```python
import numpy as np
import concourse.bass as bass
from concourse import mybir
from contextlib import ExitStack

F32 = mybir.dt.float32
I32 = mybir.dt.int32
U32 = mybir.dt.uint32
ALU = mybir.AluOpType
ACT = mybir.ActivationFunctionType
AX = mybir.AxisListType

P = 128
B, S, D = 8, 100, 512
SK = 722
H, DH = 16, 32
DC = D // P
HPC = P // DH
T = B * S
TH = T // 2
KH = SK // 2
KC = -(-SK // P)
KTAIL = SK - (KC - 1) * P
NPIECE = 2 * DC + KC
E0, K0, CAP, I0, IS0 = 64, 8, 256, 256, 1024
E1, K1, I1 = 8, 2, 2048
SLOTS0 = E0 * CAP
TILES1 = (T * K1 + E1 * (P - 1)) // P
SLOTS1 = TILES1 * P
EPS = 1e-5
MASKED = -1.0e30


class Env:
    pass


def layer_norm(nc, env, with_rows, start_acc):
    with ExitStack() as cx:
        def sb(n, s):
            return cx.enter_context(nc.sbuf_tensor(env.name(n), s, F32))

        def sem(n):
            return env.semaphore(n)

        x, xnT, ident = env.x, env.xnT, env.ident
        stats = sb("ln_stats", [S, B, 6])
        mv = sb("ln_mean_var", [S, B, 2])
        std = sb("ln_std", [S, B])
        rstd = sb("ln_rstd", [S, B])
        xn = env.acc if start_acc else sb("ln_xn", [S, B, D])
        pT = [cx.enter_context(nc.psum_tensor(env.name(f"ln_pT{n}"), [P, DC, S], F32)) for n in range(2)]
        stats_done, var_done, std_done, rstd_done = sem("stats_done"), sem("var_done"), sem("std_done"), sem("rstd_done")
        xn_done, turned, copied, rows_out = sem("xn_done"), sem("turned"), sem("copied"), sem("rows_out")
        with nc.Block() as block:
            @block.vector
            def _(dve):
                for t in range(B):
                    dve.bn_stats(stats[:, t, :], x[:, t, :]).then_inc(stats_done, 1)
                for t in range(B):
                    dve.wait_ge(stats_done, t + 1)
                    dve.bn_aggr(mv[:, t, :], stats[:, t, :]).then_inc(var_done, 1)
                dve.wait_ge(var_done, B)
                dve.tensor_scalar(stats[:, :, 0], mv[:, :, 1], EPS, None, ALU.add).then_inc(var_done, 1)
                dve.wait_ge(std_done, 1)
                dve.reciprocal(rstd[:, :], std[:, :]).then_inc(rstd_done, 1)
                dve.wait_ge(rstd_done, 1)
                for t in range(B):
                    dve.tensor_scalar(xn[:, t, :], x[:, t, :], mv[:, t, 0:1], rstd[:, t:t + 1],
                                      ALU.subtract, ALU.mult).then_inc(xn_done, 1)

            @block.scalar
            def _(act):
                act.wait_ge(var_done, B + 1)
                act.activation(std[:, :], stats[:, :, 0], ACT.Sqrt).then_inc(std_done, 1)
                for t in range(B):
                    act.wait_ge(turned, t + 1)
                    act.activation(xnT[:, :, t * S:(t + 1) * S], pT[t % 2][:, :, :], ACT.Copy).then_inc(copied, 1)

            @block.tensor
            def _(pe):
                for t in range(B):
                    pe.wait_ge(xn_done, t + 1)
                    if t >= 2:
                        pe.wait_ge(copied, t - 1)
                    for c in range(DC):
                        last = pe.transpose(pT[t % 2][:, c, :], xn[:, t, c * P:(c + 1) * P], ident[0:S, 0:S])
                    last.then_inc(turned, 1)

            @block.sync
            def _(sp):
                if with_rows:
                    for t in range(B):
                        sp.wait_ge(xn_done, t + 1)
                        sp.dma_start(env.xn_rows[t * S:(t + 1) * S, :], xn[:, t, :]).then_inc(rows_out, 16)
                    sp.wait_ge(rows_out, 16 * B)


def attention(nc, env, layer, masked, w_q, b_q, w_k, b_k, w_v, b_v, w_o, b_o):
    with ExitStack() as cx:
        def sb(n, s, dt=F32):
            return cx.enter_context(nc.sbuf_tensor(env.name(n), s, dt))

        def sem(n):
            return env.semaphore(n)

        x, xnT, ident = env.x, env.xnT, env.ident
        wk, wv, wo = sb("wk", [P, DC, D]), sb("wv", [P, DC, D]), sb("wo", [P, DC, D])
        bq, bk, bv, bo = sb("bq", [P, DC]), sb("bk", [P, DC]), sb("bv", [P, DC]), sb("bo", [S, D])
        qT = sb("qT", [P, DC, T])
        q_done = sem("q_done")

        with ExitStack() as cq:
            wq = cq.enter_context(nc.sbuf_tensor(env.name("wq"), [P, DC, D], F32))
            pq = [cq.enter_context(nc.psum_tensor(env.name(f"pq{n}"), [P, TH], F32)) for n in range(2)]
            wq_in, q_mm = (env.semaphore(n) for n in ("wq_in", "q_mm"))
            w_in = env.semaphore("w_in")
            with nc.Block() as block:
                @block.sync
                def _(sp):
                    sp.dma_start(wq[:, :, :], w_q).then_inc(wq_in, 16)
                    sp.dma_start(bq[:, :], b_q).then_inc(wq_in, 16)
                    for dst, src in ((wk, w_k), (wv, w_v), (wo, w_o)):
                        sp.dma_start(dst[:, :, :], src).then_inc(w_in, 16)
                    sp.dma_start(bk[:, :], b_k).then_inc(w_in, 16)
                    sp.dma_start(bv[:, :], b_v).then_inc(w_in, 16)
                    sp.dma_start(bo[:, :], b_o.broadcast_to([S, D])).then_inc(w_in, 16)
                    sp.wait_ge(w_in, 6 * 16)

                @block.tensor
                def _(pe):
                    pe.wait_ge(wq_in, 32)
                    for n in range(2 * DC):
                        m, half = n // 2, n % 2
                        if n >= 2:
                            pe.wait_ge(q_done, n - 1)
                        for c in range(DC):
                            last = pe.matmul(pq[n % 2][:, :], wq[:, c, m * P:(m + 1) * P],
                                             xnT[:, c, half * TH:(half + 1) * TH], start=c == 0, stop=c == DC - 1)
                        last.then_inc(q_mm, 1)

                @block.vector
                def _(dve):
                    dve.wait_ge(wq_in, 32)
                    for n in range(2 * DC):
                        m, half = n // 2, n % 2
                        dve.wait_ge(q_mm, n + 1)
                        dve.tensor_scalar(qT[:, m, half * TH:(half + 1) * TH], pq[n % 2][:, :], bq[:, m:m + 1],
                                          float(DH) ** -0.5, ALU.add, ALU.mult).then_inc(q_done, 1)

        ctx = [sb(f"ctx{p}", [P, DC, SK]) for p in range(2)]
        kT = [sb(f"kT{p}", [P, DC, SK]) for p in range(2)]
        v = [sb(f"v{p}", [P, KC, D]) for p in range(2)]
        qz = [sb(f"qz{p}", [P, DC, HPC, S]) for p in range(2)]
        probs = [sb(f"probs{p}", [S, KC * P]) for p in range(2)]
        pTs = sb("pTs", [P, 2, HPC, KC, S])
        aoT = sb("aoT", [P, DC, S])
        stat = sb("stat", [S, H, 4])
        tmp = sb("res_tmp", [S, D])
        ps = [cx.enter_context(nc.psum_tensor(env.name(f"ps{n}"), [P, 2, 512], F32)) for n in range(2)]
        pt = cx.enter_context(nc.psum_tensor(env.name("pt"), [P, 2, 512], F32))
        pp = cx.enter_context(nc.psum_tensor(env.name("pp"), [P, 512], F32))
        po = cx.enter_context(nc.psum_tensor(env.name("po"), [P, 512], F32))
        if masked:
            mraw = [sb(f"mraw{p}", [S, SK], I32) for p in range(2)]
            madd = [sb(f"madd{p}", [S, 2, KH]) for p in range(2)]
            mask_in = [sem(f"mask_in{p}") for p in range(2)]
            mask_ready = sem("mask_ready")
        ctx_in = [sem(f"ctx_in{p}") for p in range(2)]
        zeroed, zeroed_v = sem("zeroed"), sem("zeroed_v")
        q_ready = sem("q_ready")
        piece_mm, piece_out = sem("piece_mm"), sem("piece_out")
        s_mm, max_raw, max_ready, exp_done = sem("s_mm"), sem("max_raw"), sem("max_ready"), sem("exp_done")
        recip_done, norm_done = sem("recip_done"), sem("norm_done")
        t_mm, t_out, pv_mm, ao_ready = sem("t_mm"), sem("t_out"), sem("pv_mm"), sem("ao_ready")
        o_mm, o_biased, res_done = sem("o_mm"), sem("o_biased"), sem("res_done")
        passed = sem("passed")
        NG = H // HPC

        def pieces(pe, n0, p):
            def piece(k):
                if not isinstance(n0, int) or n0 + k > 0:
                    pe.wait_ge(piece_out, n0 + k)
                for c in range(DC):
                    if k < 2 * DC:
                        m, half = k // 2, k % 2
                        last = pe.matmul(pp[:, 0:KH], wk[:, c, m * P:(m + 1) * P],
                                         ctx[p][:, c, half * KH:(half + 1) * KH], start=c == 0, stop=c == DC - 1)
                    else:
                        kc = k - 2 * DC
                        n = P if kc < KC - 1 else KTAIL
                        last = pe.matmul(pp[0:n, :], ctx[p][:, c, kc * P:kc * P + n], wv[:, c, :],
                                         start=c == 0, stop=c == DC - 1)
                last.then_inc(piece_mm, 1)
            return piece

        def pieces_out(dve, n0, p):
            def piece(k):
                dve.wait_ge(piece_mm, n0 + k + 1)
                if k < 2 * DC:
                    m, half = k // 2, k % 2
                    dve.tensor_scalar(kT[p][:, m, half * KH:(half + 1) * KH], pp[:, 0:KH], bk[:, m:m + 1], None,
                                      ALU.add).then_inc(piece_out, 1)
                else:
                    kc = k - 2 * DC
                    n = P if kc < KC - 1 else KTAIL
                    dve.tensor_copy(v[p][0:n, kc, :], pp[0:n, :]).then_inc(piece_out, 1)
            return piece

        def over_batches(engine, body):
            with engine.Fori(0, B // 2 - 1) as i:
                for p in range(2):
                    body(i * 2 + p, i, p, True)
            for p in range(2):
                body(B - 2 + p, B // 2 - 1, p, p == 0)

        with nc.Block() as block:
            @block.sync
            def _(sp):
                for p in range(2):
                    sp.dma_start(ctx[p][:, :, :], env.ctxT[p]).then_inc(ctx_in[p], 16)
                    if masked:
                        sp.dma_start(mraw[p][:, :], env.mask[p]).then_inc(mask_in[p], 16)
                with sp.Fori(0, B // 2 - 1) as i:
                    for p in range(2):
                        b = i * 2 + p
                        sp.wait_ge(piece_mm, b * NPIECE + NPIECE)
                        sp.dma_start(ctx[p][:, :, :], env.ctxT[bass.ds(b + 2, 1), :, :, :]
                                     .rearrange("a p c k -> (a p) c k")).then_inc(ctx_in[p], 16)
                        if masked:
                            sp.wait_ge(mask_ready, b + 1)
                            sp.dma_start(mraw[p][:, :], env.mask[bass.ds(b + 2, 1), :, :]
                                         .rearrange("a q k -> (a q) k")).then_inc(mask_in[p], 16)

            @block.gpsimd
            def _(pool):
                for p in range(2):
                    pool.memset(qz[p][:, :, :, :], 0.0).then_inc(zeroed, 1)
                    pool.memset(probs[p][:, SK:], 0.0).then_inc(zeroed, 1)
                pool.wait_ge(zeroed, 4)

                def prepare(b, i, p):
                    for j in range(HPC):
                        rows = slice(j * DH, (j + 1) * DH)
                        src = qT[rows, :, bass.ds(b * S, S)] if not isinstance(b, int) else qT[rows, :, b * S:(b + 1) * S]
                        pool.tensor_copy(qz[p][rows, :, j, :], src).then_inc(q_ready, 1)
                        pool.wait_ge(q_ready, b * HPC + j + 1)
                        pool.sem_inc(passed, 1)
                    if masked:
                        pool.wait_ge(mask_in[p], i * 16 + 16)
                        pool.sem_inc(passed, 1)
                        pool.tensor_scalar(madd[p][:, :, :], mraw[p][:, :].rearrange("q (h k) -> q h k", h=2), 0.0,
                                           MASKED, ALU.is_equal, ALU.mult).then_inc(mask_ready, 1)
                        pool.wait_ge(mask_ready, b + 1)
                        pool.sem_inc(passed, 1)
                for p in range(2):
                    prepare(p, 0, p)
                with pool.Fori(1, B // 2) as i:
                    for p in range(2):
                        b = i * 2 + p
                        pool.wait_ge(max_ready, (b - 1) * H)
                        pool.sem_inc(passed, 1)
                        prepare(b, i, p)

            @block.tensor
            def _(pe):
                pe.sem_inc(pv_mm, 2)
                pe.wait_ge(ctx_in[0], 16)
                first = pieces(pe, 0, 0)
                for k in range(NPIECE):
                    first(k)

                def transposed(b, s):
                    pe.wait_ge(norm_done, b * H + s + 1)
                    if s > 0:
                        pe.wait_ge(t_out, b * H + s)
                    for kc in range(KC):
                        last = pe.transpose(pt[:, kc // 3, (kc % 3) * S:(kc % 3 + 1) * S],
                                            probs[s % 2][:, kc * P:(kc + 1) * P], ident[0:S, 0:S])
                    last.then_inc(t_mm, 1)

                def weighted_values(b, p, g):
                    pe.wait_ge(t_out, b * H + HPC * (g + 1))
                    if g > 0:
                        pe.wait_ge(ao_ready, b * NG + g)
                    else:
                        pe.wait_ge(res_done, b + 1)
                    for kc in range(KC):
                        for j in range(HPC):
                            h = g * HPC + j
                            last = pe.matmul(po[j * DH:(j + 1) * DH, 0:S], v[p][:, kc, h * DH:(h + 1) * DH],
                                             pTs[:, g % 2, j, kc, :], start=kc == 0, stop=kc == KC - 1,
                                             skip_group_check=True)
                    last.then_inc(pv_mm, 1)

                def body(b, i, p, more):
                    piece = pieces(pe, b * NPIECE + NPIECE, 1 - p)
                    pe.wait_ge(q_ready, b * HPC + HPC)
                    pe.wait_ge(piece_out, b * NPIECE + NPIECE)
                    if more:
                        pe.wait_ge(ctx_in[1 - p], (i + p) * 16 + 16)
                    for s in range(H):
                        if s >= 2:
                            pe.wait_ge(exp_done, b * H + s - 1)
                        for half in range(2):
                            last = pe.matmul(ps[s % 2][0:S, half, 0:KH], qz[p][:, s // HPC, s % HPC, :],
                                             kT[p][:, s // HPC, half * KH:(half + 1) * KH], start=True, stop=True)
                        last.then_inc(s_mm, 1)
                        if more and s < NPIECE - 2:
                            piece(s)
                        if s > 0:
                            transposed(b, s - 1)
                        if s % HPC == 1 and s > HPC:
                            weighted_values(b, p, s // HPC - 1)
                    if more:
                        piece(NPIECE - 2)
                    transposed(b, H - 1)
                    if more:
                        piece(NPIECE - 1)
                    weighted_values(b, p, NG - 1)
                    pe.wait_ge(ao_ready, b * NG + NG)
                    for c in range(DC):
                        last = pe.matmul(po[0:S, :], aoT[:, c, :], wo[:, c, :], start=c == 0, stop=c == DC - 1)
                    last.then_inc(o_mm, 1)
                over_batches(pe, body)

            @block.vector
            def _(dve):
                for p in range(2):
                    dve.memset(v[p][:, KC - 1, :], 0.0).then_inc(zeroed_v, 1)
                dve.wait_ge(zeroed_v, 2)
                dve.sem_inc(res_done, 1)
                first = pieces_out(dve, 0, 0)
                for k in range(NPIECE):
                    first(k)

                def normalised(b, s):
                    dve.wait_ge(exp_done, b * H + s + 1)
                    dve.reciprocal(stat[:, s, 3:4], stat[:, s, 2:3]).then_inc(recip_done, 1)
                    dve.wait_ge(recip_done, b * H + s + 1)
                    dve.tensor_scalar(probs[s % 2][:, 0:SK], probs[s % 2][:, 0:SK], stat[:, s, 3:4], None,
                                      ALU.mult).then_inc(norm_done, 1)

                def body(b, i, p, more):
                    piece = pieces_out(dve, b * NPIECE + NPIECE, 1 - p)
                    if masked:
                        dve.wait_ge(mask_ready, b + 1)
                        dve.sem_inc(passed, 1)
                    for s in range(H):
                        dve.wait_ge(s_mm, b * H + s + 1)
                        scores = ps[s % 2][0:S, :, 0:KH]
                        if masked:
                            dve.sem_inc(passed, 1)
                            dve.tensor_tensor_reduce(out=scores, in0=scores, in1=madd[p][:, :, :], scale=1.0,
                                                     scalar=-3.0e38, op0=ALU.add, op1=ALU.max,
                                                     accum_out=stat[:, s, 0:1]).then_inc(max_raw, 1)
                        else:
                            dve.tensor_reduce(stat[:, s, 0:1], scores, AX.XY, ALU.max).then_inc(max_raw, 1)
                        dve.wait_ge(max_raw, b * H + s + 1)
                        dve.tensor_scalar(stat[:, s, 1:2], stat[:, s, 0:1], -1.0, None, ALU.mult).then_inc(max_ready, 1)
                        if s > 0:
                            normalised(b, s - 1)
                        if more and s < NPIECE - 2:
                            piece(s)
                    normalised(b, H - 1)
                    if more:
                        piece(NPIECE - 2)
                        piece(NPIECE - 1)
                    dve.wait_ge(o_mm, b + 1)
                    dve.tensor_tensor(tmp[:, :], po[0:S, :], bo[:, :], ALU.add).then_inc(o_biased, 1)
                    dve.wait_ge(o_biased, b + 1)
                    xb = x[:, b:b + 1, :] if isinstance(b, int) else x[:, bass.ds(b, 1), :]
                    xb = xb.rearrange("q a n -> q (a n)")
                    dve.scalar_tensor_tensor(out=xb, in0=tmp[:, :], scalar=env.gate[0:S, layer:layer + 1], in1=xb,
                                             op0=ALU.mult, op1=ALU.add).then_inc(res_done, 1)
                over_batches(dve, body)

            @block.scalar
            def _(act):
                act.wait_ge(zeroed, 4)

                def turned(b, s):
                    act.wait_ge(pv_mm, b * NG + s // HPC + 1)
                    act.wait_ge(t_mm, b * H + s + 1)
                    g = s // HPC
                    act.activation(pTs[:, g % 2, s % HPC, :, :].rearrange("k (a c) q -> k a (c q)", a=2),
                                   pt[:, :, 0:3 * S], ACT.Copy).then_inc(t_out, 1)

                def heads_out(b, g):
                    act.wait_ge(pv_mm, b * NG + g + 3)
                    act.activation(aoT[:, g, :], po[:, 0:S], ACT.Identity, bias=bv[:, g:g + 1]).then_inc(ao_ready, 1)

                def body(b, i, p, more):
                    for s in range(H):
                        if s >= 2:
                            act.wait_ge(t_mm, b * H + s - 1)
                        act.wait_ge(max_ready, b * H + s + 1)
                        act.activation(probs[s % 2][:, 0:SK].rearrange("q (h k) -> q h k", h=2),
                                       ps[s % 2][0:S, :, 0:KH], ACT.Exp, bias=stat[:, s, 1:2],
                                       accum_out=stat[:, s, 2:3]).then_inc(exp_done, 1)
                        if s > 0:
                            turned(b, s - 1)
                        if s % HPC == 2 and s > HPC:
                            heads_out(b, s // HPC - 1)
                    turned(b, H - 1)
                    heads_out(b, NG - 1)
                over_batches(act, body)


def dense_and_route(nc, env, layer, E, K, gate_w, gate_b, w_up, b_up, w_down, b_down):
    swiglu = layer == 0
    EX = E + 1 if swiglu else E
    FC = (IS0 if swiglu else I1) // P
    slots = SLOTS0 if swiglu else SLOTS1
    with ExitStack() as cx:
        def sb(n, s, dt=F32):
            return cx.enter_context(nc.sbuf_tensor(env.name(n), s, dt))

        def sem(n):
            return env.semaphore(n)

        def pb(n, s):
            return cx.enter_context(nc.psum_tensor(env.name(n), s, F32))

        x, xnT, acc = env.x, env.xnT, env.acc
        UPW = 2 * IS0 if swiglu else I1
        wg, hT = sb("wg", [P, DC, EX]), sb("hT", [P, FC, T])
        wu = sb("wu", [P, DC, UPW])
        wd = sb("wd", [P, 8, D])
        b1 = sb("b1", [P, FC])
        sg = [sb(f"sg{n}", [P, TH]) for n in range(2)]
        up = [sb(f"up{n}", [P, TH]) for n in range(2)]
        rowb = sb("rowb", [S, D])
        gb = sb("gb", [S, E])
        ones, before = sb("ones", [S, S]), sb("before", [S, S])
        iota_i, iota_e = sb("iota_i", [S, E], I32), sb("iota_e", [S, E])
        pack_i, pack_f = sb("pack_i", [S, B, K + 1], I32), sb("pack_f", [S, B, K + 1])
        logit, z = sb("logit", [S, B, E]), sb("z", [S, B])
        red, rsum = sb("red", [S, B]), sb("rsum", [S, B])
        sig = sb("sig", [S, B])
        top, top_i = sb("top", [S, B, 8]), sb("top_i", [S, B, 8], U32)
        top_f = sb("top_f", [S, B, K])
        eq = sb("eq", [S, B, K, E])
        chosen, pos = sb("chosen", [S, B, E]), sb("pos", [S, B, E])
        posk, keep = sb("posk", [S, B, K]), sb("keep", [S, B, K])
        slot_now = [sb(f"slot_now{p}", [S, K + 1], U32) for p in range(2)]
        slot_at = sb("slot_at", [S, B, K + 1], U32)
        pl = pb("pl", [S, 2, 512])
        pg, pu = [pb(f"pg{n}", [P, 512]) for n in range(2)], [pb(f"pu{n}", [P, 512]) for n in range(2)]
        ppos, pcnt = pb("ppos", [S, 512]), pb("pcnt", [S, 512])
        if not swiglu:
            LV = -(-T // P)
            lvl_i, lvl = sb("lvl_i", [S, LV], I32), sb("lvl", [S, LV])
            tile_i, tile_n = sb("tile_i", [1, TILES1], I32), sb("tile_n", [1, TILES1])
            cmp7, cmp20 = sb("cmp7", [S, E, LV]), sb("cmp20", [1, TILES1, E])
            tiles, ends, base, cnt = sb("tiles", [S, E]), sb("ends", [S, E]), sb("base", [S, E]), sb("cnt", [S, E])
            texp = sb("texp", [1, TILES1])
        gate_in, up_in, down_in, small_in = sem("gate_in"), sem("up_in"), sem("down_in"), sem("small_in")
        down2_in = sem("down2_in")
        const_done, pool_step, table_zero = sem("const_done"), sem("pool_step"), sem("table_zero")
        logit_mm, route_step, exp_ready, exp_out = sem("logit_mm"), sem("route_step"), sem("exp_ready"), sem("exp_out")
        chosen_ready, pos_mm, slots_ready = sem("chosen_ready"), sem("pos_mm"), sem("slots_ready")
        up_mm, up_out, hidden = sem("up_mm"), sem("up_out"), sem("hidden")
        down_mm, down_out, acc_step = sem("down_mm"), sem("down_out"), sem("acc_step")
        now_ready, passed = sem("now_ready"), sem("passed")
        scattered = [sem(f"scattered{p}") for p in range(2)]
        NP_ = FC * 2
        ROUTE_AT = NP_ - 4
        NDH = FC // 8

        with nc.Block() as block:
            @block.sync
            def _(sp):
                sp.dma_start(wg[:, :, :], gate_w).then_inc(gate_in, 16)
                sp.dma_start(wu[:, :, :], w_up).then_inc(up_in, 16)
                if not swiglu:
                    sp.dma_start(b1[:, :], b_up).then_inc(up_in, 16)
                    sp.dma_start(gb[:, :], gate_b.broadcast_to([S, E])).then_inc(small_in, 16)
                    sp.dma_start(rowb[:, :], b_down.broadcast_to([S, D])).then_inc(small_in, 16)
                sp.wait_ge(const_done, 1)
                sp.dma_start(env.slot_token[0:slots, :].rearrange("(p n) a -> p (n a)", n=P),
                             env.zero[0:slots // P, :]).then_inc(table_zero, 16)
                sp.dma_start(wd[:, :, :], w_down[:, 0:8, :]).then_inc(down_in, 16)
                if NDH > 1:
                    sp.wait_ge(down_mm, B)
                    sp.dma_start(wd[:, :, :], w_down[:, 8:16, :]).then_inc(down2_in, 16)
                sp.wait_ge(table_zero, 16)

            @block.gpsimd
            def _(pool):
                pool.memset(env.zero[:, :], 0).then_inc(const_done, 1)
                pool.memset(ones[:, :], 1.0).then_inc(pool_step, 1)
                pool.memset(before[:, :], 1.0).then_inc(pool_step, 1)
                pool.wait_ge(pool_step, 2)
                pool.affine_select(out=before[:, :], in_=before[:, :], compare_op=ALU.is_gt, fill=0.0, base=0,
                                   pattern=[[1, S]], channel_multiplier=-1).then_inc(const_done, 1)
                pool.iota(iota_i[:, :], pattern=[[1, E]], base=0, channel_multiplier=0).then_inc(const_done, 1)
                pool.iota(pack_i[:, :, 0:K], pattern=[[S * K, B], [1, K]], base=slots,
                          channel_multiplier=K).then_inc(const_done, 1)
                pool.iota(pack_i[:, :, K:K + 1], pattern=[[S, B], [1, 1]], base=0, channel_multiplier=1)\
                    .then_inc(const_done, 1)
                if not swiglu:
                    pool.iota(lvl_i[:, :], pattern=[[P, LV]], base=0, channel_multiplier=0).then_inc(const_done, 1)
                    pool.iota(tile_i[:, :], pattern=[[1, TILES1]], base=0, channel_multiplier=0).then_inc(const_done, 1)
                if swiglu:
                    for n in range(NP_):
                        f, half = n // 2, n % 2
                        pool.wait_ge(up_out, n + 1)
                        pool.tensor_tensor(hT[:, f, half * TH:(half + 1) * TH], sg[n % 2][:, :], up[n % 2][:, :],
                                           ALU.mult).then_inc(hidden, 1)
                pool.wait_ge(table_zero, 16)
                pool.wait_ge(slots_ready, 1)

                def scatter(t, p):
                    at = slot_at[:, t, :] if isinstance(t, int) else \
                        slot_at[:, bass.ds(t, 1), :].rearrange("q a k -> q (a k)")
                    pool.tensor_copy(slot_now[p][:, :], at).then_inc(now_ready, 1)
                    pool.wait_ge(now_ready, t + 1)
                    pool.sem_inc(passed, 1)
                    for k in range(K):
                        pool.indirect_dma_start(
                            out=env.slot_token[:, :], in_=slot_now[p][:, K:K + 1], in_offset=None,
                            out_offset=bass.IndirectOffsetOnAxis(ap=slot_now[p][:, k:k + 1], axis=0))\
                            .then_inc(scattered[p], 16)
                for p in range(2):
                    scatter(p, p)
                with pool.Fori(1, B // 2) as i:
                    for p in range(2):
                        pool.wait_ge(scattered[p], i * (16 * K))
                        pool.sem_inc(passed, 1)
                        scatter(i * 2 + p, p)
                for p in range(2):
                    pool.wait_ge(scattered[p], (B // 2) * 16 * K)

            @block.tensor
            def _(pe):
                pe.wait_ge(gate_in, 16)
                for t in range(B):
                    for c in range(DC):
                        last = pe.matmul(pl[:, t // 4, (t % 4) * EX:(t % 4 + 1) * EX], xnT[:, c, t * S:(t + 1) * S],
                                         wg[:, c, :], start=c == 0, stop=c == DC - 1)
                last.then_inc(logit_mm, 1)
                pe.wait_ge(up_in, 16 if swiglu else 32)
                for n in range(NP_):
                    f, half = n // 2, n % 2
                    if n == ROUTE_AT:
                        pe.wait_ge(chosen_ready, 1)
                        pe.wait_ge(const_done, 2)
                        for t in range(B):
                            for j in range(t + 1):
                                pe.matmul(ppos[:, t * E:(t + 1) * E], (before if j == t else ones)[:, :],
                                          chosen[:, j, :], start=j == 0, stop=j == t)
                        for j in range(B):
                            last = pe.matmul(pcnt[:, 0:E], ones[:, :], chosen[:, j, :], start=j == 0, stop=j == B - 1)
                        last.then_inc(pos_mm, 1)
                    if n >= 2:
                        pe.wait_ge(up_out, n - 1)
                    for dst, off in ((pg, 0), (pu, IS0))[:2 if swiglu else 1]:
                        for c in range(DC):
                            last = pe.matmul(dst[n % 2][:, 0:TH], wu[:, c, off + f * P:off + (f + 1) * P],
                                             xnT[:, c, half * TH:(half + 1) * TH], start=c == 0, stop=c == DC - 1)
                    last.then_inc(up_mm, 1)
                pe.wait_ge(hidden if swiglu else up_out, NP_)
                for hf in range(NDH):
                    pe.wait_ge(down_in if hf == 0 else down2_in, 16)
                    for t in range(B):
                        n = hf * B + t
                        if n >= 2:
                            pe.wait_ge(down_out, n - 1)
                        for f in range(8):
                            last = pe.matmul(pg[n % 2][0:S, :], hT[:, hf * 8 + f, t * S:(t + 1) * S], wd[:, f, :],
                                             start=f == 0, stop=f == 7)
                        last.then_inc(down_mm, 1)

            @block.scalar
            def _(act):
                act.wait_ge(exp_ready, 1)
                act.activation(logit[:, :, :], logit[:, :, :], ACT.Exp).then_inc(exp_out, 1)
                if swiglu:
                    act.activation(z[:, :], z[:, :], ACT.Exp, scale=-1.0).then_inc(exp_out, 1)
                for n in range(NP_):
                    f, half = n // 2, n % 2
                    act.wait_ge(up_mm, n + 1)
                    if swiglu:
                        if n >= 2:
                            act.wait_ge(hidden, n - 1)
                        act.activation(sg[n % 2][:, :], pg[n % 2][:, 0:TH], ACT.Silu)
                        act.activation(up[n % 2][:, :], pu[n % 2][:, 0:TH], ACT.Copy).then_inc(up_out, 1)
                    else:
                        act.activation(hT[:, f, half * TH:(half + 1) * TH], pg[n % 2][:, 0:TH], ACT.Gelu_apprx_tanh,
                                       bias=b1[:, f:f + 1]).then_inc(up_out, 1)

            @block.vector
            def _(dve):
                steps = [0]

                def link(ins):
                    steps[0] += 1
                    ins.then_inc(route_step, 1)
                    dve.wait_ge(route_step, steps[0])

                def over_experts(a):
                    return a.unsqueeze(2).broadcast_to([S, B, E])

                dve.wait_ge(logit_mm, 1)
                for q in range(2):
                    tiles4 = pl[:, q, 0:4 * EX].rearrange("s (t e) -> s t e", e=EX)
                    if swiglu:
                        dve.tensor_copy(z[:, 4 * q:4 * q + 4], tiles4[:, :, E])
                        link(dve.tensor_copy(logit[:, 4 * q:4 * q + 4, :], tiles4[:, :, 0:E]))
                    else:
                        if q == 0:
                            dve.wait_ge(small_in, 32)
                        link(dve.tensor_tensor(logit[:, 4 * q:4 * q + 4, :], tiles4,
                                               gb[:, :].unsqueeze(1).broadcast_to([S, 4, E]), ALU.add))
                link(dve.tensor_reduce(red[:, :], logit[:, :, :], AX.X, ALU.max))
                dve.tensor_tensor(logit[:, :, :], logit[:, :, :], over_experts(red[:, :]), ALU.subtract)\
                    .then_inc(exp_ready, 1)
                dve.wait_ge(exp_out, 2 if swiglu else 1)
                if swiglu:
                    link(dve.tensor_scalar(z[:, :], z[:, :], 1.0, None, ALU.add))
                    link(dve.reciprocal(sig[:, :], z[:, :]))
                link(dve.tensor_reduce(red[:, :], logit[:, :, :], AX.X, ALU.add))
                link(dve.reciprocal(rsum[:, :], red[:, :]))
                link(dve.tensor_tensor(logit[:, :, :], logit[:, :, :], over_experts(rsum[:, :]), ALU.mult))
                for t in range(B):
                    link(dve.max(top[:, t, :], logit[:, t, :]))
                    link(dve.max_index(top_i[:, t, :], top[:, t, :], logit[:, t, :]))
                link(dve.tensor_copy(top_f[:, :, :], top_i[:, :, 0:K]))
                dve.wait_ge(const_done, 5 if swiglu else 7)
                link(dve.tensor_copy(iota_e[:, :], iota_i[:, :]))
                link(dve.tensor_copy(pack_f[:, :, :], pack_i[:, :, :]))
                for t in range(B):
                    link(dve.tensor_tensor(eq[:, t, :, :], iota_e[:, :].unsqueeze(1).broadcast_to([S, K, E]),
                                           top_f[:, t, :].unsqueeze(2).broadcast_to([S, K, E]), ALU.is_equal))
                    link(dve.tensor_reduce(chosen[:, t, :], eq[:, t, :, :].rearrange("s k e -> s e k"), AX.X, ALU.add))
                dve.sem_inc(chosen_ready, 1)
                link(dve.tensor_reduce(red[:, :], top[:, :, 0:K], AX.X, ALU.add))
                if not swiglu:
                    link(dve.tensor_scalar(red[:, :], red[:, :], 1e-9, None, ALU.add))
                link(dve.reciprocal(rsum[:, :], red[:, :]))
                link(dve.tensor_tensor(env.weight[:, :, 0:K], top[:, :, 0:K],
                                       rsum[:, :].unsqueeze(2).broadcast_to([S, B, K]), ALU.mult))
                dve.wait_ge(pos_mm, 1)
                link(dve.tensor_copy(pos[:, :, :], ppos[:, 0:B * E].rearrange("s (t e) -> s t e", e=E)))
                if not swiglu:
                    link(dve.tensor_copy(cnt[:, :], pcnt[:, 0:E]))
                    link(dve.tensor_copy(lvl[:, :], lvl_i[:, :]))
                    link(dve.tensor_tensor(cmp7[:, :, :], cnt[:, :].unsqueeze(2).broadcast_to([S, E, LV]),
                                           lvl[:, :].unsqueeze(1).broadcast_to([S, E, LV]), ALU.is_gt))
                    link(dve.tensor_reduce(tiles[:, :], cmp7[:, :, :], AX.X, ALU.add))
                    link(dve.tensor_tensor_scan(ends[:, :], ones[:, 0:E], tiles[:, :], 0.0, ALU.mult, ALU.add))
                    link(dve.tensor_tensor(base[:, :], ends[:, :], tiles[:, :], ALU.subtract))
                    link(dve.tensor_scalar(base[:, :], base[:, :], float(P), None, ALU.mult))
                    link(dve.tensor_tensor(pos[:, :, :], pos[:, :, :],
                                           base[:, :].unsqueeze(1).broadcast_to([S, B, E]), ALU.add))
                    link(dve.tensor_copy(tile_n[:, :], tile_i[:, :]))
                    link(dve.tensor_tensor(cmp20[:, :, :], tile_n[:, :].unsqueeze(2).broadcast_to([1, TILES1, E]),
                                           ends[0:1, :].unsqueeze(1).broadcast_to([1, TILES1, E]), ALU.is_ge))
                    link(dve.tensor_reduce(texp[:, :], cmp20[:, :, :], AX.X, ALU.add))
                    link(dve.tensor_scalar(texp[:, :], texp[:, :], float(E - 1), None, ALU.min))
                    link(dve.tensor_copy(env.tile_expert[:, :], texp[:, :]))
                for t in range(B):
                    link(dve.tensor_tensor(eq[:, t, :, :], eq[:, t, :, :],
                                           pos[:, t, :].unsqueeze(1).broadcast_to([S, K, E]), ALU.mult))
                    link(dve.tensor_reduce(posk[:, t, :], eq[:, t, :, :], AX.X, ALU.add))
                if swiglu:
                    link(dve.tensor_scalar(keep[:, :, :], posk[:, :, :], float(CAP), None, ALU.is_lt))
                    link(dve.scalar_tensor_tensor(out=posk[:, :, :], in0=top_f[:, :, :], scalar=float(CAP),
                                                  in1=posk[:, :, :], op0=ALU.mult, op1=ALU.add))
                    link(dve.tensor_tensor(env.weight[:, :, 0:K], env.weight[:, :, 0:K], keep[:, :, :], ALU.mult))
                    link(dve.tensor_tensor(top_f[:, :, :], posk[:, :, :], keep[:, :, :], ALU.mult))
                    link(dve.tensor_tensor(posk[:, :, :], posk[:, :, :], pack_f[:, :, 0:K], ALU.subtract))
                    link(dve.tensor_tensor(posk[:, :, :], posk[:, :, :], keep[:, :, :], ALU.mult))
                    link(dve.tensor_tensor(pack_f[:, :, 0:K], posk[:, :, :], pack_f[:, :, 0:K], ALU.add))
                    link(dve.tensor_copy(env.gather_at[:, :, 0:K], top_f[:, :, :]))
                else:
                    link(dve.tensor_copy(pack_f[:, :, 0:K], posk[:, :, :]))
                    link(dve.tensor_copy(env.gather_at[:, :, 0:K], posk[:, :, :]))
                dve.tensor_copy(slot_at[:, :, :], pack_f[:, :, :]).then_inc(slots_ready, 1)
                if not swiglu:
                    for t in range(B):
                        dve.tensor_tensor(acc[:, t, :], acc[:, t, :], rowb[:, :], ALU.add).then_inc(acc_step, 1)
                    dve.wait_ge(acc_step, B)
                for n in range(NDH * B):
                    t = n % B
                    dve.wait_ge(down_mm, n + 1)
                    if swiglu:
                        dve.tensor_scalar(acc[:, t, :], pg[n % 2][0:S, :], sig[:, t:t + 1], None, ALU.mult)\
                            .then_inc(down_out, 1)
                    else:
                        if n == B:
                            dve.wait_ge(down_out, B)
                        dve.tensor_tensor(acc[:, t, :], pg[n % 2][0:S, :], acc[:, t, :], ALU.add)\
                            .then_inc(down_out, 1)


def slot_indices(nc, env, rows):
    with ExitStack() as cx:
        tab_i = cx.enter_context(nc.sbuf_tensor(env.name("tab_i"), [rows, P], U32))
        tab_f = cx.enter_context(nc.sbuf_tensor(env.name("tab_f"), [rows, P], F32))
        pi = cx.enter_context(nc.psum_tensor(env.name("pi"), [P, 512], F32))
        loaded, as_float, turned, done = (env.semaphore(n)
                                          for n in ("loaded", "as_float", "turned", "done"))
        with nc.Block() as block:
            @block.sync
            def _(sp):
                sp.dma_start(tab_i[:, :], env.slot_token[0:rows * P, :].rearrange("(r n) a -> r (n a)", n=P))\
                    .then_inc(loaded, 16)

            @block.vector
            def _(dve):
                dve.wait_ge(loaded, 16)
                dve.tensor_copy(tab_f[:, :], tab_i[:, :]).then_inc(as_float, 1)
                dve.wait_ge(turned, 1)
                dve.tensor_copy(env.slot_index[:, 0:rows], pi[:, 0:rows]).then_inc(done, 1)

            @block.tensor
            def _(pe):
                pe.wait_ge(as_float, 1)
                pe.transpose(pi[:, 0:rows], tab_f[:, :], env.ident[0:rows, 0:rows]).then_inc(turned, 1)


def experts_swiglu(nc, env, w_gate_up, w_down):
    with ExitStack() as cx:
        def sb(n, s, dt=F32):
            return cx.enter_context(nc.sbuf_tensor(env.name(n), s, dt))

        def sem(n):
            return env.semaphore(n)

        def pb(n, s):
            return cx.enter_context(nc.psum_tensor(env.name(n), s, F32))

        ident = env.ident
        NH, FI = CAP // P, I0 // P
        wgu = [sb(f"wgu{p}", [P, DC, 2 * I0]) for p in range(2)]
        wdn = [sb(f"wdn{p}", [P, FI, D]) for p in range(2)]
        index_now = [sb(f"index_now{p}", [P, NH], U32) for p in range(2)]
        xg = [sb(f"xg{p}", [P, NH, D]) for p in range(2)]
        xT = [sb(f"xT{p}", [P, DC, CAP]) for p in range(2)]
        sg = [sb(f"sg{p}", [P, FI, CAP]) for p in range(2)]
        hT = [sb(f"hT{p}", [P, FI, CAP]) for p in range(2)]
        y = [sb(f"y{p}", [P, NH, D]) for p in range(2)]
        px = pb("px", [P, DC, CAP])
        pgu = [pb(f"pgu{p}", [P, FI, 2, CAP]) for p in range(2)]
        pd = pb("pd", [P, NH, D])
        w_in = [sem(f"w_in{p}") for p in range(2)]
        x_in = [sem(f"x_in{p}") for p in range(2)]
        y_stored = [sem(f"y_stored{p}") for p in range(2)]
        index_ready, passed = sem("index_ready"), sem("passed")
        x_mm, x_ready, gu_mm, silu_done, h_ready = sem("x_mm"), sem("x_ready"), sem("gu_mm"), sem("silu_done"), sem("h_ready")
        d_mm, y_ready = sem("d_mm"), sem("y_ready")

        def over_experts(engine, body):
            with engine.Fori(0, E0 // 2 - 1) as i:
                for p in range(2):
                    body(i * 2 + p, i, p, True)
            for p in range(2):
                body(E0 - 2 + p, E0 // 2 - 1, p, False)

        with nc.Block() as block:
            @block.sync
            def _(sp):
                def load(e, p):
                    at = (slice(e, e + 1) if isinstance(e, int) else bass.ds(e, 1))
                    sp.dma_start(wgu[p][:, :, :], w_gate_up[at, :, :, :].rearrange("a p c n -> (a p) c n"))\
                        .then_inc(w_in[p], 16)
                    sp.dma_start(wdn[p][:, :, :], w_down[at, :, :, :].rearrange("a p c n -> (a p) c n"))\
                        .then_inc(w_in[p], 16)
                for p in range(2):
                    sp.sem_inc(y_stored[p], 16)
                    load(p, p)

                def body(e, i, p, more):
                    if more:
                        sp.wait_ge(d_mm, e * NH + NH)
                        load(e + 2, p)
                    sp.wait_ge(y_ready, e * NH + 2 * NH)
                    at = slice(e * CAP, (e + 1) * CAP) if isinstance(e, int) else bass.ds(e * CAP, CAP)
                    sp.dma_start(env.y_rows[at, :].rearrange("(h p) n -> p h n", p=P), y[p][:, :, :])\
                        .then_inc(y_stored[p], 16)
                over_experts(sp, body)
                for p in range(2):
                    sp.wait_ge(y_stored[p], (E0 // 2) * 16 + 16)

            @block.gpsimd
            def _(pool):
                def fetch(e, i, p):
                    at = slice(e * NH, (e + 1) * NH) if isinstance(e, int) else bass.ds(e * NH, NH)
                    pool.tensor_copy(index_now[p][:, :], env.slot_index[:, at]).then_inc(index_ready, 1)
                    pool.wait_ge(index_ready, e + 1)
                    pool.sem_inc(passed, 1)
                    for h in range(NH):
                        pool.indirect_dma_start(
                            out=xg[p][:, h, :], out_offset=None, in_=env.xn_rows[:, :],
                            in_offset=bass.IndirectOffsetOnAxis(ap=index_now[p][:, h:h + 1], axis=0))\
                            .then_inc(x_in[p], 16)
                for p in range(2):
                    fetch(p, 0, p)
                with pool.Fori(1, E0 // 2) as i:
                    for p in range(2):
                        e = i * 2 + p
                        pool.wait_ge(x_mm, e - 1)
                        pool.sem_inc(passed, 1)
                        pool.wait_ge(x_in[p], i * (16 * NH))
                        pool.sem_inc(passed, 1)
                        fetch(e, i, p)

            @block.tensor
            def _(pe):
                def rows_turned(p, arrived):
                    pe.wait_ge(x_in[p], arrived)
                    for h in range(NH):
                        for c in range(DC):
                            last = pe.transpose(px[:, c, h * P:(h + 1) * P], xg[p][:, h, c * P:(c + 1) * P], ident[:, :])
                    last.then_inc(x_mm, 1)

                rows_turned(0, 16 * NH)

                def body(e, i, p, more):
                    pe.wait_ge(w_in[p], i * 32 + 32)
                    pe.wait_ge(x_ready, e + 1)
                    for f in range(FI):
                        for gu in range(2):
                            for c in range(DC):
                                last = pe.matmul(pgu[p][:, f, gu, :], wgu[p][:, c, (gu * FI + f) * P:(gu * FI + f + 1) * P],
                                                 xT[p][:, c, :], start=c == 0, stop=c == DC - 1)
                        last.then_inc(gu_mm, 1)
                    if more or p == 0:
                        rows_turned(1 - p, (i + p) * (16 * NH) + 16 * NH)
                    pe.wait_ge(h_ready, e * FI + FI)
                    for h in range(NH):
                        pe.wait_ge(y_ready, e * NH + h + 1)
                        for f in range(FI):
                            last = pe.matmul(pd[:, h, :], hT[p][:, f, h * P:(h + 1) * P], wdn[p][:, f, :],
                                             start=f == 0, stop=f == FI - 1)
                        last.then_inc(d_mm, 1)
                over_experts(pe, body)

            @block.scalar
            def _(act):
                act.sem_inc(y_ready, NH)

                def body(e, i, p, more):
                    for f in range(FI):
                        act.wait_ge(gu_mm, e * FI + f + 1)
                        act.activation(sg[p][:, f, :], pgu[p][:, f, 0, :], ACT.Silu).then_inc(silu_done, 1)
                    act.wait_ge(y_stored[p], i * 16 + 16)
                    for h in range(NH):
                        act.wait_ge(d_mm, e * NH + h + 1)
                        act.activation(y[p][:, h, :], pd[:, h, :], ACT.Copy).then_inc(y_ready, 1)
                over_experts(act, body)

            @block.vector
            def _(dve):
                def turned_out(e, p):
                    dve.wait_ge(x_mm, e + 1)
                    dve.tensor_copy(xT[p][:, :, :], px[:, :, :]).then_inc(x_ready, 1)
                turned_out(0, 0)

                def body(e, i, p, more):
                    for f in range(FI):
                        dve.wait_ge(silu_done, e * FI + f + 1)
                        dve.tensor_tensor(hT[p][:, f, :], sg[p][:, f, :], pgu[p][:, f, 1, :], ALU.mult)\
                            .then_inc(h_ready, 1)
                    if more or p == 0:
                        turned_out(e + 1, 1 - p)
                over_experts(dve, body)


def experts_gelu(nc, env, w_chunks, b_up, b_down):
    with ExitStack() as cx:
        def sb(n, s, dt=F32):
            return cx.enter_context(nc.sbuf_tensor(env.name(n), s, dt))

        def sem(n):
            return env.semaphore(n)

        def pb(n, s):
            return cx.enter_context(nc.psum_tensor(env.name(n), s, F32))

        ident = env.ident
        NQ, FQ = I1 // 512, 4
        NCH = 2 * NQ
        w = [sb(f"w{q}", [P, 4, 512]) for q in range(NCH)]
        b1 = [sb(f"b1_{p}", [P, I1 // P]) for p in range(2)]
        b2 = [sb(f"b2_{p}", [P, D]) for p in range(2)]
        index_now = [sb(f"index_now{p}", [P, 1], U32) for p in range(2)]
        xg = [sb(f"xg{p}", [P, D]) for p in range(2)]
        xT = [sb(f"xT{p}", [P, DC, P]) for p in range(2)]
        hT = sb("hT", [P, I1 // P, P])
        y = [sb(f"y{p}", [P, D]) for p in range(2)]
        px = pb("px", [P, DC, P])
        ph = [pb(f"ph{n}", [P, FQ, P]) for n in range(2)]
        pd = [pb(f"pd{p}", [P, D]) for p in range(2)]
        w_in = [sem(f"w_in{q}") for q in range(NCH)]
        b_in = [sem(f"b_in{p}") for p in range(2)]
        x_in = [sem(f"x_in{p}") for p in range(2)]
        y_stored = [sem(f"y_stored{p}") for p in range(2)]
        index_ready, passed = sem("index_ready"), sem("passed")
        x_mm, x_ready, chunk_mm, h_ready, y_ready = sem("x_mm"), sem("x_ready"), sem("chunk_mm"), sem("h_ready"), sem("y_ready")

        def over_tiles(engine, body):
            with engine.Fori(0, TILES1 // 2 - 1) as i:
                for p in range(2):
                    body(i * 2 + p, i, p, True)
            for p in range(2):
                body(TILES1 - 2 + p, TILES1 // 2 - 1, p, p == 0)

        with nc.Block() as block:
            @block.sync
            def _(sp):
                def expert_of(t):
                    at = slice(t, t + 1) if isinstance(t, int) else bass.ds(t, 1)
                    return sp.value_load(env.tile_expert[0:1, at], min_val=0, max_val=E1 - 1)

                def load_biases(e, p):
                    sp.dma_start(b1[p][:, :], b_up[bass.ds(e, 1), :, :].rearrange("a p f -> (a p) f")).then_inc(b_in[p], 16)
                    sp.dma_start(b2[p][:, :], b_down[bass.ds(e, 1), :].broadcast_to([P, D])).then_inc(b_in[p], 16)

                def load_chunk(e, q):
                    sp.dma_start(w[q][:, :, :], w_chunks[bass.ds(e, 1), q, :, :, :].rearrange("a p c n -> (a p) c n"))\
                        .then_inc(w_in[q], 16)
                e = expert_of(0)
                load_biases(e, 0)
                for q in range(NCH):
                    load_chunk(e, q)
                for p in range(2):
                    sp.sem_inc(y_stored[p], 16)

                def body(t, i, p, more):
                    if more:
                        e = expert_of(t + 1)
                        if isinstance(t, int) or True:
                            sp.wait_ge(y_ready, t + 1)
                        load_biases(e, 1 - p)
                    for q in range(NCH):
                        if more:
                            sp.wait_ge(chunk_mm, t * NCH + q + 1)
                            load_chunk(e, q)
                    sp.wait_ge(y_ready, t + 2)
                    at = slice(t * P, (t + 1) * P) if isinstance(t, int) else bass.ds(t * P, P)
                    sp.dma_start(env.y_rows[at, :], y[p][:, :]).then_inc(y_stored[p], 16)
                over_tiles(sp, body)
                for p in range(2):
                    sp.wait_ge(y_stored[p], (TILES1 // 2) * 16 + 16)

            @block.gpsimd
            def _(pool):
                def fetch(t, i, p):
                    at = slice(t, t + 1) if isinstance(t, int) else bass.ds(t, 1)
                    pool.tensor_copy(index_now[p][:, :], env.slot_index[:, at]).then_inc(index_ready, 1)
                    pool.wait_ge(index_ready, t + 1)
                    pool.sem_inc(passed, 1)
                    pool.indirect_dma_start(
                        out=xg[p][:, :], out_offset=None, in_=env.xn_rows[:, :],
                        in_offset=bass.IndirectOffsetOnAxis(ap=index_now[p][:, 0:1], axis=0)).then_inc(x_in[p], 16)
                for p in range(2):
                    fetch(p, 0, p)
                with pool.Fori(1, TILES1 // 2) as i:
                    for p in range(2):
                        t = i * 2 + p
                        pool.wait_ge(x_mm, t - 1)
                        pool.sem_inc(passed, 1)
                        pool.wait_ge(x_in[p], i * 16)
                        pool.sem_inc(passed, 1)
                        fetch(t, i, p)

            @block.tensor
            def _(pe):
                def rows_turned(p, arrived):
                    pe.wait_ge(x_in[p], arrived)
                    for c in range(DC):
                        last = pe.transpose(px[:, c, :], xg[p][:, c * P:(c + 1) * P], ident[:, :])
                    last.then_inc(x_mm, 1)

                rows_turned(0, 16)

                def body(t, i, p, more):
                    pe.wait_ge(x_ready, t + 1)
                    for q in range(NQ):
                        pe.wait_ge(w_in[q], t * 16 + 16)
                        if q >= 2:
                            pe.wait_ge(h_ready, t * NQ + q - 1)
                        for f in range(FQ):
                            for c in range(DC):
                                last = pe.matmul(ph[q % 2][:, f, :], w[q][:, c, f * P:(f + 1) * P], xT[p][:, c, :],
                                                 start=c == 0, stop=c == DC - 1)
                        last.then_inc(chunk_mm, 1)
                    if more:
                        rows_turned(1 - p, (i + p) * 16 + 16)
                    for q in range(NQ):
                        pe.wait_ge(w_in[NQ + q], t * 16 + 16)
                        pe.wait_ge(h_ready, t * NQ + q + 1)
                        if q == 0:
                            pe.wait_ge(y_ready, t + 1)
                        for f in range(FQ):
                            last = pe.matmul(pd[p][:, :], hT[:, q * FQ + f, :], w[NQ + q][:, f, :],
                                             start=q + f == 0, stop=(q == NQ - 1) and (f == FQ - 1))
                        last.then_inc(chunk_mm, 1)
                over_tiles(pe, body)

            @block.scalar
            def _(act):
                def body(t, i, p, more):
                    act.wait_ge(b_in[p], i * 32 + 32)
                    for q in range(NQ):
                        act.wait_ge(chunk_mm, t * NCH + q + 1)
                        for f in range(FQ):
                            last = act.activation(hT[:, q * FQ + f, :], ph[q % 2][:, f, :], ACT.Gelu_apprx_tanh,
                                                  bias=b1[p][:, q * FQ + f:q * FQ + f + 1])
                        last.then_inc(h_ready, 1)
                over_tiles(act, body)

            @block.vector
            def _(dve):
                dve.sem_inc(y_ready, 1)

                def turned_out(t, p):
                    dve.wait_ge(x_mm, t + 1)
                    dve.tensor_copy(xT[p][:, :, :], px[:, :, :]).then_inc(x_ready, 1)
                turned_out(0, 0)

                def body(t, i, p, more):
                    if more:
                        turned_out(t + 1, 1 - p)
                    dve.wait_ge(b_in[p], i * 32 + 32)
                    dve.wait_ge(y_stored[p], i * 16 + 16)
                    dve.wait_ge(chunk_mm, t * NCH + NCH)
                    dve.tensor_tensor(y[p][:, :], pd[p][:, :], b2[p][:, :], ALU.add).then_inc(y_ready, 1)
                over_tiles(dve, body)


def combine(nc, env, layer, K):
    with ExitStack() as cx:
        def sb(n, s, dt=F32):
            return cx.enter_context(nc.sbuf_tensor(env.name(n), s, dt))

        def sem(n):
            return env.semaphore(n)

        NB = 2 * K
        at_now = [sb(f"at_now{p}", [S, K], U32) for p in range(2)]
        rows = sb("rows", [S, 2, K, D])
        rows_in = [[sem(f"rows_in{p}_{k}") for k in range(K)] for p in range(2)]
        now_ready, used, done, passed, out_sem = sem("now_ready"), sem("used"), sem("done"), sem("passed"), sem("out")
        with nc.Block() as block:
            @block.gpsimd
            def _(pool):
                def fetch(t, p):
                    at = env.gather_at[:, t, 0:K] if isinstance(t, int) else \
                        env.gather_at[:, bass.ds(t, 1), 0:K].rearrange("q a k -> q (a k)")
                    pool.tensor_copy(at_now[p][:, :], at).then_inc(now_ready, 1)
                    pool.wait_ge(now_ready, t + 1)
                    pool.sem_inc(passed, 1)
                    for k in range(K):
                        pool.indirect_dma_start(
                            out=rows[:, p, k, :], out_offset=None, in_=env.y_rows[:, :],
                            in_offset=bass.IndirectOffsetOnAxis(ap=at_now[p][:, k:k + 1], axis=0))\
                            .then_inc(rows_in[p][k], 16)
                for p in range(2):
                    fetch(p, p)
                with pool.Fori(1, B // 2) as i:
                    for p in range(2):
                        t = i * 2 + p
                        pool.wait_ge(used, (t - 1) * K)
                        pool.sem_inc(passed, 1)
                        fetch(t, p)

            @block.vector
            def _(dve):
                with dve.Fori(0, B // 2) as i:
                    for p in range(2):
                        t = i * 2 + p
                        acc_t = env.acc[:, bass.ds(t, 1), :].rearrange("q a n -> q (a n)")
                        x_t = env.x[:, bass.ds(t, 1), :].rearrange("q a n -> q (a n)")
                        for k in range(K):
                            dve.wait_ge(rows_in[p][k], i * 16 + 16)
                            dve.scalar_tensor_tensor(
                                out=acc_t, in0=rows[:, p, k, :],
                                scalar=env.weight[:, bass.ds(t, 1), k:k + 1].rearrange("q a k -> q (a k)"),
                                in1=acc_t, op0=ALU.mult, op1=ALU.add).then_inc(used, 1)
                            dve.wait_ge(used, t * K + k + 1)
                        dve.scalar_tensor_tensor(out=x_t, in0=acc_t, scalar=env.gate[0:S, 2 + layer:3 + layer],
                                                 in1=x_t, op0=ALU.mult, op1=ALU.add).then_inc(done, 1)

            @block.sync
            def _(sp):
                if layer == 1:
                    sp.wait_ge(done, B)
                    sp.dma_start(env.out.rearrange("b s d -> s b d"), env.x[:, :, :]).then_inc(out_sem, 16)
                    sp.wait_ge(out_sem, 16)


def program(nc, a, out, stage=99):
    env = Env()
    count = [0]

    def name(n):
        count[0] += 1
        return f"{n}_{count[0]}"
    env.name = name
    held = []

    def semaphore(n):
        held.append(nc.alloc_semaphore(name(n)))
        return held[-1]
    env.semaphore = semaphore

    def clear_semaphores():
        nc.clear_and_free_semaphores(held)
        held.clear()
        nc.all_engine_barrier()
    env.out = out
    env.ctxT, env.mask = a["ctxT"], a["mask"]
    env.xn_rows = nc.dram_tensor("xn_rows", [T, D], F32).ap()
    env.y_rows = nc.dram_tensor("y_rows", [SLOTS0, D], F32).ap()
    slot_tables = [nc.dram_tensor(f"slot_token{l}", [n, 1], U32).ap()
                   for l, n in enumerate((SLOTS0 + T * K0, SLOTS1))]
    with ExitStack() as cx:
        def sb(n, s, dt=F32):
            return cx.enter_context(nc.sbuf_tensor(n, s, dt))
        env.x, env.xnT, env.ident = sb("x", [S, B, D]), sb("xnT", [P, DC, T]), sb("ident", [P, P])
        env.gate = sb("gate", [P, 4])
        env.weight, env.gather_at = sb("weight", [S, B, K0]), sb("gather_at", [S, B, K0], U32)
        env.tile_expert = sb("tile_expert", [1, TILES1], I32)
        env.slot_index = sb("slot_index", [P, SLOTS0 // P], U32)
        env.zero = sb("zero", [P, P], U32)

        with nc.semaphore("start_in") as start_in, nc.semaphore("ident_done") as ident_done, \
                nc.semaphore("gate_done") as gate_done, nc.Block() as block:
            @block.sync
            def _(sp):
                sp.dma_start(env.x[:, :, :], a["x"].rearrange("b s d -> s b d")).then_inc(start_in, 16)
                sp.dma_start(env.gate[:, 0:2], a["g_xattn"].broadcast_to([P, 2])).then_inc(start_in, 16)
                sp.dma_start(env.gate[:, 2:4], a["g_ffn"].broadcast_to([P, 2])).then_inc(start_in, 16)
                sp.wait_ge(start_in, 48)

            @block.gpsimd
            def _(pool):
                pool.memset(env.ident[:, :], 0.0).then_inc(ident_done, 1)
                pool.wait_ge(ident_done, 1)
                pool.affine_select(out=env.ident[:, :], in_=env.ident[:, :], compare_op=ALU.not_equal, fill=1.0,
                                   base=0, pattern=[[-1, P]], channel_multiplier=1).then_inc(ident_done, 1)

            @block.scalar
            def _(act):
                act.wait_ge(start_in, 48)
                act.activation(env.gate[:, :], env.gate[:, :], ACT.Tanh).then_inc(gate_done, 1)

        def attend(layer):
            pre = f"l{layer}_"
            layer_norm(nc, env, False, False)
            attention(nc, env, layer, layer == 0, *(a[pre + n] for n in ("wq", "bq", "wk", "bk", "wv", "bv", "wo", "bo")))

        attend(0)
        if stage >= 1:
            with nc.sbuf_tensor("acc0", [S, B, D], F32) as env.acc:
                layer_norm(nc, env, True, False)
                dense_and_route_args = (E0, K0, a["l0_gate"], None, a["l0_up"], None, a["l0_down"], None)
                env.slot_token = slot_tables[0]
                dense_and_route(nc, env, 0, *dense_and_route_args)
                slot_indices(nc, env, SLOTS0 // P)
                experts_swiglu(nc, env, a["l0_eup"], a["l0_edown"])
                combine(nc, env, 0, K0)
        clear_semaphores()
        if stage >= 2:
            attend(1)
        if stage >= 3:
            with nc.sbuf_tensor("acc1", [S, B, D], F32) as env.acc:
                layer_norm(nc, env, True, True)
                env.slot_token = slot_tables[1]
                dense_and_route(nc, env, 1, E1, K1, a["l1_gate"], a["l1_gate_b"], a["l1_up"], a["l1_up_b"],
                                a["l1_down"], a["l1_down_b"])
                slot_indices(nc, env, TILES1)
                experts_gelu(nc, env, a["l1_ew"], a["l1_eb1"], a["l1_eb2"])
                combine(nc, env, 1, K1)
        if stage < 3:
            with nc.semaphore("dbg") as dbg, nc.Block() as block:
                @block.sync
                def _(sp):
                    sp.dma_start(out.rearrange("b s d -> s b d"), env.x[:, :, :]).then_inc(dbg, 16)
                    sp.wait_ge(dbg, 16)


def lay_out(i):
    def rows(w):
        w = np.asarray(w)
        s = w.shape
        return np.ascontiguousarray(np.moveaxis(w.reshape(*s[:-2], s[-2] // P, P, s[-1]), -3, -2))

    def col(b):
        b = np.asarray(b)
        return np.ascontiguousarray(np.swapaxes(b.reshape(*b.shape[:-1], -1, P), -1, -2))

    def row(b):
        return np.ascontiguousarray(np.asarray(b).reshape(1, -1))
    i = {k: np.asarray(v) for k, v in i.items()}
    o = {"x": i["x"], "ctxT": rows(i["ctx_1024"].transpose(0, 2, 1)), "mask": i["mask_Bx1xSxS2_ik0"].reshape(B, S, SK),
         "g_xattn": row(i["g_xattn"]), "g_ffn": row(i["g_ffn"])}
    for n, m in (("wq", "w_q"), ("wk", "w_k"), ("wv", "w_v"), ("wo", "w_out")):
        o["l0_" + n] = rows(i["L0_xattn_" + m].T)
    for n, m in (("wq", "Wq"), ("wk", "Wk"), ("wv", "Wv"), ("wo", "Wo")):
        o["l1_" + n] = rows(i["L1_xattn_" + m])
    for n, m0, m1 in (("bq", "b_q", "bq"), ("bk", "b_k", "bk"), ("bv", "b_v", "bv")):
        o["l0_" + n], o["l1_" + n] = col(i["L0_xattn_" + m0]), col(i["L1_xattn_" + m1])
    o["l0_bo"], o["l1_bo"] = row(i["L0_xattn_b_out"]), row(i["L1_xattn_bo"])
    o["l0_gate"] = rows(np.concatenate([i["L0_ffn_gate_w"], i["L0_ffn_shared_gate_w"]], 1))
    o["l0_up"], o["l0_down"] = rows(i["L0_ffn_shared_gate_up_w"]), rows(i["L0_ffn_shared_down_w"])
    o["l0_eup"], o["l0_edown"] = rows(i["L0_ffn_expert_gate_up_w"]), rows(i["L0_ffn_expert_down_w"])
    o["l1_gate"], o["l1_gate_b"] = rows(i["L1_ffn_gate_w"]), row(i["L1_ffn_gate_b"])
    o["l1_up"], o["l1_up_b"] = rows(i["L1_ffn_sh_w1"]), col(i["L1_ffn_sh_b1"])
    o["l1_down"], o["l1_down_b"] = rows(i["L1_ffn_sh_w2"]), row(i["L1_ffn_sh_b2"])
    w1 = rows(i["L1_ffn_ew1"]).reshape(E1, P, DC, I1 // 512, 512).transpose(0, 3, 1, 2, 4)
    w2 = rows(i["L1_ffn_ew2"]).reshape(E1, P, I1 // 512, 4, D).transpose(0, 2, 1, 3, 4)
    o["l1_ew"] = np.concatenate([w1, w2], 1)
    o["l1_eb1"], o["l1_eb2"] = col(i["L1_ffn_eb1"]), i["L1_ffn_eb2"]
    return {k: np.ascontiguousarray(v) for k, v in o.items()}


def kernel(**inputs):
    import concourse.bacc as bacc
    from concourse.bass_utils import run_bass_kernel_spmd

    arrays = lay_out(inputs)
    nc = bacc.Bacc("TRN2", target_bir_lowering=False, num_devices=1)
    aps = {n: nc.dram_tensor("in_" + n, v.shape, mybir.dt.from_np(v.dtype), kind="ExternalInput").ap()
           for n, v in arrays.items()}
    out = nc.dram_tensor("out", (B, S, D), F32, kind="ExternalOutput").ap()
    program(nc, aps, out)
    r = run_bass_kernel_spmd(nc, [{"in_" + n: v for n, v in arrays.items()}], core_ids=[0])
    return r.results[0]["out"]
```

```python
import numpy as np
import concourse.bass as bass
from concourse import mybir
from contextlib import ExitStack

F32 = mybir.dt.float32
F32R = mybir.dt.float32r
I32 = mybir.dt.int32
U32 = mybir.dt.uint32
ALU = mybir.AluOpType
ACT = mybir.ActivationFunctionType
AX = mybir.AxisListType

P = 128
B, S, D = 8, 100, 512
SK = 722
H, DH = 16, 32
DC = D // P
HPC = P // DH
T = B * S
TH = T // 2
SEG = ((0, 512), (512, SK))
KC = -(-SK // P)
KTAIL = SK - (KC - 1) * P
NPIECE = 2 * DC + KC
E0, K0, CAP, I0, IS0 = 64, 8, 256, 256, 1024
E1, K1, I1 = 8, 2, 2048
TILES0 = (T * K0 + E0 * (P - 1)) // P // 2 * 2 + 2
TILES1 = (T * K1 + E1 * (P - 1)) // P
AHEAD0, AHEAD1 = 2, 1
SLOTS0, SLOTS1 = (TILES0 + AHEAD0) * P, (TILES1 + AHEAD1) * P
FULL = float(1 << 20)
EPS = 1e-5
PARTS = ((0, 0), (0, 1), (1, 0))
MASKED = -1.0e30


class Env:
    pass


def layer_norm(nc, env, with_rows, start_acc):
    with ExitStack() as cx:
        def sb(n, s):
            return cx.enter_context(nc.sbuf_tensor(env.name(n), s, F32))

        def sem(n):
            return env.semaphore(n)

        x, xnT, ident = env.x, env.xnT, env.ident
        stats = sb("ln_stats", [S, B, 6])
        mv = sb("ln_mean_var", [S, B, 2])
        std = sb("ln_std", [S, B])
        rstd = sb("ln_rstd", [S, B])
        xn = env.acc if start_acc else sb("ln_xn", [S, B, D])
        pT = [cx.enter_context(nc.psum_tensor(env.name(f"ln_pT{n}"), [P, DC, S], F32)) for n in range(2)]
        stats_done, var_done, std_done, rstd_done = sem("stats_done"), sem("var_done"), sem("std_done"), sem("rstd_done")
        xn_done, turned, copied, rows_out = sem("xn_done"), sem("turned"), sem("copied"), sem("rows_out")
        with nc.Block() as block:
            @block.vector
            def _(dve):
                for t in range(B):
                    dve.bn_stats(stats[:, t, :], x[:, t, :]).then_inc(stats_done, 1)
                for t in range(B):
                    dve.wait_ge(stats_done, t + 1)
                    dve.bn_aggr(mv[:, t, :], stats[:, t, :]).then_inc(var_done, 1)
                dve.wait_ge(var_done, B)
                dve.tensor_scalar(stats[:, :, 0], mv[:, :, 1], EPS, None, ALU.add).then_inc(var_done, 1)
                dve.wait_ge(std_done, 1)
                dve.reciprocal(rstd[:, :], std[:, :]).then_inc(rstd_done, 1)
                dve.wait_ge(rstd_done, 1)
                for t in range(B):
                    dve.tensor_scalar(xn[:, t, :], x[:, t, :], mv[:, t, 0:1], rstd[:, t:t + 1],
                                      ALU.subtract, ALU.mult).then_inc(xn_done, 1)

            @block.scalar
            def _(act):
                act.wait_ge(var_done, B + 1)
                act.activation(std[:, :], stats[:, :, 0], ACT.Sqrt).then_inc(std_done, 1)
                for t in range(B):
                    act.wait_ge(turned, t + 1)
                    act.activation(xnT[:, :, t * S:(t + 1) * S], pT[t % 2][:, :, :], ACT.Copy).then_inc(copied, 1)

            @block.tensor
            def _(pe):
                for t in range(B):
                    pe.wait_ge(xn_done, t + 1)
                    if t >= 2:
                        pe.wait_ge(copied, t - 1)
                    for c in range(DC):
                        last = pe.transpose(pT[t % 2][:, c, :], xn[:, t, c * P:(c + 1) * P], ident[0:S, 0:S])
                    last.then_inc(turned, 1)

            @block.sync
            def _(sp):
                if with_rows:
                    for t in range(B):
                        sp.wait_ge(xn_done, t + 1)
                        sp.dma_start(env.xn_rows[t * S:(t + 1) * S, :], xn[:, t, :]).then_inc(rows_out, 16)
                    sp.wait_ge(rows_out, 16 * B)


def attention(nc, env, layer, masked, w_q, b_q, w_k, b_k, w_v, b_v, w_o, b_o):
    with ExitStack() as cx:
        def sb(n, s, dt=F32):
            return cx.enter_context(nc.sbuf_tensor(env.name(n), s, dt))

        def sem(n):
            return env.semaphore(n)

        x, xnT, ident = env.x, env.xnT, env.ident
        wk = [sb(f"wk{part}", [P, DC, D], F32R) for part in ("_high", "_low")]
        wv = [sb(f"wv{part}", [P, DC, D], F32R) for part in ("_high", "_low")]
        wo = sb("wo", [P, DC, D])
        bq, bk, bv, bo = sb("bq", [P, DC]), sb("bk", [P, DC]), sb("bv", [P, DC]), sb("bo", [S, D])
        qT = sb("qT", [P, DC, T])
        q_done = sem("q_done")

        with ExitStack() as cq:
            wq, wk_raw, wv_raw = (cq.enter_context(nc.sbuf_tensor(env.name(n), [P, DC, D], F32))
                                  for n in ("wq", "wk_raw", "wv_raw"))
            kv_in = [env.semaphore(n) for n in ("wk_in", "wv_in")]
            high_done = env.semaphore("high_done")
            pq = [cq.enter_context(nc.psum_tensor(env.name(f"pq{n}"), [P, TH], F32)) for n in range(2)]
            wq_in, q_mm = (env.semaphore(n) for n in ("wq_in", "q_mm"))
            w_in = env.semaphore("w_in")
            with nc.Block() as block:
                @block.sync
                def _(sp):
                    sp.dma_start(wq[:, :, :], w_q).then_inc(wq_in, 16)
                    sp.dma_start(bq[:, :], b_q).then_inc(wq_in, 16)
                    for n, (dst, src) in enumerate(((wk_raw, w_k), (wv_raw, w_v))):
                        sp.dma_start(dst[:, :, :], src).then_inc(kv_in[n], 16)
                    sp.dma_start(wo[:, :, :], w_o).then_inc(w_in, 16)
                    sp.dma_start(bk[:, :], b_k).then_inc(w_in, 16)
                    sp.dma_start(bv[:, :], b_v).then_inc(w_in, 16)
                    sp.dma_start(bo[:, :], b_o.broadcast_to([S, D])).then_inc(w_in, 16)
                    sp.wait_ge(w_in, 4 * 16)

                @block.tensor
                def _(pe):
                    pe.wait_ge(wq_in, 32)
                    for n in range(2 * DC):
                        m, half = n // 2, n % 2
                        if n >= 2:
                            pe.wait_ge(q_done, n - 1)
                        for c in range(DC):
                            last = pe.matmul(pq[n % 2][:, :], wq[:, c, m * P:(m + 1) * P],
                                             xnT[:, c, half * TH:(half + 1) * TH], start=c == 0, stop=c == DC - 1)
                        last.then_inc(q_mm, 1)

                @block.vector
                def _(dve):
                    dve.wait_ge(wq_in, 32)
                    for n in range(2 * DC):
                        m, half = n // 2, n % 2
                        dve.wait_ge(q_mm, n + 1)
                        dve.tensor_scalar(qT[:, m, half * TH:(half + 1) * TH], pq[n % 2][:, :], bq[:, m:m + 1],
                                          float(DH) ** -0.5, ALU.add, ALU.mult).then_inc(q_done, 1)
                    for n, (raw, w) in enumerate(((wk_raw, wk), (wv_raw, wv))):
                        dve.wait_ge(high_done, n + 1)
                        dve.tensor_tensor(w[1][:, :, :], raw[:, :, :], w[0][:, :, :].bitcast(F32), ALU.subtract)

                @block.scalar
                def _(act):
                    for n, (raw, w) in enumerate(((wk_raw, wk), (wv_raw, wv))):
                        act.wait_ge(kv_in[n], 16)
                        act.activation(w[0][:, :, :], raw[:, :, :], ACT.Copy).then_inc(high_done, 1)

        raw = xnT[:, :, 0:SK]
        ctx = [sb(f"ctx{part}", [P, DC, SK], F32R) for part in ("_high", "_low")]
        kT = [sb(f"kT{part}", [P, DC, SK], F32R) for part in ("_high", "_low")]
        v = [sb(f"v{p}", [P, KC, D]) for p in range(2)]
        qz = [[sb(f"qz{n}{part}", [P, HPC, S], F32R) for part in ("_high", "_low")] for n in range(2)]
        probs = [sb(f"probs{p}", [S, KC * P]) for p in range(2)]
        pTs = sb("pTs", [P, 2, HPC, KC, S])
        aoT = sb("aoT", [P, DC, S])
        stat = sb("stat", [S, H, 4])
        tmp = sb("res_tmp", [S, D])
        ps = [cx.enter_context(nc.psum_tensor(env.name(f"ps{n}"), [P, 1024], F32)) for n in range(2)]
        pt = cx.enter_context(nc.psum_tensor(env.name("pt"), [P, 2, 512], F32))
        pp = cx.enter_context(nc.psum_tensor(env.name("pp"), [P, 512], F32))
        po = cx.enter_context(nc.psum_tensor(env.name("po"), [P, 512], F32))
        if masked:
            zrow, zrow_done, y_zeroed = sb("zrow", [P, D]), sem("zrow_done"), sem("y_zeroed")
            ZT = TILES0 // (B - 2)
            assert ZT * (B - 2) == TILES0
            mraw = sb("mraw", [S, SK], I32)
            madd = [sb(f"madd{p}", [S, SK]) for p in range(2)]
            mask_in, mask_ready = sem("mask_in"), sem("mask_ready")
        ctx_in, high_ready, low_ready, k_high = sem("ctx_in"), sem("high_ready"), sem("low_ready"), sem("k_high")
        zeroed, zeroed_v = sem("zeroed"), sem("zeroed_v")
        q_ready = sem("q_ready")
        piece_mm, piece_out = sem("piece_mm"), sem("piece_out")
        s_mm, max_ready, exp_done = sem("s_mm"), sem("max_ready"), sem("exp_done")
        recip_done, norm_done = sem("recip_done"), sem("norm_done")
        t_mm, t_out, pv_mm, ao_ready = sem("t_mm"), sem("t_out"), sem("pv_mm"), sem("ao_ready")
        o_mm, o_biased, res_done = sem("o_mm"), sem("o_biased"), sem("res_done")
        passed = sem("passed")
        NG = H // HPC

        BESIDE = {3: ("v", 0), 4: ("v", 1), 5: ("k", 0, 0), 6: ("k", 0, 1), 7: ("v", 2), 8: ("v", 3), 9: ("k", 1, 0),
                  10: ("k", 1, 1), 11: ("v", 4), 12: ("k", 2, 0), 13: ("k", 2, 1), 14: ("v", 5), 15: ("k", 3, 0),
                  16: ("k", 3, 1)}
        PIECES = list(BESIDE.values())
        K_ORDER = [x for x in PIECES if x[0] == "k"]
        assert len(PIECES) == NPIECE
        assert all(step >= x[1] * HPC + HPC - 1 for step, x in BESIDE.items() if x[0] == "k")
        SPLIT = {2: (0, 256), 3: (256, 512), 4: (512, SK)}
        NS = len(SPLIT)

        def keys_of(kc):
            return P if kc < KC - 1 else KTAIL

        def at_step(b, p, s):
            return (b, p, s) if s < H else (b + 1, 1 - p, s - H)

        def bank_of(what, first_batch):
            return po if first_batch and PIECES.index(what) % 2 else pp

        def make_piece(pe, what, b, first_batch):
            pk, n = bank_of(what, first_batch), PIECES.index(what)
            if not first_batch:
                pe.wait_ge(piece_out, b * NPIECE + n)
            elif n >= 2:
                pe.wait_ge(piece_out, n - 1)
            end = SEG[what[2]][1] if what[0] == "k" else what[1] * P + keys_of(what[1])
            pe.wait_ge(low_ready, b * NS + 1 + sum(k1 < end for _, k1 in SPLIT.values()))
            for c in range(DC):
                for x, y in PARTS:
                    first, last_one = c == 0 and (x, y) == PARTS[0], c == DC - 1 and (x, y) == PARTS[-1]
                    if what[0] == "k":
                        m, (k0, k1) = what[1], SEG[what[2]]
                        last = pe.matmul(pk[:, 0:k1 - k0], wk[x][:, c, m * P:(m + 1) * P], ctx[y][:, c, k0:k1],
                                         start=first, stop=last_one)
                    else:
                        kc = what[1]
                        last = pe.matmul(pk[0:keys_of(kc), :], ctx[x][:, c, kc * P:kc * P + keys_of(kc)],
                                         wv[y][:, c, :], start=first, stop=last_one)
            last.then_inc(piece_mm, 1)

        def piece_high(act, what, b, first_batch):
            if what[0] == "k":
                m, (k0, k1) = what[1], SEG[what[2]]
                act.wait_ge(piece_mm, b * NPIECE + PIECES.index(what) + 1)
                act.activation(kT[0][:, m, k0:k1], bank_of(what, first_batch)[:, 0:k1 - k0], ACT.Identity,
                               bias=bk[:, m:m + 1]).then_inc(k_high, 1)

        def piece_rest(dve, what, b, p, first_batch):
            pk = bank_of(what, first_batch)
            if what[0] == "k":
                m, (k0, k1) = what[1], SEG[what[2]]
                dve.wait_ge(k_high, b * (2 * DC) + K_ORDER.index(what) + 1)
                dve.scalar_tensor_tensor(out=kT[1][:, m, k0:k1], in0=pk[:, 0:k1 - k0], scalar=bk[:, m:m + 1],
                                         in1=kT[0][:, m, k0:k1].bitcast(F32), op0=ALU.add, op1=ALU.subtract)\
                    .then_inc(piece_out, 1)
            else:
                kc = what[1]
                dve.wait_ge(piece_mm, b * NPIECE + PIECES.index(what) + 1)
                dve.tensor_copy(v[p][0:keys_of(kc), kc, :], pk[0:keys_of(kc), :]).then_inc(piece_out, 1)

        def split_high(act, k0, k1):
            act.activation(ctx[0][:, :, k0:k1], raw[:, :, k0:k1], ACT.Copy).then_inc(high_ready, 1)

        def split_low(dve, k0, k1, n):
            dve.wait_ge(high_ready, n)
            dve.tensor_tensor(ctx[1][:, :, k0:k1], raw[:, :, k0:k1], ctx[0][:, :, k0:k1].bitcast(F32), ALU.subtract)\
                .then_inc(low_ready, 1)

        def over_batches(engine, body):
            with engine.Fori(0, B // 2 - 1) as i:
                for p in range(2):
                    body(i * 2 + p, p, True)
            for p in range(2):
                body(B - 2 + p, p, p == 0)

        with nc.Block() as block:
            @block.sync
            def _(sp):
                sp.dma_start(raw, env.ctxT[0]).then_inc(ctx_in, 16)
                if masked:
                    sp.dma_start(mraw[:, :], env.mask[0]).then_inc(mask_in, 16)
                sp.wait_ge(low_ready, NS)
                sp.dma_start(raw, env.ctxT[1]).then_inc(ctx_in, 16)
                if masked:
                    sp.wait_ge(mask_ready, 1)
                    sp.dma_start(mraw[:, :], env.mask[1]).then_inc(mask_in, 16)
                if masked:
                    sp.wait_ge(zrow_done, 1)
                with sp.Fori(0, B // 2 - 1) as i:
                    for p in range(2):
                        b = i * 2 + p
                        if masked:
                            sp.dma_start(env.y_rows[bass.ds(b * (ZT * P), ZT * P), :]
                                         .rearrange("(z p) n -> p z n", p=P),
                                         zrow[:, :].unsqueeze(1).broadcast_to([P, ZT, D])).then_inc(y_zeroed, 16)
                        sp.wait_ge(low_ready, b * NS + 2 * NS)
                        sp.dma_start(raw, env.ctxT[bass.ds(b + 2, 1), :, :, :]
                                     .rearrange("a p c k -> (a p) c k")).then_inc(ctx_in, 16)
                        if masked:
                            sp.wait_ge(mask_ready, b + 2)
                            sp.dma_start(mraw[:, :], env.mask[bass.ds(b + 2, 1), :, :]
                                         .rearrange("a q k -> (a q) k")).then_inc(mask_in, 16)
                if masked:
                    sp.wait_ge(y_zeroed, 16 * (B - 2))

            @block.gpsimd
            def _(pool):
                if masked:
                    pool.memset(zrow[:, :], 0.0).then_inc(zrow_done, 1)
                for p in range(2):
                    for part in range(2):
                        pool.memset(qz[p][part][:, :, :].bitcast(F32), 0.0).then_inc(zeroed, 1)
                    pool.memset(probs[p][:, SK:], 0.0).then_inc(zeroed, 1)
                pool.wait_ge(zeroed, 6)

                def serial(sem_, value):
                    pool.wait_ge(sem_, value)
                    pool.sem_inc(passed, 1)

                def prepare(b, p):
                    if masked:
                        if not isinstance(b, int):
                            pool.wait_ge(max_ready, b * H - H)
                            pool.sem_inc(passed, 1)
                        pool.wait_ge(mask_in, b * 16 + 16)
                        pool.sem_inc(passed, 1)
                        pool.tensor_scalar(madd[p][:, :], mraw[:, :], 0.0, MASKED, ALU.is_equal, ALU.mult)\
                            .then_inc(mask_ready, 1)
                        serial(mask_ready, b + 1)
                    for g in range(NG):
                        if not isinstance(b, int) or b * NG + g >= 2:
                            pool.wait_ge(s_mm, b * H + HPC * g - HPC)
                            pool.sem_inc(passed, 1)
                        for j in range(HPC):
                            rows = slice(j * DH, (j + 1) * DH)
                            src = qT[rows, g, b * S:(b + 1) * S] if isinstance(b, int) else qT[rows, g, bass.ds(b * S, S)]
                            n = b * (2 * H) + (2 * HPC * g + 2 * j)
                            high, low = (qz[g % 2][part][rows, j, :] for part in range(2))
                            pool.tensor_copy(high, src).then_inc(q_ready, 1)
                            serial(q_ready, n + 1)
                            pool.tensor_tensor(low, src, high.bitcast(F32), ALU.subtract).then_inc(q_ready, 1)
                            serial(q_ready, n + 2)
                for b in range(2):
                    prepare(b, b)
                with pool.Fori(1, B // 2) as i:
                    for p in range(2):
                        prepare(i * 2 + p, p)

            @block.tensor
            def _(pe):
                pe.sem_inc(pv_mm, 2)

                def scores(b, s, first_two=False):
                    c, j = s // HPC, s % HPC
                    if j == 0:
                        pe.wait_ge(q_ready, b * (2 * H) + 2 * HPC * (c + 1))
                        pe.wait_ge(piece_out, b * NPIECE + PIECES.index(("k", c, 1)) + 1)
                    if not first_two:
                        pe.wait_ge(exp_done, b * H + (s - 1))
                    for k0, k1 in SEG:
                        for x, y in PARTS:
                            last = pe.matmul(ps[s % 2][0:S, k0:k1], qz[c % 2][x][:, j, :], kT[y][:, c, k0:k1],
                                             start=(x, y) == PARTS[0], stop=(x, y) == PARTS[-1])
                    last.then_inc(s_mm, 1)

                def transposed(b, s, very_first=False):
                    pe.wait_ge(norm_done, b * H + s + 1)
                    if not very_first:
                        pe.wait_ge(t_out, b * H + s)
                    for kc in range(KC):
                        last = pe.transpose(pt[:, kc // 3, (kc % 3) * S:(kc % 3 + 1) * S],
                                            probs[s % 2][:, kc * P:(kc + 1) * P], ident[0:S, 0:S])
                    last.then_inc(t_mm, 1)

                def weighted_values(b, p, g):
                    pe.wait_ge(t_out, b * H + HPC * (g + 1))
                    pe.wait_ge(piece_out, b * NPIECE + NPIECE)
                    if g > 0:
                        pe.wait_ge(ao_ready, b * NG + g)
                    else:
                        pe.wait_ge(res_done, b + 1)
                    for kc in range(KC):
                        for j in range(HPC):
                            h = g * HPC + j
                            last = pe.matmul(po[j * DH:(j + 1) * DH, 0:S], v[p][:, kc, h * DH:(h + 1) * DH],
                                             pTs[:, g % 2, j, kc, :], start=kc == 0, stop=kc == KC - 1,
                                             skip_group_check=True)
                    last.then_inc(pv_mm, 1)

                for what in PIECES:
                    make_piece(pe, what, 0, True)
                scores(0, 0, True)
                scores(0, 1, True)
                transposed(0, 0, True)

                def body(b, p, more):
                    for step in range(2, H + 2):
                        bb, _, s = at_step(b, p, step)
                        if step < H or more:
                            scores(bb, s)
                        if step % HPC == 1:
                            weighted_values(b, p, step // HPC - 1)
                        if more and step in BESIDE:
                            make_piece(pe, BESIDE[step], b + 1, False)
                        if step <= H or more:
                            tb, _, ts = at_step(b, p, step - 1)
                            transposed(tb, ts)
                    pe.wait_ge(ao_ready, b * NG + NG)
                    for c in range(DC):
                        last = pe.matmul(po[0:S, :], aoT[:, c, :], wo[:, c, :], start=c == 0, stop=c == DC - 1)
                    last.then_inc(o_mm, 1)
                over_batches(pe, body)

            @block.vector
            def _(dve):
                for p in range(2):
                    dve.memset(v[p][:, KC - 1, :], 0.0).then_inc(zeroed_v, 1)
                dve.wait_ge(zeroed_v, 2)
                dve.sem_inc(res_done, 1)
                for n, (k0, k1) in enumerate(SPLIT.values()):
                    split_low(dve, k0, k1, n + 1)
                for what in PIECES:
                    piece_rest(dve, what, 0, 0, True)

                def normalised(b, s):
                    dve.wait_ge(exp_done, b * H + s + 1)
                    dve.reciprocal(stat[:, s, 3:4], stat[:, s, 2:3]).then_inc(recip_done, 1)
                    dve.wait_ge(recip_done, b * H + s + 1)
                    dve.tensor_scalar(probs[s % 2][:, 0:SK], probs[s % 2][:, 0:SK], stat[:, s, 3:4], None,
                                      ALU.mult).then_inc(norm_done, 1)

                def maximum(b, p, s):
                    if masked and s == 0:
                        dve.wait_ge(mask_ready, b + 1)
                        dve.sem_inc(passed, 1)
                    dve.wait_ge(s_mm, b * H + s + 1)
                    scores = ps[s % 2][0:S, 0:SK]
                    if masked:
                        dve.sem_inc(passed, 1)
                        dve.tensor_tensor_reduce(out=scores, in0=scores, in1=madd[p][:, :], scale=-1.0,
                                                 scalar=3.0e38, op0=ALU.add, op1=ALU.min,
                                                 accum_out=stat[:, s, 1:2]).then_inc(max_ready, 1)
                    else:
                        dve.tensor_reduce(stat[:, s, 1:2], scores, AX.X, ALU.max, negate=True)\
                            .then_inc(max_ready, 1)
                maximum(0, 0, 0)
                normalised(0, 0)
                maximum(0, 0, 1)

                def body(b, p, more):
                    for step in range(2, H + 2):
                        if step <= H or more:
                            tb, _, ts = at_step(b, p, step - 1)
                            normalised(tb, ts)
                        if step < H or more:
                            maximum(*at_step(b, p, step))
                        if more and step in SPLIT:
                            split_low(dve, *SPLIT[step], b * NS + NS + (list(SPLIT).index(step) + 1))
                        if more and step in BESIDE:
                            piece_rest(dve, BESIDE[step], b + 1, 1 - p, False)
                    dve.wait_ge(o_mm, b + 1)
                    dve.tensor_tensor(tmp[:, :], po[0:S, :], bo[:, :], ALU.add).then_inc(o_biased, 1)
                    dve.wait_ge(o_biased, b + 1)
                    xb = x[:, b:b + 1, :] if isinstance(b, int) else x[:, bass.ds(b, 1), :]
                    xb = xb.rearrange("q a n -> q (a n)")
                    dve.scalar_tensor_tensor(out=xb, in0=tmp[:, :], scalar=env.gate[0:S, layer:layer + 1], in1=xb,
                                             op0=ALU.mult, op1=ALU.add).then_inc(res_done, 1)
                over_batches(dve, body)

            @block.scalar
            def _(act):
                act.wait_ge(zeroed, 6)
                act.wait_ge(ctx_in, 16)
                for k0, k1 in SPLIT.values():
                    split_high(act, k0, k1)
                for what in PIECES:
                    piece_high(act, what, 0, True)

                def turned(b, s):
                    act.wait_ge(pv_mm, b * NG + s // HPC + 1)
                    act.wait_ge(t_mm, b * H + s + 1)
                    g = s // HPC
                    act.activation(pTs[:, g % 2, s % HPC, :, :].rearrange("k (a c) q -> k a (c q)", a=2),
                                   pt[:, :, 0:3 * S], ACT.Copy).then_inc(t_out, 1)

                def heads_out(b, g):
                    act.wait_ge(pv_mm, b * NG + g + 3)
                    act.activation(aoT[:, g, :], po[:, 0:S], ACT.Identity, bias=bv[:, g:g + 1]).then_inc(ao_ready, 1)

                def exponents(b, s, first_two=False):
                    if not first_two:
                        act.wait_ge(t_mm, b * H + (s - 1))
                    act.wait_ge(max_ready, b * H + s + 1)
                    act.activation(probs[s % 2][:, 0:SK], ps[s % 2][0:S, 0:SK], ACT.Exp, bias=stat[:, s, 1:2],
                                   scale=-1.0 if masked else 1.0,
                                   accum_out=stat[:, s, 2:3]).then_inc(exp_done, 1)
                exponents(0, 0, True)
                exponents(0, 1, True)
                turned(0, 0)

                def body(b, p, more):
                    for step in range(2, H + 2):
                        bb, _, s = at_step(b, p, step)
                        if more and step in SPLIT:
                            if step == min(SPLIT):
                                act.wait_ge(ctx_in, b * 16 + 32)
                                act.wait_ge(piece_mm, b * NPIECE + NPIECE)
                            split_high(act, *SPLIT[step])
                        if step < H or more:
                            exponents(bb, s)
                        if step % HPC == 1:
                            heads_out(b, step // HPC - 1)
                        if more and step in BESIDE:
                            piece_high(act, BESIDE[step], b + 1, False)
                        if step <= H or more:
                            tb, _, ts = at_step(b, p, step - 1)
                            turned(tb, ts)
                over_batches(act, body)


def dense_and_route(nc, env, layer, E, K, gate_w, gate_b, w_up, b_up, w_down, b_down):
    swiglu = layer == 0
    EX = E + 1 if swiglu else E
    FC = (IS0 if swiglu else I1) // P
    slots = SLOTS0 if swiglu else SLOTS1
    with ExitStack() as cx:
        def sb(n, s, dt=F32):
            return cx.enter_context(nc.sbuf_tensor(env.name(n), s, dt))

        def sem(n):
            return env.semaphore(n)

        def pb(n, s):
            return cx.enter_context(nc.psum_tensor(env.name(n), s, F32))

        x, xnT, acc = env.x, env.xnT, env.acc
        UPW = 2 * IS0 if swiglu else I1
        wg, hT = sb("wg", [P, DC, EX]), sb("hT", [P, FC, T])
        wu = sb("wu", [P, DC, UPW])
        wd = sb("wd", [P, 8, D])
        b1 = sb("b1", [P, FC])
        sg = [sb(f"sg{n}", [P, TH]) for n in range(2)]
        up = [sb(f"up{n}", [P, TH]) for n in range(2)]
        rowb = sb("rowb", [S, D])
        gb = sb("gb", [S, E])
        ones, before = sb("ones", [S, S]), sb("before", [S, S])
        iota_i, iota_e = sb("iota_i", [S, E], I32), sb("iota_e", [S, E])
        pack_i, pack_f = sb("pack_i", [S, B, K + 1], I32), sb("pack_f", [S, B, K + 1])
        logit, z = sb("logit", [S, B, E]), sb("z", [S, B])
        red, rsum = sb("red", [S, B]), sb("rsum", [S, B])
        sig = sb("sig", [S, B])
        top, top_i = sb("top", [S, B, 8]), sb("top_i", [S, B, 8], U32)
        top_f = sb("top_f", [S, B, K])
        eq = sb("eq", [S, B, K, E])
        chosen, pos = sb("chosen", [S, B, E]), sb("pos", [S, B, E])
        posk, keep = sb("posk", [S, B, K]), sb("keep", [S, B, K])
        slot_now = [sb(f"slot_now{p}", [S, K + 1], U32) for p in range(2)]
        slot_at = sb("slot_at", [S, B, K + 1], U32)
        pl = pb("pl", [S, 2, 512])
        pg, pu = [pb(f"pg{n}", [P, 512]) for n in range(2)], [pb(f"pu{n}", [P, 512]) for n in range(2)]
        ppos, pcnt = pb("ppos", [S, 512]), pb("pcnt", [S, 512])
        NT = TILES0 if swiglu else TILES1
        LV = CAP // P if swiglu else -(-T // P)
        lvl_i, lvl = sb("lvl_i", [S, LV], I32), sb("lvl", [S, LV])
        tile_i, tile_n = sb("tile_i", [1, NT], I32), sb("tile_n", [1, NT])
        by_level, by_tile = sb("by_level", [S, E, LV]), sb("by_tile", [1, NT, E])
        tiles, ends, base, cnt = sb("tiles", [S, E]), sb("ends", [S, E]), sb("base", [S, E]), sb("cnt", [S, E])
        full = sb("full", [S, B, E])
        texp, tcount = sb("texp", [1, NT]), sb("tcount", [1, 1])
        gate_in, up_in, down_in, small_in = sem("gate_in"), sem("up_in"), sem("down_in"), sem("small_in")
        down2_in = sem("down2_in")
        const_done, pool_step, table_zero = sem("const_done"), sem("pool_step"), sem("table_zero")
        logit_mm, route_step, exp_ready, exp_out = sem("logit_mm"), sem("route_step"), sem("exp_ready"), sem("exp_out")
        chosen_ready, pos_mm, slots_ready = sem("chosen_ready"), sem("pos_mm"), sem("slots_ready")
        up_mm, up_out, hidden = sem("up_mm"), sem("up_out"), sem("hidden")
        down_mm, down_out, acc_step = sem("down_mm"), sem("down_out"), sem("acc_step")
        now_ready, passed = sem("now_ready"), sem("passed")
        scattered = [sem(f"scattered{p}") for p in range(2)]
        NP_ = FC * 2
        ROUTE_AT = NP_ - 4
        NDH = FC // 8

        with nc.Block() as block:
            @block.sync
            def _(sp):
                sp.dma_start(wg[:, :, :], gate_w).then_inc(gate_in, 16)
                sp.dma_start(wu[:, :, :], w_up).then_inc(up_in, 16)
                if not swiglu:
                    sp.dma_start(b1[:, :], b_up).then_inc(up_in, 16)
                    sp.dma_start(gb[:, :], gate_b.broadcast_to([S, E])).then_inc(small_in, 16)
                    sp.dma_start(rowb[:, :], b_down.broadcast_to([S, D])).then_inc(small_in, 16)
                sp.wait_ge(const_done, 1)
                sp.dma_start(env.slot_token[0:slots, :].rearrange("(p n) a -> p (n a)", n=P),
                             env.zero[0:slots // P, :]).then_inc(table_zero, 16)
                sp.dma_start(wd[:, :, :], w_down[:, 0:8, :]).then_inc(down_in, 16)
                if NDH > 1:
                    sp.wait_ge(down_mm, B)
                    sp.dma_start(wd[:, :, :], w_down[:, 8:16, :]).then_inc(down2_in, 16)
                sp.wait_ge(table_zero, 16)

            @block.gpsimd
            def _(pool):
                pool.memset(env.zero[:, :], 0).then_inc(const_done, 1)
                pool.memset(ones[:, :], 1.0).then_inc(pool_step, 1)
                pool.memset(before[:, :], 1.0).then_inc(pool_step, 1)
                pool.wait_ge(pool_step, 2)
                pool.affine_select(out=before[:, :], in_=before[:, :], compare_op=ALU.is_gt, fill=0.0, base=0,
                                   pattern=[[1, S]], channel_multiplier=-1).then_inc(const_done, 1)
                pool.iota(iota_i[:, :], pattern=[[1, E]], base=0, channel_multiplier=0).then_inc(const_done, 1)
                pool.iota(pack_i[:, :, 0:K], pattern=[[S * K, B], [1, K]], base=slots,
                          channel_multiplier=K).then_inc(const_done, 1)
                pool.iota(pack_i[:, :, K:K + 1], pattern=[[S, B], [1, 1]], base=0, channel_multiplier=1)\
                    .then_inc(const_done, 1)
                pool.iota(lvl_i[:, :], pattern=[[P, LV]], base=0, channel_multiplier=0).then_inc(const_done, 1)
                pool.iota(tile_i[:, :], pattern=[[1, NT]], base=0, channel_multiplier=0).then_inc(const_done, 1)
                if swiglu:
                    for n in range(NP_):
                        f, half = n // 2, n % 2
                        pool.wait_ge(up_out, n + 1)
                        pool.tensor_tensor(hT[:, f, half * TH:(half + 1) * TH], sg[n % 2][:, :], up[n % 2][:, :],
                                           ALU.mult).then_inc(hidden, 1)
                pool.wait_ge(table_zero, 16)
                pool.wait_ge(slots_ready, 1)

                def scatter(t, p):
                    at = slot_at[:, t, :] if isinstance(t, int) else \
                        slot_at[:, bass.ds(t, 1), :].rearrange("q a k -> q (a k)")
                    pool.tensor_copy(slot_now[p][:, :], at).then_inc(now_ready, 1)
                    pool.wait_ge(now_ready, t + 1)
                    pool.sem_inc(passed, 1)
                    for k in range(K):
                        pool.indirect_dma_start(
                            out=env.slot_token[:, :], in_=slot_now[p][:, K:K + 1], in_offset=None,
                            out_offset=bass.IndirectOffsetOnAxis(ap=slot_now[p][:, k:k + 1], axis=0))\
                            .then_inc(scattered[p], 16)
                for p in range(2):
                    scatter(p, p)
                with pool.Fori(1, B // 2) as i:
                    for p in range(2):
                        pool.wait_ge(scattered[p], i * (16 * K))
                        pool.sem_inc(passed, 1)
                        scatter(i * 2 + p, p)
                for p in range(2):
                    pool.wait_ge(scattered[p], (B // 2) * 16 * K)

            @block.tensor
            def _(pe):
                pe.wait_ge(gate_in, 16)
                for t in range(B):
                    for c in range(DC):
                        last = pe.matmul(pl[:, t // 4, (t % 4) * EX:(t % 4 + 1) * EX], xnT[:, c, t * S:(t + 1) * S],
                                         wg[:, c, :], start=c == 0, stop=c == DC - 1)
                last.then_inc(logit_mm, 1)
                pe.wait_ge(up_in, 16 if swiglu else 32)
                for n in range(NP_):
                    f, half = n // 2, n % 2
                    if n == ROUTE_AT:
                        pe.wait_ge(chosen_ready, 1)
                        pe.wait_ge(const_done, 2)
                        for t in range(B):
                            for j in range(t + 1):
                                pe.matmul(ppos[:, t * E:(t + 1) * E], (before if j == t else ones)[:, :],
                                          chosen[:, j, :], start=j == 0, stop=j == t)
                        for j in range(B):
                            last = pe.matmul(pcnt[:, 0:E], ones[:, :], chosen[:, j, :], start=j == 0, stop=j == B - 1)
                        last.then_inc(pos_mm, 1)
                    if n >= 2:
                        pe.wait_ge(up_out, n - 1)
                    for dst, off in ((pg, 0), (pu, IS0))[:2 if swiglu else 1]:
                        for c in range(DC):
                            last = pe.matmul(dst[n % 2][:, 0:TH], wu[:, c, off + f * P:off + (f + 1) * P],
                                             xnT[:, c, half * TH:(half + 1) * TH], start=c == 0, stop=c == DC - 1)
                    last.then_inc(up_mm, 1)
                pe.wait_ge(hidden if swiglu else up_out, NP_)
                for hf in range(NDH):
                    pe.wait_ge(down_in if hf == 0 else down2_in, 16)
                    for t in range(B):
                        n = hf * B + t
                        if n >= 2:
                            pe.wait_ge(down_out, n - 1)
                        for f in range(8):
                            last = pe.matmul(pg[n % 2][0:S, :], hT[:, hf * 8 + f, t * S:(t + 1) * S], wd[:, f, :],
                                             start=f == 0, stop=f == 7)
                        last.then_inc(down_mm, 1)

            @block.scalar
            def _(act):
                act.wait_ge(exp_ready, 1)
                act.activation(logit[:, :, :], logit[:, :, :], ACT.Exp).then_inc(exp_out, 1)
                if swiglu:
                    act.activation(z[:, :], z[:, :], ACT.Exp, scale=-1.0).then_inc(exp_out, 1)
                for n in range(NP_):
                    f, half = n // 2, n % 2
                    act.wait_ge(up_mm, n + 1)
                    if swiglu:
                        if n >= 2:
                            act.wait_ge(hidden, n - 1)
                        act.activation(sg[n % 2][:, :], pg[n % 2][:, 0:TH], ACT.Silu)
                        act.activation(up[n % 2][:, :], pu[n % 2][:, 0:TH], ACT.Copy).then_inc(up_out, 1)
                    else:
                        act.activation(hT[:, f, half * TH:(half + 1) * TH], pg[n % 2][:, 0:TH], ACT.Gelu_apprx_tanh,
                                       bias=b1[:, f:f + 1]).then_inc(up_out, 1)

            @block.vector
            def _(dve):
                steps = [0]

                def link(ins):
                    steps[0] += 1
                    ins.then_inc(route_step, 1)
                    dve.wait_ge(route_step, steps[0])

                def over_experts(a):
                    return a.unsqueeze(2).broadcast_to([S, B, E])

                dve.wait_ge(logit_mm, 1)
                for q in range(2):
                    tiles4 = pl[:, q, 0:4 * EX].rearrange("s (t e) -> s t e", e=EX)
                    if swiglu:
                        dve.tensor_copy(z[:, 4 * q:4 * q + 4], tiles4[:, :, E])
                        link(dve.tensor_copy(logit[:, 4 * q:4 * q + 4, :], tiles4[:, :, 0:E]))
                    else:
                        if q == 0:
                            dve.wait_ge(small_in, 32)
                        link(dve.tensor_tensor(logit[:, 4 * q:4 * q + 4, :], tiles4,
                                               gb[:, :].unsqueeze(1).broadcast_to([S, 4, E]), ALU.add))
                link(dve.tensor_reduce(red[:, :], logit[:, :, :], AX.X, ALU.max))
                dve.tensor_tensor(logit[:, :, :], logit[:, :, :], over_experts(red[:, :]), ALU.subtract)\
                    .then_inc(exp_ready, 1)
                dve.wait_ge(exp_out, 2 if swiglu else 1)
                if swiglu:
                    link(dve.tensor_scalar(z[:, :], z[:, :], 1.0, None, ALU.add))
                    link(dve.reciprocal(sig[:, :], z[:, :]))
                link(dve.tensor_reduce(red[:, :], logit[:, :, :], AX.X, ALU.add))
                link(dve.reciprocal(rsum[:, :], red[:, :]))
                link(dve.tensor_tensor(logit[:, :, :], logit[:, :, :], over_experts(rsum[:, :]), ALU.mult))
                for t in range(B):
                    link(dve.max(top[:, t, :], logit[:, t, :]))
                    link(dve.max_index(top_i[:, t, :], top[:, t, :], logit[:, t, :]))
                link(dve.tensor_copy(top_f[:, :, :], top_i[:, :, 0:K]))
                dve.wait_ge(const_done, 7)
                link(dve.tensor_copy(iota_e[:, :], iota_i[:, :]))
                link(dve.tensor_copy(pack_f[:, :, :], pack_i[:, :, :]))
                for t in range(B):
                    link(dve.tensor_tensor(eq[:, t, :, :], iota_e[:, :].unsqueeze(1).broadcast_to([S, K, E]),
                                           top_f[:, t, :].unsqueeze(2).broadcast_to([S, K, E]), ALU.is_equal))
                    link(dve.tensor_reduce(chosen[:, t, :], eq[:, t, :, :].rearrange("s k e -> s e k"), AX.X, ALU.add))
                dve.sem_inc(chosen_ready, 1)
                link(dve.tensor_reduce(red[:, :], top[:, :, 0:K], AX.X, ALU.add))
                if not swiglu:
                    link(dve.tensor_scalar(red[:, :], red[:, :], 1e-9, None, ALU.add))
                link(dve.reciprocal(rsum[:, :], red[:, :]))
                link(dve.tensor_tensor(env.weight[:, :, 0:K], top[:, :, 0:K],
                                       rsum[:, :].unsqueeze(2).broadcast_to([S, B, K]), ALU.mult))
                dve.wait_ge(pos_mm, 1)
                link(dve.tensor_copy(pos[:, :, :], ppos[:, 0:B * E].rearrange("s (t e) -> s t e", e=E)))
                if swiglu:
                    link(dve.tensor_scalar(full[:, :, :], pos[:, :, :], float(CAP), FULL, ALU.is_ge, ALU.mult))
                    link(dve.tensor_tensor(pos[:, :, :], pos[:, :, :], full[:, :, :], ALU.add))
                link(dve.tensor_copy(cnt[:, :], pcnt[:, 0:E]))
                link(dve.tensor_copy(lvl[:, :], lvl_i[:, :]))
                link(dve.tensor_tensor(by_level[:, :, :], cnt[:, :].unsqueeze(2).broadcast_to([S, E, LV]),
                                       lvl[:, :].unsqueeze(1).broadcast_to([S, E, LV]), ALU.is_gt))
                link(dve.tensor_reduce(tiles[:, :], by_level[:, :, :], AX.X, ALU.add))
                link(dve.tensor_tensor_scan(ends[:, :], ones[:, 0:E], tiles[:, :], 0.0, ALU.mult, ALU.add))
                link(dve.tensor_tensor(base[:, :], ends[:, :], tiles[:, :], ALU.subtract))
                link(dve.tensor_scalar(base[:, :], base[:, :], float(P), None, ALU.mult))
                link(dve.tensor_tensor(pos[:, :, :], pos[:, :, :],
                                       base[:, :].unsqueeze(1).broadcast_to([S, B, E]), ALU.add))
                link(dve.tensor_copy(tile_n[:, :], tile_i[:, :]))
                link(dve.tensor_tensor(by_tile[:, :, :], tile_n[:, :].unsqueeze(2).broadcast_to([1, NT, E]),
                                       ends[0:1, :].unsqueeze(1).broadcast_to([1, NT, E]), ALU.is_ge))
                link(dve.tensor_reduce(texp[:, :], by_tile[:, :, :], AX.X, ALU.add))
                link(dve.tensor_scalar(texp[:, :], texp[:, :], float(E - 1), None, ALU.min))
                link(dve.tensor_copy(env.tile_expert[:, 0:NT], texp[:, :]))
                step = 2 if swiglu else 1
                evens = tile_n[:, :].rearrange("a (n s) -> a n s", s=step)[:, :, 0]
                link(dve.tensor_scalar(texp[:, 0:NT // step], evens, ends[0:1, E - 1:E], None, ALU.is_lt))
                link(dve.tensor_reduce(tcount[:, :], texp[:, 0:NT // step], AX.X, ALU.add))
                link(dve.tensor_copy(env.tile_count[:, 0:1], tcount[:, :]))
                link(dve.tensor_copy(env.tile_ends[:, 0:E], ends[0:1, :]))
                for t in range(B):
                    link(dve.tensor_tensor(eq[:, t, :, :], eq[:, t, :, :],
                                           pos[:, t, :].unsqueeze(1).broadcast_to([S, K, E]), ALU.mult))
                    link(dve.tensor_reduce(posk[:, t, :], eq[:, t, :, :], AX.X, ALU.add))
                if swiglu:
                    link(dve.tensor_scalar(keep[:, :, :], posk[:, :, :], FULL, None, ALU.is_lt))
                    link(dve.tensor_tensor(env.weight[:, :, 0:K], env.weight[:, :, 0:K], keep[:, :, :], ALU.mult))
                    link(dve.tensor_tensor(top_f[:, :, :], posk[:, :, :], keep[:, :, :], ALU.mult))
                    link(dve.tensor_tensor(posk[:, :, :], posk[:, :, :], pack_f[:, :, 0:K], ALU.subtract))
                    link(dve.tensor_tensor(posk[:, :, :], posk[:, :, :], keep[:, :, :], ALU.mult))
                    link(dve.tensor_tensor(pack_f[:, :, 0:K], posk[:, :, :], pack_f[:, :, 0:K], ALU.add))
                    link(dve.tensor_copy(env.gather_at[:, :, 0:K], top_f[:, :, :]))
                else:
                    link(dve.tensor_copy(pack_f[:, :, 0:K], posk[:, :, :]))
                    link(dve.tensor_copy(env.gather_at[:, :, 0:K], posk[:, :, :]))
                dve.tensor_copy(slot_at[:, :, :], pack_f[:, :, :]).then_inc(slots_ready, 1)
                if not swiglu:
                    for t in range(B):
                        dve.tensor_tensor(acc[:, t, :], acc[:, t, :], rowb[:, :], ALU.add).then_inc(acc_step, 1)
                    dve.wait_ge(acc_step, B)
                for n in range(NDH * B):
                    t = n % B
                    dve.wait_ge(down_mm, n + 1)
                    if swiglu:
                        dve.tensor_scalar(acc[:, t, :], pg[n % 2][0:S, :], sig[:, t:t + 1], None, ALU.mult)\
                            .then_inc(down_out, 1)
                    else:
                        if n == B:
                            dve.wait_ge(down_out, B)
                        dve.tensor_tensor(acc[:, t, :], pg[n % 2][0:S, :], acc[:, t, :], ALU.add)\
                            .then_inc(down_out, 1)


def slot_indices(nc, env, rows):
    with ExitStack() as cx:
        tab_i = cx.enter_context(nc.sbuf_tensor(env.name("tab_i"), [rows, P], U32))
        tab_f = cx.enter_context(nc.sbuf_tensor(env.name("tab_f"), [rows, P], F32))
        pi = cx.enter_context(nc.psum_tensor(env.name("pi"), [P, 512], F32))
        loaded, as_float, turned, done = (env.semaphore(n)
                                          for n in ("loaded", "as_float", "turned", "done"))
        with nc.Block() as block:
            @block.sync
            def _(sp):
                sp.dma_start(tab_i[:, :], env.slot_token[0:rows * P, :].rearrange("(r n) a -> r (n a)", n=P))\
                    .then_inc(loaded, 16)

            @block.vector
            def _(dve):
                dve.wait_ge(loaded, 16)
                dve.tensor_copy(tab_f[:, :], tab_i[:, :]).then_inc(as_float, 1)
                dve.wait_ge(turned, 1)
                dve.tensor_copy(env.slot_index[:, 0:rows], pi[:, 0:rows]).then_inc(done, 1)

            @block.tensor
            def _(pe):
                pe.wait_ge(as_float, 1)
                pe.transpose(pi[:, 0:rows], tab_f[:, :], env.ident[0:rows, 0:rows]).then_inc(turned, 1)


def experts_swiglu(nc, env, w_gate_up, w_down):
    with ExitStack() as cx:
        def sb(n, s, dt=F32):
            return cx.enter_context(nc.sbuf_tensor(env.name(n), s, dt))

        def sem(n):
            return env.semaphore(n)

        def pb(n, s):
            return cx.enter_context(nc.psum_tensor(env.name(n), s, F32))

        ident = env.ident
        FI = I0 // P
        wgu = [sb(f"wgu{p}", [P, DC, 2 * I0]) for p in range(2)]
        wdn = [sb(f"wdn{p}", [P, FI, D]) for p in range(2)]
        index_now = [sb(f"index_now{p}", [P, 1], U32) for p in range(2)]
        xg = [sb(f"xg{p}", [P, D]) for p in range(2)]
        xT = [sb(f"xT{p}", [P, DC, P]) for p in range(2)]
        sg = [sb(f"sg{p}", [P, I0]) for p in range(2)]
        h = [sb(f"h{p}", [P, I0]) for p in range(2)]
        hT = [sb(f"hT{p}", [P, FI, P]) for p in range(2)]
        y = [sb(f"y{p}", [P, D]) for p in range(2)]
        px, ph = pb("px", [P, DC, P]), pb("ph", [P, 4, P])
        pgu = [pb(f"pgu{p}", [P, 2 * I0]) for p in range(2)]
        pd = [pb(f"pd{p}", [P, D]) for p in range(2)]
        wgu_in, wdn_in = [sem(f"wgu_in{p}") for p in range(2)], [sem(f"wdn_in{p}") for p in range(2)]
        x_in = [sem(f"x_in{p}") for p in range(2)]
        y_stored = [sem(f"y_stored{p}") for p in range(2)]
        index_ready, passed = sem("index_ready"), sem("passed")
        x_mm, x_ready, gu_mm, silu_done, h_ready = sem("x_mm"), sem("x_ready"), sem("gu_mm"), sem("silu_done"), sem("h_ready")
        h_mm, hT_ready, d_mm, y_ready = sem("h_mm"), sem("hT_ready"), sem("d_mm"), sem("y_ready")

        def pairs_of(engine):
            return engine.value_load(env.tile_count[0:1, 0:1], min_val=1, max_val=TILES0 // 2)

        with nc.Block() as block:
            @block.sync
            def _(sp):
                n_pairs = pairs_of(sp)

                def load(t, p, again):
                    at = slice(t, t + 1) if isinstance(t, int) else bass.ds(t, 1)
                    e = sp.value_load(env.tile_expert[0:1, at], min_val=0, max_val=E0 - 1)
                    if again:
                        sp.wait_ge(gu_mm, t - 1)
                    sp.dma_start(wgu[p][:, :, :], w_gate_up[bass.ds(e, 1), :, :, :].rearrange("a p c n -> (a p) c n"))\
                        .then_inc(wgu_in[p], 16)
                    if again:
                        sp.wait_ge(d_mm, t - 1)
                    sp.dma_start(wdn[p][:, :, :], w_down[bass.ds(e, 1), :, :, :].rearrange("a p c n -> (a p) c n"))\
                        .then_inc(wdn_in[p], 16)
                for p in range(2):
                    load(p, p, False)
                with sp.Fori(1, n_pairs) as i:
                    for p in range(2):
                        load(i * 2 + p, p, True)

            @block.gpsimd
            def _(pool):
                n_pairs = pairs_of(pool)

                def fetch(t, p):
                    at = slice(t, t + 1) if isinstance(t, int) else bass.ds(t, 1)
                    pool.tensor_copy(index_now[p][:, :], env.slot_index[:, at]).then_inc(index_ready, 1)
                    pool.wait_ge(index_ready, t + 1)
                    pool.sem_inc(passed, 1)
                    pool.indirect_dma_start(
                        out=xg[p][:, :], out_offset=None, in_=env.xn_rows[:, :],
                        in_offset=bass.IndirectOffsetOnAxis(ap=index_now[p][:, 0:1], axis=0)).then_inc(x_in[p], 16)
                for p in range(2):
                    fetch(p, p)
                with pool.Fori(1, n_pairs + 1) as i:
                    for p in range(2):
                        pool.wait_ge(x_mm, i * 2 + p - 1)
                        pool.sem_inc(passed, 1)
                        pool.wait_ge(x_in[p], i * 16)
                        pool.sem_inc(passed, 1)
                        fetch(i * 2 + p, p)
                for p in range(2):
                    pool.wait_ge(x_in[p], n_pairs * 16 + 16)
                    pool.sem_inc(passed, 1)

            @block.tensor
            def _(pe):
                n_pairs = pairs_of(pe)

                def rows_turned(p, arrived):
                    pe.wait_ge(x_in[p], arrived)
                    for c in range(DC):
                        last = pe.transpose(px[:, c, :], xg[p][:, c * P:(c + 1) * P], ident[:, :])
                    last.then_inc(x_mm, 1)

                def gate_up(t, i, p):
                    pe.wait_ge(wgu_in[p], i * 16 + 16)
                    pe.wait_ge(x_ready, t + 1)
                    for c in range(DC):
                        last = pe.matmul(pgu[p][:, :], xT[p][:, c, :], wgu[p][:, c, :], start=c == 0, stop=c == DC - 1)
                    last.then_inc(gu_mm, 1)

                def hidden_turned(t, p):
                    pe.wait_ge(h_ready, t + 1)
                    for f in range(FI):
                        last = pe.transpose(ph[:, f, :], h[p][:, f * P:(f + 1) * P], ident[:, :])
                    last.then_inc(h_mm, 1)

                def down(t, i, p):
                    pe.wait_ge(wdn_in[p], i * 16 + 16)
                    pe.wait_ge(y_ready, t + 1)
                    pe.wait_ge(hT_ready, t + 1)
                    for f in range(FI):
                        last = pe.matmul(pd[p][:, :], hT[p][:, f, :], wdn[p][:, f, :], start=f == 0, stop=f == FI - 1)
                    last.then_inc(d_mm, 1)

                def tile(t, i, p, ib, first):
                    gate_up(t, i, p)
                    if not first:
                        hidden_turned(t - 1, 1 - p)
                    rows_turned(1 - p, (i + p) * 16 + 16)
                    if not first:
                        down(t - 1, ib, 1 - p)
                rows_turned(0, 16)
                tile(0, 0, 0, 0, True)
                tile(1, 0, 1, 0, False)
                with pe.Fori(1, n_pairs) as i:
                    tile(i * 2, i, 0, i - 1, False)
                    tile(i * 2 + 1, i, 1, i, False)
                hidden_turned(n_pairs * 2 - 1, 1)
                down(n_pairs * 2 - 1, n_pairs - 1, 1)

            @block.scalar
            def _(act):
                n_pairs = pairs_of(act)
                act.sem_inc(y_ready, 2)
                for p in range(2):
                    act.sem_inc(y_stored[p], 16)

                def row_out(t, p, stored):
                    act.wait_ge(d_mm, t + 1)
                    act.wait_ge(y_stored[p], stored)
                    act.activation(y[p][:, :], pd[p][:, :], ACT.Copy).then_inc(y_ready, 1)
                    act.wait_ge(y_ready, t + 3)
                    at = slice(t * P, (t + 1) * P) if isinstance(t, int) else bass.ds(t * P, P)
                    act.dma_start(env.y_rows[at, :], y[p][:, :]).then_inc(y_stored[p], 16)

                def silu(t, p):
                    act.wait_ge(gu_mm, t + 1)
                    act.activation(sg[p][:, :], pgu[p][:, 0:I0], ACT.Silu).then_inc(silu_done, 1)
                silu(0, 0)
                silu(1, 1)
                row_out(0, 0, 16)
                with act.Fori(1, n_pairs) as i:
                    silu(i * 2, 0)
                    row_out(i * 2 - 1, 1, i * 16)
                    silu(i * 2 + 1, 1)
                    row_out(i * 2, 0, i * 16 + 16)
                row_out(n_pairs * 2 - 1, 1, n_pairs * 16)
                for p in range(2):
                    act.wait_ge(y_stored[p], n_pairs * 16 + 16)
                    act.sem_inc(passed, 1)

            @block.vector
            def _(dve):
                n_pairs = pairs_of(dve)

                def rows_out(t, p):
                    dve.wait_ge(x_mm, t + 1)
                    dve.tensor_copy(xT[p][:, :, :], px[:, :, :]).then_inc(x_ready, 1)

                def hidden(t, p):
                    dve.wait_ge(silu_done, t + 1)
                    dve.tensor_tensor(h[p][:, :], sg[p][:, :], pgu[p][:, I0:], ALU.mult).then_inc(h_ready, 1)

                def hidden_out(t, p):
                    dve.wait_ge(h_mm, t + 1)
                    dve.tensor_copy(hT[p][:, :, :], ph[:, 0:FI, :]).then_inc(hT_ready, 1)

                def tile(t, p, first):
                    if not first:
                        hidden_out(t - 1, 1 - p)
                    rows_out(t + 1, 1 - p)
                    hidden(t, p)
                rows_out(0, 0)
                tile(0, 0, True)
                tile(1, 1, False)
                with dve.Fori(1, n_pairs) as i:
                    tile(i * 2, 0, False)
                    tile(i * 2 + 1, 1, False)
                hidden_out(n_pairs * 2 - 1, 1)


def experts_gelu(nc, env, w_chunks, b_up, b_down):
    with ExitStack() as cx:
        def sb(n, s, dt=F32):
            return cx.enter_context(nc.sbuf_tensor(env.name(n), s, dt))

        def sem(n):
            return env.semaphore(n)

        def pb(n, s):
            return cx.enter_context(nc.psum_tensor(env.name(n), s, F32))

        ident = env.ident
        NQ = I1 // 512
        FQ = 512 // P
        NCH = 2 * NQ
        w = [sb(f"w{q}", [P, 4, 512]) for q in range(NCH)]
        b1, b2 = sb("b1", [P, I1]), sb("b2", [P, D])
        index_now, xg, xT = sb("index_now", [P, 1], U32), sb("xg", [P, D]), sb("xT", [P, DC, P])
        hb = [sb(f"hb{n}", [P, 512]) for n in range(2)]
        h = [sb(f"h{n}", [P, 512]) for n in range(2)]
        hT, y = sb("hT", [P, I1 // P, P]), sb("y", [P, D])
        px = pb("px", [P, DC, P])
        pu = [pb(f"pu{n}", [P, 512]) for n in range(2)]
        ph = [pb(f"ph{n}", [P, FQ, P]) for n in range(2)]
        pd = pb("pd", [P, D])
        w_in = [sem(f"w_in{q}") for q in range(NCH)]
        b1_in, b2_in, x_in, y_stored = sem("b1_in"), sem("b2_in"), sem("x_in"), sem("y_stored")
        index_ready, passed = sem("index_ready"), sem("passed")
        x_mm, x_ready, chunk_mm, biased, h_ready = sem("x_mm"), sem("x_ready"), sem("chunk_mm"), sem("biased"), sem("h_ready")
        h_mm, hT_ready, y_ready = sem("h_mm"), sem("hT_ready"), sem("y_ready")

        def tiles_of(engine):
            return engine.value_load(env.tile_count[0:1, 0:1], min_val=1, max_val=TILES1)

        def expert_of(engine, t):
            return engine.value_load(env.tile_expert[0:1, bass.ds(t, 1)], min_val=0, max_val=E1 - 1)

        with nc.Block() as block:
            @block.sync
            def _(sp):
                for e in range(E1):
                    if e > 0:
                        ended = sp.value_load(env.tile_ends[0:1, e - 1:e], min_val=0, max_val=TILES1)

                    def load(dst, src, arrived, used, value):
                        if e > 0:
                            sp.wait_ge(arrived, 16 * e)
                            sp.wait_ge(used, value)
                        sp.dma_start(dst, src).then_inc(arrived, 16)
                    load(b1[:, :], b_up[e:e + 1, :].broadcast_to([P, I1]), b1_in, biased, e and ended * NQ + 1)
                    for q in range(NCH):
                        load(w[q][:, :, :], w_chunks[e, q], w_in[q], chunk_mm, e and ended * NCH + (q + 1))
                    load(b2[:, :], b_down[e:e + 1, :].broadcast_to([P, D]), b2_in, y_ready, e and ended + 1)

            @block.gpsimd
            def _(pool):
                n_tiles = tiles_of(pool)

                def fetch(t):
                    at = slice(t, t + 1) if isinstance(t, int) else bass.ds(t, 1)
                    pool.tensor_copy(index_now[:, :], env.slot_index[:, at]).then_inc(index_ready, 1)
                    pool.wait_ge(index_ready, t + 1)
                    pool.sem_inc(passed, 1)
                    pool.indirect_dma_start(
                        out=xg[:, :], out_offset=None, in_=env.xn_rows[:, :],
                        in_offset=bass.IndirectOffsetOnAxis(ap=index_now[:, 0:1], axis=0)).then_inc(x_in, 16)
                fetch(0)
                with pool.Fori(1, n_tiles + 1) as t:
                    pool.wait_ge(x_mm, t)
                    pool.sem_inc(passed, 1)
                    fetch(t)

            @block.tensor
            def _(pe):
                n_tiles = tiles_of(pe)
                pe.sem_inc(chunk_mm, NCH)

                def rows_turned(t):
                    pe.wait_ge(x_in, t * 16 + 16)
                    for c in range(DC):
                        last = pe.transpose(px[:, c, :], xg[:, c * P:(c + 1) * P], ident[:, :])
                    last.then_inc(x_mm, 1)

                rows_turned(0)
                with pe.Fori(0, n_tiles) as t:
                    e = expert_of(pe, t)

                    def up(q):
                        pe.wait_ge(w_in[q], e * 16 + 16)
                        if q >= 2:
                            pe.wait_ge(biased, t * NQ + q)
                        for c in range(DC):
                            last = pe.matmul(pu[q % 2][:, :], xT[:, c, :], w[q][:, c, :], start=c == 0, stop=c == DC - 1)
                        last.then_inc(chunk_mm, 1)

                    def turned(q):
                        pe.wait_ge(h_ready, t * NQ + q + 1)
                        if q >= 2:
                            pe.wait_ge(hT_ready, t * NQ + q - 1)
                        for f in range(FQ):
                            last = pe.transpose(ph[q % 2][:, f, :], h[q % 2][:, f * P:(f + 1) * P], ident[:, :])
                        last.then_inc(h_mm, 1)

                    def down(q):
                        pe.wait_ge(w_in[NQ + q], e * 16 + 16)
                        pe.wait_ge(hT_ready, t * NQ + q + 1)
                        if q == 0:
                            pe.wait_ge(y_ready, t + 1)
                        for f in range(FQ):
                            last = pe.matmul(pd[:, :], hT[:, q * FQ + f, :], w[NQ + q][:, f, :],
                                             start=q + f == 0, stop=(q == NQ - 1) and (f == FQ - 1))
                        last.then_inc(chunk_mm, 1)
                    pe.wait_ge(x_ready, t + 1)
                    up(0)
                    for q in range(1, NQ):
                        up(q)
                        turned(q - 1)
                    rows_turned(t + 1)
                    down(0)
                    turned(NQ - 1)
                    for q in range(1, NQ):
                        down(q)

            @block.scalar
            def _(act):
                n_tiles = tiles_of(act)
                act.sem_inc(y_stored, 16)
                with act.Fori(0, n_tiles) as t:
                    for q in range(NQ):
                        act.wait_ge(biased, t * NQ + q + 2)
                        if q >= 2:
                            act.wait_ge(h_mm, t * NQ + q - 1)
                        act.activation(h[q % 2][:, :], hb[q % 2][:, :], ACT.Gelu_apprx_tanh).then_inc(h_ready, 1)
                    act.wait_ge(y_ready, t + 2)
                    act.sem_inc(passed, 1)
                    act.dma_start(env.y_rows[bass.ds(t * P, P), :], y[:, :]).then_inc(y_stored, 16)
                act.wait_ge(y_stored, n_tiles * 16 + 16)
                act.sem_inc(passed, 1)

            @block.vector
            def _(dve):
                n_tiles = tiles_of(dve)
                dve.sem_inc(y_ready, 1)
                dve.sem_inc(biased, 1)

                def rows_out(t):
                    dve.wait_ge(x_mm, t + 1)
                    dve.tensor_copy(xT[:, :, :], px[:, :, :]).then_inc(x_ready, 1)

                rows_out(0)
                with dve.Fori(0, n_tiles) as t:
                    e = expert_of(dve, t)

                    def add_bias(q):
                        if q >= 2:
                            dve.wait_ge(h_ready, t * NQ + q - 1)
                        dve.wait_ge(chunk_mm, t * NCH + NCH + q + 1)
                        dve.tensor_tensor(hb[q % 2][:, :], pu[q % 2][:, :], b1[:, q * 512:(q + 1) * 512], ALU.add)\
                            .then_inc(biased, 1)

                    def hidden_out(q):
                        dve.wait_ge(h_mm, t * NQ + q + 1)
                        dve.tensor_copy(hT[:, q * FQ:(q + 1) * FQ, :], ph[q % 2][:, :, :]).then_inc(hT_ready, 1)
                    dve.wait_ge(b1_in, e * 16 + 16)
                    add_bias(0)
                    for q in range(1, NQ):
                        add_bias(q)
                        hidden_out(q - 1)
                    rows_out(t + 1)
                    hidden_out(NQ - 1)
                    dve.wait_ge(b2_in, e * 16 + 16)
                    dve.wait_ge(y_stored, t * 16 + 16)
                    dve.wait_ge(chunk_mm, t * NCH + 2 * NCH)
                    dve.tensor_tensor(y[:, :], pd[:, :], b2[:, :], ALU.add).then_inc(y_ready, 1)


def combine(nc, env, layer, K):
    with ExitStack() as cx:
        def sb(n, s, dt=F32):
            return cx.enter_context(nc.sbuf_tensor(env.name(n), s, dt))

        def sem(n):
            return env.semaphore(n)

        NB = 2 * K
        at_now = [sb(f"at_now{p}", [S, K], U32) for p in range(2)]
        rows = sb("rows", [S, 2, K, D])
        rows_in = [[sem(f"rows_in{p}_{k}") for k in range(K)] for p in range(2)]
        now_ready, used, done, passed, out_sem = sem("now_ready"), sem("used"), sem("done"), sem("passed"), sem("out")
        with nc.Block() as block:
            @block.gpsimd
            def _(pool):
                def fetch(t, p):
                    at = env.gather_at[:, t, 0:K] if isinstance(t, int) else \
                        env.gather_at[:, bass.ds(t, 1), 0:K].rearrange("q a k -> q (a k)")
                    pool.tensor_copy(at_now[p][:, :], at).then_inc(now_ready, 1)
                    pool.wait_ge(now_ready, t + 1)
                    pool.sem_inc(passed, 1)
                    for k in range(K):
                        pool.indirect_dma_start(
                            out=rows[:, p, k, :], out_offset=None, in_=env.y_rows[:, :],
                            in_offset=bass.IndirectOffsetOnAxis(ap=at_now[p][:, k:k + 1], axis=0))\
                            .then_inc(rows_in[p][k], 16)
                for p in range(2):
                    fetch(p, p)
                with pool.Fori(1, B // 2) as i:
                    for p in range(2):
                        t = i * 2 + p
                        pool.wait_ge(used, (t - 1) * K)
                        pool.sem_inc(passed, 1)
                        fetch(t, p)

            @block.vector
            def _(dve):
                with dve.Fori(0, B // 2) as i:
                    for p in range(2):
                        t = i * 2 + p
                        acc_t = env.acc[:, bass.ds(t, 1), :].rearrange("q a n -> q (a n)")
                        x_t = env.x[:, bass.ds(t, 1), :].rearrange("q a n -> q (a n)")
                        for k in range(K):
                            dve.wait_ge(rows_in[p][k], i * 16 + 16)
                            dve.scalar_tensor_tensor(
                                out=acc_t, in0=rows[:, p, k, :],
                                scalar=env.weight[:, bass.ds(t, 1), k:k + 1].rearrange("q a k -> q (a k)"),
                                in1=acc_t, op0=ALU.mult, op1=ALU.add).then_inc(used, 1)
                            dve.wait_ge(used, t * K + k + 1)
                        dve.scalar_tensor_tensor(out=x_t, in0=acc_t, scalar=env.gate[0:S, 2 + layer:3 + layer],
                                                 in1=x_t, op0=ALU.mult, op1=ALU.add).then_inc(done, 1)

            @block.sync
            def _(sp):
                if layer == 1:
                    sp.wait_ge(done, B)
                    sp.dma_start(env.out.rearrange("b s d -> s b d"), env.x[:, :, :]).then_inc(out_sem, 16)
                    sp.wait_ge(out_sem, 16)


def program(nc, a, out, stage=99):
    env = Env()
    count = [0]

    def name(n):
        count[0] += 1
        return f"{n}_{count[0]}"
    env.name = name
    held = []

    def semaphore(n):
        held.append(nc.alloc_semaphore(name(n)))
        return held[-1]
    env.semaphore = semaphore

    def clear_semaphores():
        nc.clear_and_free_semaphores(held)
        held.clear()
        nc.all_engine_barrier()
    env.out = out
    env.ctxT, env.mask = a["ctxT"], a["mask"]
    env.xn_rows = nc.dram_tensor("xn_rows", [T, D], F32).ap()
    env.y_rows = nc.dram_tensor("y_rows", [TILES0 * P, D], F32).ap()
    slot_tables = [nc.dram_tensor(f"slot_token{l}", [n, 1], U32).ap()
                   for l, n in enumerate((SLOTS0 + T * K0, SLOTS1))]
    with ExitStack() as cx:
        def sb(n, s, dt=F32):
            return cx.enter_context(nc.sbuf_tensor(n, s, dt))
        env.x, env.xnT, env.ident = sb("x", [S, B, D]), sb("xnT", [P, DC, T]), sb("ident", [P, P])
        env.gate = sb("gate", [P, 4])
        env.weight, env.gather_at = sb("weight", [S, B, K0]), sb("gather_at", [S, B, K0], U32)
        env.tile_expert, env.tile_count = sb("tile_expert", [1, TILES0], I32), sb("tile_count", [1, 1], I32)
        env.tile_ends = sb("tile_ends", [1, E0], I32)
        env.slot_index = sb("slot_index", [P, SLOTS0 // P], U32)
        env.zero = sb("zero", [P, P], U32)

        with nc.semaphore("start_in") as start_in, nc.semaphore("ident_done") as ident_done, \
                nc.semaphore("gate_done") as gate_done, nc.Block() as block:
            @block.sync
            def _(sp):
                sp.dma_start(env.x[:, :, :], a["x"].rearrange("b s d -> s b d")).then_inc(start_in, 16)
                sp.dma_start(env.gate[:, 0:2], a["g_xattn"].broadcast_to([P, 2])).then_inc(start_in, 16)
                sp.dma_start(env.gate[:, 2:4], a["g_ffn"].broadcast_to([P, 2])).then_inc(start_in, 16)
                sp.wait_ge(start_in, 48)

            @block.gpsimd
            def _(pool):
                pool.memset(env.ident[:, :], 0.0).then_inc(ident_done, 1)
                pool.wait_ge(ident_done, 1)
                pool.affine_select(out=env.ident[:, :], in_=env.ident[:, :], compare_op=ALU.not_equal, fill=1.0,
                                   base=0, pattern=[[-1, P]], channel_multiplier=1).then_inc(ident_done, 1)

            @block.scalar
            def _(act):
                act.wait_ge(start_in, 48)
                act.activation(env.gate[:, :], env.gate[:, :], ACT.Tanh).then_inc(gate_done, 1)

        def attend(layer):
            pre = f"l{layer}_"
            layer_norm(nc, env, False, False)
            attention(nc, env, layer, layer == 0, *(a[pre + n] for n in ("wq", "bq", "wk", "bk", "wv", "bv", "wo", "bo")))

        attend(0)
        if stage >= 1:
            with nc.sbuf_tensor("acc0", [S, B, D], F32) as env.acc:
                layer_norm(nc, env, True, False)
                dense_and_route_args = (E0, K0, a["l0_gate"], None, a["l0_up"], None, a["l0_down"], None)
                env.slot_token = slot_tables[0]
                dense_and_route(nc, env, 0, *dense_and_route_args)
                slot_indices(nc, env, SLOTS0 // P)
                experts_swiglu(nc, env, a["l0_eup"], a["l0_edown"])
                combine(nc, env, 0, K0)
        clear_semaphores()
        if stage >= 2:
            attend(1)
        if stage >= 3:
            with nc.sbuf_tensor("acc1", [S, B, D], F32) as env.acc:
                layer_norm(nc, env, True, True)
                env.slot_token = slot_tables[1]
                dense_and_route(nc, env, 1, E1, K1, a["l1_gate"], a["l1_gate_b"], a["l1_up"], a["l1_up_b"],
                                a["l1_down"], a["l1_down_b"])
                slot_indices(nc, env, SLOTS1 // P)
                experts_gelu(nc, env, a["l1_ew"], a["l1_eb1"], a["l1_eb2"])
                combine(nc, env, 1, K1)
        if stage < 3:
            with nc.semaphore("dbg") as dbg, nc.Block() as block:
                @block.sync
                def _(sp):
                    sp.dma_start(out.rearrange("b s d -> s b d"), env.x[:, :, :]).then_inc(dbg, 16)
                    sp.wait_ge(dbg, 16)


def lay_out(i):
    def rows(w):
        w = np.asarray(w)
        s = w.shape
        return np.ascontiguousarray(np.moveaxis(w.reshape(*s[:-2], s[-2] // P, P, s[-1]), -3, -2))

    def col(b):
        b = np.asarray(b)
        return np.ascontiguousarray(np.swapaxes(b.reshape(*b.shape[:-1], -1, P), -1, -2))

    def row(b):
        return np.ascontiguousarray(np.asarray(b).reshape(1, -1))
    i = {k: np.asarray(v) for k, v in i.items()}
    o = {"x": i["x"], "ctxT": rows(i["ctx_1024"].transpose(0, 2, 1)), "mask": i["mask_Bx1xSxS2_ik0"].reshape(B, S, SK),
         "g_xattn": row(i["g_xattn"]), "g_ffn": row(i["g_ffn"])}
    for n, m in (("wq", "w_q"), ("wk", "w_k"), ("wv", "w_v"), ("wo", "w_out")):
        o["l0_" + n] = rows(i["L0_xattn_" + m].T)
    for n, m in (("wq", "Wq"), ("wk", "Wk"), ("wv", "Wv"), ("wo", "Wo")):
        o["l1_" + n] = rows(i["L1_xattn_" + m])
    for n, m0, m1 in (("bq", "b_q", "bq"), ("bk", "b_k", "bk"), ("bv", "b_v", "bv")):
        o["l0_" + n], o["l1_" + n] = col(i["L0_xattn_" + m0]), col(i["L1_xattn_" + m1])
    o["l0_bo"], o["l1_bo"] = row(i["L0_xattn_b_out"]), row(i["L1_xattn_bo"])
    o["l0_gate"] = rows(np.concatenate([i["L0_ffn_gate_w"], i["L0_ffn_shared_gate_w"]], 1))
    o["l0_up"], o["l0_down"] = rows(i["L0_ffn_shared_gate_up_w"]), rows(i["L0_ffn_shared_down_w"])
    o["l0_eup"], o["l0_edown"] = rows(i["L0_ffn_expert_gate_up_w"]), rows(i["L0_ffn_expert_down_w"])
    o["l1_gate"], o["l1_gate_b"] = rows(i["L1_ffn_gate_w"]), row(i["L1_ffn_gate_b"])
    o["l1_up"], o["l1_up_b"] = rows(i["L1_ffn_sh_w1"]), col(i["L1_ffn_sh_b1"])
    o["l1_down"], o["l1_down_b"] = rows(i["L1_ffn_sh_w2"]), row(i["L1_ffn_sh_b2"])
    o["l1_eb1"] = i["L1_ffn_eb1"]
    w1 = rows(i["L1_ffn_ew1"]).reshape(E1, P, DC, I1 // 512, 512).transpose(0, 3, 1, 2, 4)
    w2 = rows(i["L1_ffn_ew2"]).reshape(E1, P, I1 // 512, 4, D).transpose(0, 2, 1, 3, 4)
    o["l1_ew"] = np.concatenate([w1, w2], 1)
    o["l1_eb2"] = i["L1_ffn_eb2"]
    return {k: np.ascontiguousarray(v) for k, v in o.items()}


def kernel(**inputs):
    import concourse.bacc as bacc
    from concourse.bass_utils import run_bass_kernel_spmd

    arrays = lay_out(inputs)
    nc = bacc.Bacc("TRN2", target_bir_lowering=False, num_devices=1)
    aps = {n: nc.dram_tensor("in_" + n, v.shape, mybir.dt.from_np(v.dtype), kind="ExternalInput").ap()
           for n, v in arrays.items()}
    out = nc.dram_tensor("out", (B, S, D), F32, kind="ExternalOutput").ap()
    program(nc, aps, out)
    r = run_bass_kernel_spmd(nc, [{"in_" + n: v for n, v in arrays.items()}], core_ids=[0])
    return r.results[0]["out"]
```

```python
import numpy as np
import concourse.bass as bass
from concourse import mybir
from contextlib import ExitStack

F32 = mybir.dt.float32
F32R = mybir.dt.float32r
I32 = mybir.dt.int32
U32 = mybir.dt.uint32
ALU = mybir.AluOpType
ACT = mybir.ActivationFunctionType
AX = mybir.AxisListType

P = 128
B, S, D = 8, 100, 512
SK = 722
H, DH = 16, 32
DC = D // P
HPC = P // DH
T = B * S
TH = T // 2
SEG = ((0, 512), (512, SK))
KC = -(-SK // P)
KTAIL = SK - (KC - 1) * P
NPIECE = 2 * DC + KC
E0, K0, CAP, I0, IS0 = 64, 8, 256, 256, 1024
E1, K1, I1 = 8, 2, 2048
TILES0 = (T * K0 + E0 * (P - 1)) // P // 2 * 2 + 2
TILES1 = (T * K1 + E1 * P) // P
AHEAD0, AHEAD1 = 2, 1
SLOTS0, SLOTS1 = (TILES0 + AHEAD0) * P, (TILES1 + AHEAD1) * P
TOKEN_ROWS = T + P
MOE_ROWS = -(-TOKEN_ROWS // P) * P
MIN_PAIRS0 = K0 * (CAP // P) // 2
MIN_TILES1 = -(-T * K1 // P)
FULL = float(1 << 20)
EPS = 1e-5
PARTS = ((0, 0), (0, 1), (1, 0))
MASKED = -1.0e30


class Env:
    pass


def layer_norm(nc, env, with_rows, loads):
    with ExitStack() as cx:
        def sb(n, s):
            return cx.enter_context(nc.sbuf_tensor(env.name(n), s, F32))

        def sem(n):
            return env.semaphore(n)

        x, xnT, ident = env.x, env.xnT, env.ident
        stats = sb("ln_stats", [S, B, 6])
        mv = sb("ln_mean_var", [S, B, 2])
        std = sb("ln_std", [S, B])
        rstd = sb("ln_rstd", [S, B])
        xn = env.acc if with_rows else sb("ln_xn", [S, B, D])
        pT = [cx.enter_context(nc.psum_tensor(env.name(f"ln_pT{n}"), [P, DC, S], F32)) for n in range(2)]
        stats_done, var_done, std_done, rstd_done = sem("stats_done"), sem("var_done"), sem("std_done"), sem("rstd_done")
        xn_done, turned, copied, env.rows_out = sem("xn_done"), sem("turned"), sem("copied"), sem("rows_out")
        with nc.Block() as block:
            @block.vector
            def _(dve):
                for t in range(B):
                    dve.bn_stats(stats[:, t, :], x[:, t, :]).then_inc(stats_done, 1)
                for t in range(B):
                    dve.wait_ge(stats_done, t + 1)
                    dve.bn_aggr(mv[:, t, :], stats[:, t, :]).then_inc(var_done, 1)
                dve.wait_ge(var_done, B)
                dve.tensor_scalar(stats[:, :, 0], mv[:, :, 1], EPS, None, ALU.add).then_inc(var_done, 1)
                dve.wait_ge(std_done, 1)
                dve.reciprocal(rstd[:, :], std[:, :]).then_inc(rstd_done, 1)
                dve.wait_ge(rstd_done, 1)
                for t in range(B):
                    dve.tensor_scalar(xn[:, t, :], x[:, t, :], mv[:, t, 0:1], rstd[:, t:t + 1],
                                      ALU.subtract, ALU.mult).then_inc(xn_done, 1)

            @block.scalar
            def _(act):
                act.wait_ge(var_done, B + 1)
                act.activation(std[:, :], stats[:, :, 0], ACT.Sqrt).then_inc(std_done, 1)
                for t in range(B):
                    act.wait_ge(turned, t + 1)
                    act.activation(xnT[:, :, t * S:(t + 1) * S], pT[t % 2][:, :, :], ACT.Copy).then_inc(copied, 1)

            @block.tensor
            def _(pe):
                for t in range(B):
                    pe.wait_ge(xn_done, t + 1)
                    if t >= 2:
                        pe.wait_ge(copied, t - 1)
                    for c in range(DC):
                        last = pe.transpose(pT[t % 2][:, c, :], xn[:, t, c * P:(c + 1) * P], ident[0:S, 0:S])
                    last.then_inc(turned, 1)

            @block.sync
            def _(sp):
                for dst, src, arrived in loads:
                    sp.dma_start(dst, src).then_inc(arrived, 16)
                if with_rows:
                    for t in range(B):
                        sp.wait_ge(xn_done, t + 1)
                        sp.dma_start(env.xn_rows[t * S:(t + 1) * S, :], xn[:, t, :]).then_inc(env.rows_out, 16)


def attention(nc, env, layer, masked, w_q, b_q, w_k, b_k, w_v, b_v, w_o, b_o):
    with ExitStack() as cx:
        def sb(n, s, dt=F32):
            return cx.enter_context(nc.sbuf_tensor(env.name(n), s, dt))

        def sem(n):
            return env.semaphore(n)

        x, xnT, ident = env.x, env.xnT, env.ident
        wk = [sb(f"wk{part}", [P, DC, D], F32R) for part in ("_high", "_low")]
        wv = [sb(f"wv{part}", [P, DC, D], F32R) for part in ("_high", "_low")]
        wo = sb("wo", [P, DC, D])
        bq, bk, bv, bo = sb("bq", [P, DC]), sb("bk", [P, DC]), sb("bv", [P, DC]), sb("bo", [S, D])
        qT = sb("qT", [P, DC, T])
        q_done = sem("q_done")
        ctx = [sb(f"ctx{part}", [P, DC, SK], F32R) for part in ("_high", "_low")]
        SPLIT = {2: (0, 256), 3: (256, 512), 4: (512, SK)}
        NS = len(SPLIT)
        high_ready, low_ready = sem("high_ready"), sem("low_ready")

        with ExitStack() as cq:
            wq, wk_raw, wv_raw = (cq.enter_context(nc.sbuf_tensor(env.name(n), [P, DC, D], F32))
                                  for n in ("wq", "wk_raw", "wv_raw"))
            kv_in = [env.semaphore(n) for n in ("wk_in", "wv_in")]
            high_done = env.semaphore("high_done")
            wq_in, q_mm = (env.semaphore(n) for n in ("wq_in", "q_mm"))
            first_raw = cq.enter_context(nc.sbuf_tensor(env.name("first_raw"), [P, DC, SK], F32))
            first_in = env.semaphore("first_in")
            layer_norm(nc, env, False, (
                (wq[:, :, :], w_q, wq_in), (bq[:, :], b_q, wq_in), (wk_raw[:, :, :], w_k, kv_in[0]),
                (wv_raw[:, :, :], w_v, kv_in[1]), (first_raw[:, :, :], env.ctxT[0], first_in)))
            pq = [cq.enter_context(nc.psum_tensor(env.name(f"pq{n}"), [P, TH], F32)) for n in range(2)]
            w_in = env.semaphore("w_in")
            with nc.Block() as block:
                @block.sync
                def _(sp):
                    sp.dma_start(wo[:, :, :], w_o).then_inc(w_in, 16)
                    sp.dma_start(bk[:, :], b_k).then_inc(w_in, 16)
                    sp.dma_start(bv[:, :], b_v).then_inc(w_in, 16)
                    sp.dma_start(bo[:, :], b_o.broadcast_to([S, D])).then_inc(w_in, 16)
                    sp.wait_ge(w_in, 4 * 16)

                @block.tensor
                def _(pe):
                    pe.wait_ge(wq_in, 32)
                    for n in range(2 * DC):
                        m, half = n // 2, n % 2
                        if n >= 2:
                            pe.wait_ge(q_done, n - 1)
                        for c in range(DC):
                            last = pe.matmul(pq[n % 2][:, :], wq[:, c, m * P:(m + 1) * P],
                                             xnT[:, c, half * TH:(half + 1) * TH], start=c == 0, stop=c == DC - 1)
                        last.then_inc(q_mm, 1)

                @block.vector
                def _(dve):
                    dve.wait_ge(wq_in, 32)
                    for n in range(2 * DC):
                        m, half = n // 2, n % 2
                        dve.wait_ge(q_mm, n + 1)
                        dve.tensor_scalar(qT[:, m, half * TH:(half + 1) * TH], pq[n % 2][:, :], bq[:, m:m + 1],
                                          float(DH) ** -0.5, ALU.add, ALU.mult).then_inc(q_done, 1)
                        if n in (1, 3):
                            raw_w, w = ((wk_raw, wk), (wv_raw, wv))[n // 2]
                            dve.wait_ge(high_done, n // 2 + 1)
                            dve.tensor_tensor(w[1][:, :, :], raw_w[:, :, :], w[0][:, :, :].bitcast(F32), ALU.subtract)
                        if 4 <= n < 4 + NS:
                            k0, k1 = list(SPLIT.values())[n - 4]
                            dve.wait_ge(high_ready, n - 3)
                            dve.tensor_tensor(ctx[1][:, :, k0:k1], first_raw[:, :, k0:k1],
                                              ctx[0][:, :, k0:k1].bitcast(F32), ALU.subtract).then_inc(low_ready, 1)

                @block.scalar
                def _(act):
                    for n, (raw_w, w) in enumerate(((wk_raw, wk), (wv_raw, wv))):
                        act.wait_ge(kv_in[n], 16)
                        act.activation(w[0][:, :, :], raw_w[:, :, :], ACT.Copy).then_inc(high_done, 1)
                    act.wait_ge(first_in, 16)
                    for k0, k1 in SPLIT.values():
                        act.activation(ctx[0][:, :, k0:k1], first_raw[:, :, k0:k1], ACT.Copy).then_inc(high_ready, 1)

        raw = xnT[:, :, 0:SK]
        kT = [sb(f"kT{part}", [P, DC, SK], F32R) for part in ("_high", "_low")]
        v = [sb(f"v{p}", [P, KC, D]) for p in range(2)]
        qz = [[sb(f"qz{n}{part}", [P, HPC, S], F32R) for part in ("_high", "_low")] for n in range(2)]
        probs = [sb(f"probs{p}", [S, KC * P]) for p in range(2)]
        pTs = sb("pTs", [P, 2, HPC, KC, S])
        aoT = sb("aoT", [P, DC, S])
        stat = sb("stat", [S, H, 4])
        tmp = sb("res_tmp", [S, D])
        ps = [cx.enter_context(nc.psum_tensor(env.name(f"ps{n}"), [P, 1024], F32)) for n in range(2)]
        pt = cx.enter_context(nc.psum_tensor(env.name("pt"), [P, 2, 512], F32))
        pp = cx.enter_context(nc.psum_tensor(env.name("pp"), [P, 512], F32))
        po = cx.enter_context(nc.psum_tensor(env.name("po"), [P, 512], F32))
        if masked:
            zrow, zrow_done, rows_zeroed = sb("zrow", [P, D]), sem("zrow_done"), sem("rows_zeroed")
            mraw = sb("mraw", [S, SK], I32)
            madd = [sb(f"madd{p}", [S, SK]) for p in range(2)]
            mask_in, mask_ready = sem("mask_in"), sem("mask_ready")
        ctx_in, k_high = sem("ctx_in"), sem("k_high")
        zeroed, zeroed_v = sem("zeroed"), sem("zeroed_v")
        q_ready = sem("q_ready")
        piece_mm, piece_out = sem("piece_mm"), sem("piece_out")
        s_mm, max_ready, exp_done = sem("s_mm"), sem("max_ready"), sem("exp_done")
        recip_done, norm_done = sem("recip_done"), sem("norm_done")
        t_mm, t_out, pv_mm, ao_ready = sem("t_mm"), sem("t_out"), sem("pv_mm"), sem("ao_ready")
        o_mm, o_biased, res_done = sem("o_mm"), sem("o_biased"), sem("res_done")
        passed = sem("passed")
        NG = H // HPC

        BESIDE = {3: ("v", 0), 4: ("v", 1), 5: ("k", 0, 0), 6: ("k", 0, 1), 7: ("v", 2), 8: ("v", 3), 9: ("k", 1, 0),
                  10: ("k", 1, 1), 11: ("v", 4), 12: ("k", 2, 0), 13: ("k", 2, 1), 14: ("v", 5), 15: ("k", 3, 0),
                  16: ("k", 3, 1)}
        PIECES = list(BESIDE.values())
        K_ORDER = [x for x in PIECES if x[0] == "k"]
        assert len(PIECES) == NPIECE
        assert all(step >= x[1] * HPC + HPC - 1 for step, x in BESIDE.items() if x[0] == "k")

        def keys_of(kc):
            return P if kc < KC - 1 else KTAIL

        def at_step(b, p, s):
            return (b, p, s) if s < H else (b + 1, 1 - p, s - H)

        def bank_of(what):
            return (pp, po)[PIECES.index(what) % 2]

        def scores_of(s):
            return ps[s % 2][0:S, 0:SK]

        def make_piece(pe, what, b, first_batch=False):
            pk, n = bank_of(what), PIECES.index(what)
            if not first_batch:
                pe.wait_ge(piece_out, b * NPIECE + (n - 1))
            elif n >= 2:
                pe.wait_ge(piece_out, n - 1)
            end = SEG[what[2]][1] if what[0] == "k" else what[1] * P + keys_of(what[1])
            pe.wait_ge(low_ready, b * NS + 1 + sum(k1 < end for _, k1 in SPLIT.values()))
            for c in range(DC):
                for x, y in PARTS:
                    first, last_one = c == 0 and (x, y) == PARTS[0], c == DC - 1 and (x, y) == PARTS[-1]
                    if what[0] == "k":
                        m, (k0, k1) = what[1], SEG[what[2]]
                        last = pe.matmul(pk[:, 0:k1 - k0], wk[x][:, c, m * P:(m + 1) * P], ctx[y][:, c, k0:k1],
                                         start=first, stop=last_one)
                    else:
                        kc = what[1]
                        last = pe.matmul(pk[0:keys_of(kc), :], ctx[x][:, c, kc * P:kc * P + keys_of(kc)],
                                         wv[y][:, c, :], start=first, stop=last_one)
            last.then_inc(piece_mm, 1)

        def piece_high(act, what, b):
            if what[0] == "k":
                m, (k0, k1) = what[1], SEG[what[2]]
                act.wait_ge(piece_mm, b * NPIECE + PIECES.index(what) + 1)
                act.activation(kT[0][:, m, k0:k1], bank_of(what)[:, 0:k1 - k0], ACT.Identity,
                               bias=bk[:, m:m + 1]).then_inc(k_high, 1)

        def piece_rest(dve, what, b, p):
            pk = bank_of(what)
            if what[0] == "k":
                m, (k0, k1) = what[1], SEG[what[2]]
                dve.wait_ge(k_high, b * (2 * DC) + K_ORDER.index(what) + 1)
                dve.scalar_tensor_tensor(out=kT[1][:, m, k0:k1], in0=pk[:, 0:k1 - k0], scalar=bk[:, m:m + 1],
                                         in1=kT[0][:, m, k0:k1].bitcast(F32), op0=ALU.add, op1=ALU.subtract)\
                    .then_inc(piece_out, 1)
            else:
                kc = what[1]
                dve.wait_ge(piece_mm, b * NPIECE + PIECES.index(what) + 1)
                dve.tensor_copy(v[p][0:keys_of(kc), kc, :], pk[0:keys_of(kc), :]).then_inc(piece_out, 1)

        def split_high(act, k0, k1):
            act.activation(ctx[0][:, :, k0:k1], raw[:, :, k0:k1], ACT.Copy).then_inc(high_ready, 1)

        def split_low(dve, k0, k1, n):
            dve.wait_ge(high_ready, n)
            dve.tensor_tensor(ctx[1][:, :, k0:k1], raw[:, :, k0:k1], ctx[0][:, :, k0:k1].bitcast(F32), ALU.subtract)\
                .then_inc(low_ready, 1)

        def over_batches(engine, body):
            with engine.Fori(0, B // 2 - 1) as i:
                for p in range(2):
                    body(i * 2 + p, p, True)
            for p in range(2):
                body(B - 2 + p, p, p == 0)

        with nc.Block() as block:
            @block.sync
            def _(sp):
                if masked:
                    sp.dma_start(mraw[:, :], env.mask[0]).then_inc(mask_in, 16)
                sp.dma_start(raw, env.ctxT[1]).then_inc(ctx_in, 16)
                if masked:
                    sp.wait_ge(mask_ready, 1)
                    sp.dma_start(mraw[:, :], env.mask[1]).then_inc(mask_in, 16)
                if masked:
                    sp.wait_ge(zrow_done, 1)
                    for sums in env.moe_sums:
                        sp.dma_start(sums[:, :].rearrange("(z p) n -> p z n", p=P),
                                     zrow[:, :].unsqueeze(1).broadcast_to([P, MOE_ROWS // P, D]))\
                            .then_inc(rows_zeroed, 16)
                    sp.dma_start(env.xn_rows[T:TOKEN_ROWS, :], zrow[:, :]).then_inc(rows_zeroed, 16)
                with sp.Fori(0, B // 2 - 1) as i:
                    for p in range(2):
                        b = i * 2 + p
                        sp.wait_ge(low_ready, b * NS + 2 * NS)
                        sp.dma_start(raw, env.ctxT[bass.ds(b + 2, 1), :, :, :]
                                     .rearrange("a p c k -> (a p) c k")).then_inc(ctx_in, 16)
                        if masked:
                            sp.wait_ge(mask_ready, b + 2)
                            sp.dma_start(mraw[:, :], env.mask[bass.ds(b + 2, 1), :, :]
                                         .rearrange("a q k -> (a q) k")).then_inc(mask_in, 16)
                if masked:
                    sp.wait_ge(rows_zeroed, 3 * 16)

            @block.gpsimd
            def _(pool):
                if masked:
                    pool.memset(zrow[:, :], 0.0).then_inc(zrow_done, 1)
                for p in range(2):
                    for part in range(2):
                        pool.memset(qz[p][part][:, :, :].bitcast(F32), 0.0).then_inc(zeroed, 1)
                    pool.memset(probs[p][:, SK:], 0.0).then_inc(zeroed, 1)
                pool.wait_ge(zeroed, 6)

                def serial(sem_, value):
                    pool.wait_ge(sem_, value)
                    pool.sem_inc(passed, 1)

                def prepare(b, p):
                    if masked:
                        if not isinstance(b, int):
                            pool.wait_ge(max_ready, b * H - H)
                            pool.sem_inc(passed, 1)
                        pool.wait_ge(mask_in, b * 16 + 16)
                        pool.sem_inc(passed, 1)
                        pool.tensor_scalar(madd[p][:, :], mraw[:, :], 0.0, MASKED, ALU.is_equal, ALU.mult)\
                            .then_inc(mask_ready, 1)
                        serial(mask_ready, b + 1)
                    for g in range(NG):
                        if not isinstance(b, int) or b * NG + g >= 2:
                            pool.wait_ge(s_mm, b * H + HPC * g - HPC)
                            pool.sem_inc(passed, 1)
                        for j in range(HPC):
                            rows = slice(j * DH, (j + 1) * DH)
                            src = qT[rows, g, b * S:(b + 1) * S] if isinstance(b, int) else qT[rows, g, bass.ds(b * S, S)]
                            n = b * (2 * H) + (2 * HPC * g + 2 * j)
                            high, low = (qz[g % 2][part][rows, j, :] for part in range(2))
                            pool.tensor_copy(high, src).then_inc(q_ready, 1)
                            serial(q_ready, n + 1)
                            pool.tensor_tensor(low, src, high.bitcast(F32), ALU.subtract).then_inc(q_ready, 1)
                            serial(q_ready, n + 2)
                for b in range(2):
                    prepare(b, b)
                with pool.Fori(1, B // 2) as i:
                    for p in range(2):
                        prepare(i * 2 + p, p)

            @block.tensor
            def _(pe):
                pe.sem_inc(pv_mm, 2)

                def scores(b, s, first_two=False):
                    c, j = s // HPC, s % HPC
                    if j == 0:
                        pe.wait_ge(q_ready, b * (2 * H) + 2 * HPC * (c + 1))
                        pe.wait_ge(piece_out, b * NPIECE + PIECES.index(("k", c, 1)) + 1)
                    if not first_two:
                        pe.wait_ge(exp_done, b * H + (s - 1))
                    for k0, k1 in SEG:
                        for x, y in PARTS:
                            last = pe.matmul(ps[s % 2][0:S, k0:k1], qz[c % 2][x][:, j, :], kT[y][:, c, k0:k1],
                                             start=(x, y) == PARTS[0], stop=(x, y) == PARTS[-1])
                    last.then_inc(s_mm, 1)

                def transposed(b, s, very_first=False):
                    pe.wait_ge(norm_done, b * H + s + 1)
                    if not very_first:
                        pe.wait_ge(t_out, b * H + s)
                    for kc in range(KC):
                        last = pe.transpose(pt[:, kc // 3, (kc % 3) * S:(kc % 3 + 1) * S],
                                            probs[s % 2][:, kc * P:(kc + 1) * P], ident[0:S, 0:S])
                    last.then_inc(t_mm, 1)

                def weighted_values(b, p, g):
                    pe.wait_ge(t_out, b * H + HPC * (g + 1))
                    pe.wait_ge(piece_out, b * NPIECE + NPIECE)
                    if g > 0:
                        pe.wait_ge(ao_ready, b * NG + g)
                    else:
                        pe.wait_ge(res_done, b + 1)
                    for kc in range(KC):
                        for j in range(HPC):
                            h = g * HPC + j
                            last = pe.matmul(po[j * DH:(j + 1) * DH, 0:S], v[p][:, kc, h * DH:(h + 1) * DH],
                                             pTs[:, g % 2, j, kc, :], start=kc == 0, stop=kc == KC - 1,
                                             skip_group_check=True)
                    last.then_inc(pv_mm, 1)

                for what in PIECES:
                    make_piece(pe, what, 0, True)
                scores(0, 0, True)
                scores(0, 1, True)
                transposed(0, 0, True)

                def body(b, p, more):
                    for step in range(2, H + 2):
                        bb, _, s = at_step(b, p, step)
                        if step < H or more:
                            scores(bb, s)
                        if step % HPC == 1:
                            if more:
                                pe.wait_ge(piece_out, b * NPIECE + (NPIECE + PIECES.index(BESIDE[step - 1]) + 1))
                            weighted_values(b, p, step // HPC - 1)
                        if more and step in BESIDE:
                            if step == HPC:
                                pe.wait_ge(res_done, b + 1)
                            elif step % HPC == 2:
                                pe.wait_ge(ao_ready, b * NG + (step // HPC))
                            make_piece(pe, BESIDE[step], b + 1)
                        if step <= H or more:
                            tb, _, ts = at_step(b, p, step - 1)
                            transposed(tb, ts)
                    pe.wait_ge(ao_ready, b * NG + NG)
                    for c in range(DC):
                        last = pe.matmul(po[0:S, :], aoT[:, c, :], wo[:, c, :], start=c == 0, stop=c == DC - 1)
                    last.then_inc(o_mm, 1)
                over_batches(pe, body)

            @block.vector
            def _(dve):
                for p in range(2):
                    dve.memset(v[p][:, KC - 1, :], 0.0).then_inc(zeroed_v, 1)
                dve.wait_ge(zeroed_v, 2)
                dve.sem_inc(res_done, 1)
                for what in PIECES:
                    piece_rest(dve, what, 0, 0)

                def normalised(b, s):
                    dve.wait_ge(exp_done, b * H + s + 1)
                    dve.reciprocal(stat[:, s, 3:4], stat[:, s, 2:3]).then_inc(recip_done, 1)
                    dve.wait_ge(recip_done, b * H + s + 1)
                    dve.tensor_scalar(probs[s % 2][:, 0:SK], probs[s % 2][:, 0:SK], stat[:, s, 3:4], None,
                                      ALU.mult).then_inc(norm_done, 1)

                def maximum(b, p, s):
                    if masked and s == 0:
                        dve.wait_ge(mask_ready, b + 1)
                        dve.sem_inc(passed, 1)
                    dve.wait_ge(s_mm, b * H + s + 1)
                    scores = scores_of(s)
                    if masked:
                        dve.sem_inc(passed, 1)
                        dve.tensor_tensor_reduce(out=scores, in0=scores, in1=madd[p][:, :], scale=-1.0,
                                                 scalar=3.0e38, op0=ALU.add, op1=ALU.min,
                                                 accum_out=stat[:, s, 1:2]).then_inc(max_ready, 1)
                    else:
                        dve.tensor_reduce(stat[:, s, 1:2], scores, AX.X, ALU.max, negate=True)\
                            .then_inc(max_ready, 1)
                maximum(0, 0, 0)
                normalised(0, 0)
                maximum(0, 0, 1)

                def body(b, p, more):
                    for step in range(2, H + 2):
                        if step <= H or more:
                            tb, _, ts = at_step(b, p, step - 1)
                            normalised(tb, ts)
                        if step < H or more:
                            maximum(*at_step(b, p, step))
                        if more and step in SPLIT:
                            split_low(dve, *SPLIT[step], b * NS + NS + (list(SPLIT).index(step) + 1))
                        if more and step in BESIDE:
                            piece_rest(dve, BESIDE[step], b + 1, 1 - p)
                    dve.wait_ge(o_mm, b + 1)
                    dve.tensor_tensor(tmp[:, :], po[0:S, :], bo[:, :], ALU.add).then_inc(o_biased, 1)
                    dve.wait_ge(o_biased, b + 1)
                    xb = x[:, b:b + 1, :] if isinstance(b, int) else x[:, bass.ds(b, 1), :]
                    xb = xb.rearrange("q a n -> q (a n)")
                    dve.scalar_tensor_tensor(out=xb, in0=tmp[:, :], scalar=env.gate[0:S, layer:layer + 1], in1=xb,
                                             op0=ALU.mult, op1=ALU.add).then_inc(res_done, 1)
                over_batches(dve, body)

            @block.scalar
            def _(act):
                act.wait_ge(zeroed, 6)
                for what in PIECES:
                    piece_high(act, what, 0)

                def turned(b, s):
                    act.wait_ge(pv_mm, b * NG + s // HPC + 1)
                    act.wait_ge(t_mm, b * H + s + 1)
                    g = s // HPC
                    act.activation(pTs[:, g % 2, s % HPC, :, :].rearrange("k (a c) q -> k a (c q)", a=2),
                                   pt[:, :, 0:3 * S], ACT.Copy).then_inc(t_out, 1)

                def heads_out(b, g):
                    act.wait_ge(pv_mm, b * NG + g + 3)
                    act.activation(aoT[:, g, :], po[:, 0:S], ACT.Identity, bias=bv[:, g:g + 1]).then_inc(ao_ready, 1)

                def exponents(b, s, first_two=False):
                    if not first_two:
                        act.wait_ge(t_mm, b * H + (s - 1))
                    act.wait_ge(max_ready, b * H + s + 1)
                    act.activation(probs[s % 2][:, 0:SK], scores_of(s), ACT.Exp, bias=stat[:, s, 1:2],
                                   scale=-1.0 if masked else 1.0,
                                   accum_out=stat[:, s, 2:3]).then_inc(exp_done, 1)
                exponents(0, 0, True)
                exponents(0, 1, True)
                turned(0, 0)

                def body(b, p, more):
                    for step in range(2, H + 2):
                        bb, _, s = at_step(b, p, step)
                        if more and step in SPLIT:
                            if step == min(SPLIT):
                                act.wait_ge(ctx_in, b * 16 + 16)
                                act.wait_ge(piece_mm, b * NPIECE + NPIECE)
                            split_high(act, *SPLIT[step])
                        if step < H or more:
                            exponents(bb, s)
                        if step % HPC == 1:
                            heads_out(b, step // HPC - 1)
                        if more and step in BESIDE:
                            piece_high(act, BESIDE[step], b + 1)
                        if step <= H or more:
                            tb, _, ts = at_step(b, p, step - 1)
                            turned(tb, ts)
                over_batches(act, body)


def dense_and_route(nc, env, layer, E, K, gate_w, gate_b, w_up, b_up, w_down, b_down):
    swiglu = layer == 0
    EX = E + 1 if swiglu else E
    FC = (IS0 if swiglu else I1) // P
    slots = SLOTS0 if swiglu else SLOTS1
    with ExitStack() as cx:
        def sb(n, s, dt=F32):
            return cx.enter_context(nc.sbuf_tensor(env.name(n), s, dt))

        def sem(n):
            return env.semaphore(n)

        def pb(n, s):
            return cx.enter_context(nc.psum_tensor(env.name(n), s, F32))

        x, xnT, acc = env.x, env.xnT, env.acc
        UPW = 2 * IS0 if swiglu else I1
        wg, hT = sb("wg", [P, DC, EX]), sb("hT", [P, FC, T])
        wu = sb("wu", [P, DC, UPW])
        wd = [sb("wd", [P, 8, D]), wu[:, 0:2, :].rearrange("p c (m n) -> p (c m) n", n=D)]
        b1 = sb("b1", [P, FC])
        if swiglu:
            sg, up = ([sb(f"{name}{n}", [P, TH]) for n in range(2)] for name in ("sg", "up"))
        if not swiglu:
            rowb, gb = sb("rowb", [S, D]), sb("gb", [S, E])
        ones, before = sb("ones", [S, S]), sb("before", [S, S])
        iota_i, iota_e = sb("iota_i", [S, E], I32), sb("iota_e", [S, E])
        behind_i, behind = sb("behind_i", [S, B, K], I32), sb("behind", [S, B, K])
        token_i = sb("token_i", [S, B], I32)
        entry = sb("entry", [S, B, K, 2])
        unused_i, unused = sb("unused_i", [P, P], I32), sb("unused", [P, P, 2])
        logit, z = sb("logit", [S, B, E]), sb("z", [S, B])
        red, rsum = sb("red", [S, B]), sb("rsum", [S, B])
        sig = sb("sig", [S, B])
        top, top_i = sb("top", [S, B, 8]), sb("top_i", [S, B, 8], U32)
        top_f = sb("top_f", [S, B, K])
        eq = sb("eq", [S, B, K, E])
        chosen, pos = sb("chosen", [S, B, E]), sb("pos", [S, B, E])
        weight = sb("weight", [S, B, K])
        posk, keep = sb("posk", [S, B, K]), sb("keep", [S, B, K])
        slot_now = [sb(f"slot_now{p}", [S, K], U32) for p in range(2)]
        entry_now = [sb(f"entry_now{p}", [S, K, 2]) for p in range(2)]
        slot_at = sb("slot_at", [S, B, K], U32)
        gate_in, up_in, small_in = sem("gate_in"), sem("up_in"), sem("small_in")
        layer_norm(nc, env, True, [(wg[:, :, :], gate_w, gate_in), (wu[:, :, :], w_up, up_in)] + (
            [] if swiglu else [(b1[:, :], b_up, up_in), (gb[:, :], gate_b.broadcast_to([S, E]), small_in),
                               (rowb[:, :], b_down.broadcast_to([S, D]), small_in)]))
        NM = 2 if swiglu else 1
        wu_by_chunk = wu[:, :, :].rearrange("p c (m n) -> p c m n", m=NM)
        xs = [sb(f"xs{part}", [P, DC, T], F32R) for part in ("_high", "_low")]
        ws = [[sb(f"ws{n}{part}", [P, DC, NM, P], F32R) for part in ("_high", "_low")] for n in range(2)]
        x_high, x_low, w_high, w_low = sem("x_high"), sem("x_low"), sem("w_high"), sem("w_low")
        pl = pb("pl", [S, 2, 512])
        pg, pu = [pb(f"pg{n}", [P, 512]) for n in range(2)], [pb(f"pu{n}", [P, 512]) for n in range(2)]
        ppos, pcnt = pb("ppos", [S, 512]), pb("pcnt", [S, 512])
        NT = TILES0 if swiglu else TILES1 + AHEAD1
        NR = NT // 6 if swiglu else NT
        assert NT % NR == 0
        LV = CAP // P if swiglu else -(-T // P)
        lvl_i, lvl = sb("lvl_i", [S, LV], I32), sb("lvl", [S, LV])
        tile_i, tile_n = sb("tile_i", [1, NT], I32), sb("tile_n", [1, NT])
        by_level, by_tile = sb("by_level", [S, E, LV]), sb("by_tile", [1, NR, E])
        tiles, ends, base, cnt = sb("tiles", [S, E]), sb("ends", [S, E]), sb("base", [S, E]), sb("cnt", [S, E])
        full = sb("full", [S, B, E])
        texp, tcount = sb("texp", [1, NT]), sb("tcount", [1, 1])
        down_in, down2_in = sem("down_in"), sem("down2_in")
        unused_ready = sem("unused_ready")
        const_done, pool_step, table_zero = sem("const_done"), sem("pool_step"), sem("table_zero")
        logit_mm, route_step, exp_ready, exp_out = sem("logit_mm"), sem("route_step"), sem("exp_ready"), sem("exp_out")
        chosen_ready, pos_mm, slots_ready = sem("chosen_ready"), sem("pos_mm"), sem("slots_ready")
        up_mm, up_out, hidden, hidden_late = sem("up_mm"), sem("up_out"), sem("hidden"), sem("hidden_late")
        down_mm, down_out, acc_step = sem("down_mm"), sem("down_out"), sem("acc_step")
        now_ready, passed = sem("now_ready"), sem("passed")
        scattered = [sem(f"scattered{p}") for p in range(2)]
        NP_ = FC * 2
        ROUTE_AT = 6 if swiglu else 12
        BY_POOL = ROUTE_AT + 6
        NDH = FC // 8

        with nc.Block() as block:
            @block.sync
            def _(sp):
                sp.wait_ge(unused_ready, 2)
                sp.dma_start(env.slot_table[0:slots, :].rearrange("(r n) a -> r n a", n=P),
                             unused[0:slots // P, :, :]).then_inc(table_zero, 16)
                sp.dma_start(wd[0][:, :, :], w_down[:, 0:8, :]).then_inc(down_in, 16)
                if NDH > 1:
                    sp.wait_ge(w_low, FC)
                    sp.dma_start(wd[1], w_down[:, 8:16, :]).then_inc(down2_in, 16)
                sp.wait_ge(table_zero, 16)
                sp.wait_ge(env.rows_out, 16 * B)

            @block.gpsimd
            def _(pool):
                pool.memset(unused[:, :, 1:2], 0.0).then_inc(unused_ready, 1)
                pool.iota(unused_i[:, :], pattern=[[1, P]], base=T, channel_multiplier=0).then_inc(const_done, 1)
                pool.wait_ge(const_done, 1)
                pool.wait_ge(unused_ready, 1)
                pool.sem_inc(passed, 1)
                pool.tensor_copy(unused[:, :, 0:1], unused_i[:, :].unsqueeze(2)).then_inc(unused_ready, 1)
                pool.memset(ones[:, :], 1.0).then_inc(pool_step, 1)
                pool.memset(before[:, :], 1.0).then_inc(pool_step, 1)
                pool.wait_ge(pool_step, 2)
                pool.affine_select(out=before[:, :], in_=before[:, :], compare_op=ALU.is_gt, fill=0.0, base=0,
                                   pattern=[[1, S]], channel_multiplier=-1).then_inc(const_done, 1)
                pool.iota(iota_i[:, :], pattern=[[1, E]], base=0, channel_multiplier=0).then_inc(const_done, 1)
                pool.iota(behind_i[:, :, :], pattern=[[S * K, B], [1, K]], base=slots,
                          channel_multiplier=K).then_inc(const_done, 1)
                pool.iota(token_i[:, :], pattern=[[S, B]], base=0, channel_multiplier=1)\
                    .then_inc(const_done, 1)
                pool.iota(lvl_i[:, :], pattern=[[P, LV]], base=0, channel_multiplier=0).then_inc(const_done, 1)
                pool.iota(tile_i[:, :], pattern=[[1, NT]], base=0, channel_multiplier=0).then_inc(const_done, 1)

                def split_low(f):
                    pool.wait_ge(w_high, f + 1)
                    pool.sem_inc(passed, 1)
                    pool.tensor_tensor(ws[f % 2][1][:, :, :, :], wu_by_chunk[:, :, :, f * P:(f + 1) * P],
                                       ws[f % 2][0][:, :, :, :].bitcast(F32), ALU.subtract).then_inc(w_low, 1)
                    pool.wait_ge(w_low, f + 1)
                    pool.sem_inc(passed, 1)
                split_low(0)
                split_low(1)
                for n in range(BY_POOL if swiglu else NP_):
                    f, half = n // 2, n % 2
                    if swiglu:
                        pool.wait_ge(up_out, n + 1)
                        pool.tensor_tensor(hT[:, f, half * TH:(half + 1) * TH], sg[n % 2][:, :], up[n % 2][:, :],
                                           ALU.mult).then_inc(hidden, 1)
                        pool.wait_ge(hidden, n + 1)
                        pool.sem_inc(passed, 1)
                    if half == 1 and f + 2 < FC:
                        split_low(f + 2)
                pool.wait_ge(table_zero, 16)
                pool.wait_ge(slots_ready, 2)
                pool.sem_inc(passed, 1)

                def scatter(t, p):
                    tt = slice(t, t + 1) if isinstance(t, int) else bass.ds(t, 1)
                    pool.tensor_copy(slot_now[p][:, :], slot_at[:, tt, :].rearrange("q a k -> q (a k)"))\
                        .then_inc(now_ready, 1)
                    pool.tensor_copy(entry_now[p][:, :, :].rearrange("q k e -> q (k e)"),
                                     entry[:, tt, :, :].rearrange("q a k e -> q (a k e)")).then_inc(now_ready, 1)
                    pool.wait_ge(now_ready, t * 2 + 2)
                    pool.sem_inc(passed, 1)
                    for k in range(K):
                        pool.indirect_dma_start(
                            out=env.slot_table[:, :], in_=entry_now[p][:, k, :], in_offset=None,
                            out_offset=bass.IndirectOffsetOnAxis(ap=slot_now[p][:, k:k + 1], axis=0))\
                            .then_inc(scattered[p], 16)
                for p in range(2):
                    scatter(p, p)
                with pool.Fori(1, B // 2) as i:
                    for p in range(2):
                        pool.wait_ge(scattered[p], i * (16 * K))
                        pool.sem_inc(passed, 1)
                        scatter(i * 2 + p, p)
                for p in range(2):
                    pool.wait_ge(scattered[p], (B // 2) * 16 * K)

            @block.tensor
            def _(pe):
                pe.wait_ge(gate_in, 16)
                for t in range(B):
                    for c in range(DC):
                        last = pe.matmul(pl[:, t // 4, (t % 4) * EX:(t % 4 + 1) * EX], xnT[:, c, t * S:(t + 1) * S],
                                         wg[:, c, :], start=c == 0, stop=c == DC - 1)
                last.then_inc(logit_mm, 1)
                pe.wait_ge(x_low, 1)
                for n in range(NP_):
                    f, half = n // 2, n % 2
                    if n == ROUTE_AT:
                        pe.wait_ge(chosen_ready, 1)
                        pe.wait_ge(const_done, 2)
                        for t in range(B):
                            for j in range(t + 1):
                                pe.matmul(ppos[:, t * E:(t + 1) * E], (before if j == t else ones)[:, :],
                                          chosen[:, j, :], start=j == 0, stop=j == t)
                        for j in range(B):
                            last = pe.matmul(pcnt[:, 0:E], ones[:, :], chosen[:, j, :], start=j == 0, stop=j == B - 1)
                        last.then_inc(pos_mm, 1)
                    if n >= 2:
                        pe.wait_ge(up_out, n - 1)
                    pe.wait_ge(w_low, f + 1)
                    for m, dst in enumerate((pg, pu)[:NM]):
                        for c in range(DC):
                            for i, j in PARTS:
                                last = pe.matmul(dst[n % 2][:, 0:TH], ws[f % 2][i][:, c, m, :],
                                                 xs[j][:, c, half * TH:(half + 1) * TH],
                                                 start=c == 0 and (i, j) == PARTS[0],
                                                 stop=c == DC - 1 and (i, j) == PARTS[-1])
                    last.then_inc(up_mm, 1)
                pe.wait_ge(hidden if swiglu else up_out, BY_POOL if swiglu else NP_)
                if swiglu:
                    pe.wait_ge(hidden_late, NP_ - BY_POOL)
                for hf in range(NDH):
                    pe.wait_ge(down_in if hf == 0 else down2_in, 16)
                    for t in range(B):
                        n = hf * B + t
                        if n >= 2:
                            pe.wait_ge(down_out, n - 1)
                        for f in range(8):
                            last = pe.matmul(pg[n % 2][0:S, :], hT[:, hf * 8 + f, t * S:(t + 1) * S], wd[hf][:, f, :],
                                             start=f == 0, stop=f == 7)
                        last.then_inc(down_mm, 1)

            @block.scalar
            def _(act):
                act.activation(xs[0][:, :, :], xnT[:, :, :], ACT.Copy).then_inc(x_high, 1)
                act.wait_ge(up_in, 16 if swiglu else 32)

                def split_high(f):
                    if f >= 2:
                        act.wait_ge(up_mm, 2 * f - 2)
                    act.activation(ws[f % 2][0][:, :, :, :], wu_by_chunk[:, :, :, f * P:(f + 1) * P], ACT.Copy)\
                        .then_inc(w_high, 1)
                split_high(0)
                split_high(1)
                act.wait_ge(exp_ready, 1)
                act.activation(logit[:, :, :], logit[:, :, :], ACT.Exp).then_inc(exp_out, 1)
                if swiglu:
                    act.activation(z[:, :], z[:, :], ACT.Exp, scale=-1.0).then_inc(exp_out, 1)
                for n in range(NP_):
                    f, half = n // 2, n % 2
                    act.wait_ge(up_mm, n + 1)
                    if swiglu:
                        if 2 <= n < BY_POOL + 2:
                            act.wait_ge(hidden, n - 1)
                        elif n >= 2:
                            act.wait_ge(hidden_late, n - 1 - BY_POOL)
                        act.activation(sg[n % 2][:, :], pg[n % 2][:, 0:TH], ACT.Silu)
                        act.activation(up[n % 2][:, :], pu[n % 2][:, 0:TH], ACT.Copy).then_inc(up_out, 1)
                    else:
                        act.activation(hT[:, f, half * TH:(half + 1) * TH], pg[n % 2][:, 0:TH], ACT.Gelu_apprx_tanh,
                                       bias=b1[:, f:f + 1]).then_inc(up_out, 1)
                    if half == 1 and f + 2 < FC:
                        split_high(f + 2)

            @block.vector
            def _(dve):
                steps = [0]

                def link(ins):
                    steps[0] += 1
                    ins.then_inc(route_step, 1)
                    dve.wait_ge(route_step, steps[0])

                def over_experts(a):
                    return a.unsqueeze(2).broadcast_to([S, B, E])

                dve.wait_ge(x_high, 1)
                dve.tensor_tensor(xs[1][:, :, :], xnT[:, :, :], xs[0][:, :, :].bitcast(F32), ALU.subtract)\
                    .then_inc(x_low, 1)
                dve.wait_ge(logit_mm, 1)
                for q in range(2):
                    tiles4 = pl[:, q, 0:4 * EX].rearrange("s (t e) -> s t e", e=EX)
                    if swiglu:
                        dve.tensor_copy(z[:, 4 * q:4 * q + 4], tiles4[:, :, E])
                        link(dve.tensor_copy(logit[:, 4 * q:4 * q + 4, :], tiles4[:, :, 0:E]))
                    else:
                        if q == 0:
                            dve.wait_ge(small_in, 32)
                        link(dve.tensor_tensor(logit[:, 4 * q:4 * q + 4, :], tiles4,
                                               gb[:, :].unsqueeze(1).broadcast_to([S, 4, E]), ALU.add))
                link(dve.tensor_reduce(red[:, :], logit[:, :, :], AX.X, ALU.max))
                dve.tensor_tensor(logit[:, :, :], logit[:, :, :], over_experts(red[:, :]), ALU.subtract)\
                    .then_inc(exp_ready, 1)
                dve.wait_ge(exp_out, 2 if swiglu else 1)
                if swiglu:
                    link(dve.tensor_scalar(z[:, :], z[:, :], 1.0, None, ALU.add))
                    link(dve.reciprocal(sig[:, :], z[:, :]))
                link(dve.tensor_reduce(red[:, :], logit[:, :, :], AX.X, ALU.add))
                link(dve.reciprocal(rsum[:, :], red[:, :]))
                link(dve.tensor_tensor(logit[:, :, :], logit[:, :, :], over_experts(rsum[:, :]), ALU.mult))
                for t in range(B):
                    link(dve.max(top[:, t, :], logit[:, t, :]))
                    link(dve.max_index(top_i[:, t, :], top[:, t, :], logit[:, t, :]))
                link(dve.tensor_copy(top_f[:, :, :], top_i[:, :, 0:K]))
                dve.wait_ge(const_done, 7)
                link(dve.tensor_copy(iota_e[:, :], iota_i[:, :]))
                link(dve.tensor_copy(behind[:, :, :], behind_i[:, :, :]))
                for k in range(K):
                    link(dve.tensor_copy(entry[:, :, k, 0], token_i[:, :]))
                for t in range(B):
                    link(dve.tensor_tensor(eq[:, t, :, :], iota_e[:, :].unsqueeze(1).broadcast_to([S, K, E]),
                                           top_f[:, t, :].unsqueeze(2).broadcast_to([S, K, E]), ALU.is_equal))
                    link(dve.tensor_reduce(chosen[:, t, :], eq[:, t, :, :].rearrange("s k e -> s e k"), AX.X, ALU.add))
                dve.sem_inc(chosen_ready, 1)
                link(dve.tensor_reduce(red[:, :], top[:, :, 0:K], AX.X, ALU.add))
                if not swiglu:
                    link(dve.tensor_scalar(red[:, :], red[:, :], 1e-9, None, ALU.add))
                link(dve.reciprocal(rsum[:, :], red[:, :]))
                link(dve.tensor_tensor(weight[:, :, :], top[:, :, 0:K],
                                       rsum[:, :].unsqueeze(2).broadcast_to([S, B, K]), ALU.mult))
                dve.wait_ge(pos_mm, 1)
                link(dve.tensor_copy(pos[:, :, :], ppos[:, 0:B * E].rearrange("s (t e) -> s t e", e=E)))
                if swiglu:
                    link(dve.tensor_scalar(full[:, :, :], pos[:, :, :], float(CAP), FULL, ALU.is_ge, ALU.mult))
                    link(dve.tensor_tensor(pos[:, :, :], pos[:, :, :], full[:, :, :], ALU.add))
                link(dve.tensor_copy(cnt[:, :], pcnt[:, 0:E]))
                link(dve.tensor_copy(lvl[:, :], lvl_i[:, :]))
                link(dve.tensor_tensor(by_level[:, :, :], cnt[:, :].unsqueeze(2).broadcast_to([S, E, LV]),
                                       lvl[:, :].unsqueeze(1).broadcast_to([S, E, LV]), ALU.is_gt))
                link(dve.tensor_reduce(tiles[:, :], by_level[:, :, :], AX.X, ALU.add))
                if not swiglu:
                    link(dve.tensor_scalar(tiles[:, :], tiles[:, :], 1.0, None, ALU.max))
                link(dve.tensor_tensor_scan(ends[:, :], ones[:, 0:E], tiles[:, :], 0.0, ALU.mult, ALU.add))
                link(dve.tensor_tensor(base[:, :], ends[:, :], tiles[:, :], ALU.subtract))
                link(dve.tensor_scalar(base[:, :], base[:, :], float(P), None, ALU.mult))
                link(dve.tensor_tensor(pos[:, :, :], pos[:, :, :],
                                       base[:, :].unsqueeze(1).broadcast_to([S, B, E]), ALU.add))
                for t in range(B):
                    link(dve.tensor_tensor(eq[:, t, :, :], eq[:, t, :, :],
                                           pos[:, t, :].unsqueeze(1).broadcast_to([S, K, E]), ALU.mult))
                    link(dve.tensor_reduce(posk[:, t, :], eq[:, t, :, :], AX.X, ALU.add))
                if swiglu:
                    link(dve.tensor_scalar(keep[:, :, :], posk[:, :, :], FULL, None, ALU.is_lt))
                    link(dve.tensor_tensor(weight[:, :, :], weight[:, :, :], keep[:, :, :], ALU.mult))
                    link(dve.tensor_tensor(posk[:, :, :], posk[:, :, :], behind[:, :, :], ALU.subtract))
                    link(dve.tensor_tensor(posk[:, :, :], posk[:, :, :], keep[:, :, :], ALU.mult))
                    link(dve.tensor_tensor(posk[:, :, :], posk[:, :, :], behind[:, :, :], ALU.add))
                dve.tensor_copy(entry[:, :, :, 1], weight[:, :, :]).then_inc(slots_ready, 1)
                dve.tensor_copy(slot_at[:, :, :], posk[:, :, :]).then_inc(slots_ready, 1)
                dve.wait_ge(env.rows_out, 16 * B)
                if swiglu:
                    for n in range(BY_POOL, NP_):
                        f, half = n // 2, n % 2
                        dve.wait_ge(up_out, n + 1)
                        dve.tensor_tensor(hT[:, f, half * TH:(half + 1) * TH], sg[n % 2][:, :], up[n % 2][:, :],
                                          ALU.mult).then_inc(hidden_late, 1)
                else:
                    for t in range(B):
                        dve.tensor_tensor(acc[:, t, :], acc[:, t, :], rowb[:, :], ALU.add).then_inc(acc_step, 1)
                    dve.wait_ge(acc_step, B)
                link(dve.tensor_copy(tile_n[:, :], tile_i[:, :]))

                def look_up(r):
                    link(dve.tensor_tensor(by_tile[:, :, :],
                                           tile_n[:, r:r + NR].unsqueeze(2).broadcast_to([1, NR, E]),
                                           ends[0:1, :].unsqueeze(1).broadcast_to([1, NR, E]), ALU.is_ge))
                    link(dve.tensor_reduce(texp[:, r:r + NR], by_tile[:, :, :], AX.X, ALU.add))

                def tile_tables():
                    link(dve.tensor_scalar(texp[:, :], texp[:, :], float(E - 1), None, ALU.min))
                    link(dve.tensor_copy(env.tile_expert[:, 0:NT], texp[:, :]))
                    step = 2 if swiglu else 1
                    evens = tile_n[:, :].rearrange("a (n s) -> a n s", s=step)[:, :, 0]
                    link(dve.tensor_scalar(texp[:, 0:NT // step], evens, ends[0:1, E - 1:E], None, ALU.is_lt))
                    link(dve.tensor_reduce(tcount[:, :], texp[:, 0:NT // step], AX.X, ALU.add))
                    link(dve.tensor_copy(env.tile_count[:, 0:1], tcount[:, :]))
                    link(dve.tensor_scalar(tcount[:, :], tcount[:, :], -1.0, None, ALU.add))
                    link(dve.tensor_copy(env.tile_count[:, 1:2], tcount[:, :]))
                    link(dve.tensor_copy(env.tile_ends[:, 0:E], ends[0:1, :]))
                for n in range(NDH * B):
                    t = n % B
                    dve.wait_ge(down_mm, n + 1)
                    if swiglu:
                        dve.tensor_scalar(acc[:, t, :], pg[n % 2][0:S, :], sig[:, t:t + 1], None, ALU.mult)\
                            .then_inc(down_out, 1)
                    else:
                        if n == B:
                            dve.wait_ge(down_out, B)
                        dve.tensor_tensor(acc[:, t, :], pg[n % 2][0:S, :], acc[:, t, :], ALU.add)\
                            .then_inc(down_out, 1)
                    if n < NT // NR:
                        look_up(n * NR)
                    if n == NT // NR:
                        tile_tables()


def slot_indices(nc, env, rows):
    with ExitStack() as cx:
        table = cx.enter_context(nc.sbuf_tensor(env.name("table"), [rows, P, 2], F32))
        pi = cx.enter_context(nc.psum_tensor(env.name("pi"), [P, 2, P], F32))
        loaded, turned, done = (env.semaphore(n) for n in ("loaded", "turned", "done"))
        with nc.Block() as block:
            @block.sync
            def _(sp):
                sp.dma_start(table[:, :, :], env.slot_table[0:rows * P, :].rearrange("(r n) a -> r n a", n=P))\
                    .then_inc(loaded, 16)

            @block.vector
            def _(dve):
                dve.wait_ge(turned, 1)
                dve.tensor_copy(env.slot_token[:, 0:rows], pi[:, 0, 0:rows]).then_inc(done, 1)
                dve.tensor_copy(env.slot_weight[:, 0:rows], pi[:, 1, 0:rows]).then_inc(done, 1)

            @block.tensor
            def _(pe):
                pe.wait_ge(loaded, 16)
                for n in range(2):
                    last = pe.transpose(pi[:, n, 0:rows], table[:, :, n], env.ident[0:rows, 0:rows])
                last.then_inc(turned, 1)


def experts_swiglu(nc, env, w_gate_up, w_down):
    with ExitStack() as cx:
        def sb(n, s, dt=F32):
            return cx.enter_context(nc.sbuf_tensor(env.name(n), s, dt))

        def sem(n):
            return env.semaphore(n)

        def pb(n, s):
            return cx.enter_context(nc.psum_tensor(env.name(n), s, F32))

        ident = env.ident
        FI = I0 // P
        wgu = [sb(f"wgu{p}", [P, DC, 2 * I0]) for p in range(2)]
        wdn = [sb(f"wdn{p}", [P, FI, D]) for p in range(2)]
        index_now = [sb(f"index_now{p}", [P, 1], U32) for p in range(2)]
        sum_at = sb("sum_at", [P, 1], U32)
        xg = [sb(f"xg{p}", [P, D]) for p in range(2)]
        xT = [sb(f"xT{p}", [P, DC, P]) for p in range(2)]
        sg = [sb(f"sg{p}", [P, I0]) for p in range(2)]
        h = [sb(f"h{p}", [P, I0]) for p in range(2)]
        hT = [sb(f"hT{p}", [P, FI, P]) for p in range(2)]
        y = [sb(f"y{p}", [P, D]) for p in range(2)]
        px, ph = pb("px", [P, DC, P]), pb("ph", [P, 4, P])
        pgu = [pb(f"pgu{p}", [P, 2 * I0]) for p in range(2)]
        pd = [pb(f"pd{p}", [P, D]) for p in range(2)]
        wgu_in, wdn_in = [sem(f"wgu_in{p}") for p in range(2)], [sem(f"wdn_in{p}") for p in range(2)]
        x_in = [sem(f"x_in{p}") for p in range(2)]
        added, sum_at_ready = sem("added"), sem("sum_at_ready")
        index_ready, passed = sem("index_ready"), sem("passed")
        x_mm, x_ready, gu_mm, silu_done, h_ready = sem("x_mm"), sem("x_ready"), sem("gu_mm"), sem("silu_done"), sem("h_ready")
        h_mm, hT_ready, d_mm, y_ready = sem("h_mm"), sem("hT_ready"), sem("d_mm"), sem("y_ready")

        def last_pair_of(engine):
            return engine.value_load(env.tile_count[0:1, 1:2], min_val=MIN_PAIRS0 - 1, max_val=TILES0 // 2 - 1)

        def pairs_of(engine):
            return engine.value_load(env.tile_count[0:1, 0:1], min_val=MIN_PAIRS0, max_val=TILES0 // 2)

        with nc.Block() as block:
            @block.sync
            def _(sp):
                def expert_of(t):
                    at = slice(t, t + 1) if isinstance(t, int) else bass.ds(t, 1)
                    return sp.value_load(env.tile_expert[0:1, at], min_val=0, max_val=E0 - 1)

                def load_gate_up(t, p, again=True):
                    e = expert_of(t)
                    if again:
                        sp.wait_ge(gu_mm, t - 1)
                    sp.dma_start(wgu[p][:, :, :], w_gate_up[bass.ds(e, 1), :, :, :].rearrange("a p c n -> (a p) c n"))\
                        .then_inc(wgu_in[p], 16)

                def load_down(t, p, used=None):
                    e = expert_of(t)
                    if used is not None:
                        sp.wait_ge(d_mm, used)
                    sp.dma_start(wdn[p][:, :, :], w_down[bass.ds(e, 1), :, :, :].rearrange("a p c n -> (a p) c n"))\
                        .then_inc(wdn_in[p], 16)
                load_gate_up(0, 0, False)
                load_gate_up(1, 1, False)
                load_down(0, 0)
                load_gate_up(2, 0)
                load_down(1, 1)
                with sp.Fori(1, last_pair_of(sp)) as i:
                    load_gate_up(i * 2 + 1, 1)
                    load_down(i * 2, 0, i * 2 - 1)
                    load_gate_up(i * 2 + 2, 0)
                    load_down(i * 2 + 1, 1, i * 2)
                last = last_pair_of(sp)
                load_gate_up(last * 2 + 1, 1)
                load_down(last * 2, 0, last * 2)
                load_down(last * 2 + 1, 1, last * 2)

            @block.gpsimd
            def _(pool):
                n_pairs = pairs_of(pool)

                def fetch(t, p):
                    at = slice(t, t + 1) if isinstance(t, int) else bass.ds(t, 1)
                    pool.tensor_copy(index_now[p][:, :], env.slot_token[:, at]).then_inc(index_ready, 1)
                    pool.wait_ge(index_ready, t + 1)
                    pool.sem_inc(passed, 1)
                    pool.indirect_dma_start(
                        out=xg[p][:, :], out_offset=None, in_=env.xn_rows[:, :],
                        in_offset=bass.IndirectOffsetOnAxis(ap=index_now[p][:, 0:1], axis=0)).then_inc(x_in[p], 16)
                def fetch_next(i, p):
                    pool.wait_ge(x_mm, i * 2 + (p - 1))
                    pool.sem_inc(passed, 1)
                    pool.wait_ge(x_in[p], i * 16)
                    pool.sem_inc(passed, 1)
                    fetch(i * 2 + p, p)

                def add_rows(i, p, very_first=False):
                    t = i * 2 + p
                    at = slice(t, t + 1) if isinstance(t, int) else bass.ds(t, 1)
                    if not very_first:
                        pool.wait_ge(added, t * 16)
                        pool.sem_inc(passed, 1)
                    pool.tensor_copy(sum_at[:, :], env.slot_token[:, at]).then_inc(sum_at_ready, 1)
                    pool.wait_ge(sum_at_ready, t + 1)
                    pool.sem_inc(passed, 1)
                    pool.wait_ge(y_ready, t + 3)
                    pool.sem_inc(passed, 1)
                    pool.indirect_dma_start(
                        out=env.moe_sum[:, :], in_=y[p][:, :], in_offset=None, compute_op=ALU.add,
                        out_offset=bass.IndirectOffsetOnAxis(ap=sum_at[:, 0:1], axis=0)).then_inc(added, 16)
                for p in range(2):
                    fetch(p, p)
                for p in range(2):
                    fetch_next(1, p)
                for p in range(2):
                    fetch_next(2, p)
                    add_rows(0, p, p == 0)
                with pool.Fori(3, n_pairs + 1) as i:
                    for p in range(2):
                        fetch_next(i, p)
                        add_rows(i - 2, p)
                last = last_pair_of(pool)
                for p in range(2):
                    add_rows(last, p)
                pool.wait_ge(added, n_pairs * 32)
                pool.sem_inc(passed, 1)
                for p in range(2):
                    pool.wait_ge(x_in[p], n_pairs * 16 + 16)
                    pool.sem_inc(passed, 1)

            @block.tensor
            def _(pe):
                n_pairs = pairs_of(pe)

                def rows_turned(p, arrived):
                    pe.wait_ge(x_in[p], arrived)
                    for c in range(DC):
                        last = pe.transpose(px[:, c, :], xg[p][:, c * P:(c + 1) * P], ident[:, :])
                    last.then_inc(x_mm, 1)

                def gate_up(t, i, p):
                    pe.wait_ge(wgu_in[p], i * 16 + 16)
                    pe.wait_ge(x_ready, t + 1)
                    for c in range(DC):
                        last = pe.matmul(pgu[p][:, :], xT[p][:, c, :], wgu[p][:, c, :], start=c == 0, stop=c == DC - 1)
                    last.then_inc(gu_mm, 1)

                def hidden_turned(t, p):
                    pe.wait_ge(h_ready, t + 1)
                    for f in range(FI):
                        last = pe.transpose(ph[:, f, :], h[p][:, f * P:(f + 1) * P], ident[:, :])
                    last.then_inc(h_mm, 1)

                def down(t, i, p):
                    pe.wait_ge(wdn_in[p], i * 16 + 16)
                    pe.wait_ge(y_ready, t + 1)
                    pe.wait_ge(hT_ready, t + 1)
                    for f in range(FI):
                        last = pe.matmul(pd[p][:, :], hT[p][:, f, :], wdn[p][:, f, :], start=f == 0, stop=f == FI - 1)
                    last.then_inc(d_mm, 1)

                def tile(t, i, p, ib, first):
                    gate_up(t, i, p)
                    if not first:
                        hidden_turned(t - 1, 1 - p)
                    rows_turned(1 - p, (i + p) * 16 + 16)
                    if not first:
                        down(t - 1, ib, 1 - p)
                rows_turned(0, 16)
                tile(0, 0, 0, 0, True)
                tile(1, 0, 1, 0, False)
                with pe.Fori(1, n_pairs) as i:
                    tile(i * 2, i, 0, i - 1, False)
                    tile(i * 2 + 1, i, 1, i, False)
                hidden_turned(n_pairs * 2 - 1, 1)
                down(n_pairs * 2 - 1, n_pairs - 1, 1)

            @block.scalar
            def _(act):
                n_pairs = pairs_of(act)
                act.sem_inc(y_ready, 2)

                def row_out(t, p, before=None):
                    act.wait_ge(d_mm, t + 1)
                    if before is not None:
                        act.wait_ge(added, before)
                    at = slice(t, t + 1) if isinstance(t, int) else bass.ds(t, 1)
                    act.activation(y[p][:, :], pd[p][:, :], ACT.Copy, scale=env.slot_weight[:, at]).then_inc(y_ready, 1)

                def silu(t, p):
                    act.wait_ge(gu_mm, t + 1)
                    act.activation(sg[p][:, :], pgu[p][:, 0:I0], ACT.Silu).then_inc(silu_done, 1)
                silu(0, 0)
                silu(1, 1)
                row_out(0, 0)
                silu(2, 0)
                row_out(1, 1)
                silu(3, 1)
                row_out(2, 0, 16)
                with act.Fori(2, n_pairs) as i:
                    silu(i * 2, 0)
                    row_out(i * 2 - 1, 1, i * 32 - 32)
                    silu(i * 2 + 1, 1)
                    row_out(i * 2, 0, i * 32 - 16)
                last_pair = last_pair_of(act)
                row_out(last_pair * 2 + 1, 1, last_pair * 32)

            @block.vector
            def _(dve):
                n_pairs = pairs_of(dve)

                def rows_out(t, p):
                    dve.wait_ge(x_mm, t + 1)
                    dve.tensor_copy(xT[p][:, :, :], px[:, :, :]).then_inc(x_ready, 1)

                def hidden(t, p):
                    dve.wait_ge(silu_done, t + 1)
                    dve.tensor_tensor(h[p][:, :], sg[p][:, :], pgu[p][:, I0:], ALU.mult).then_inc(h_ready, 1)

                def hidden_out(t, p):
                    dve.wait_ge(h_mm, t + 1)
                    dve.tensor_copy(hT[p][:, :, :], ph[:, 0:FI, :]).then_inc(hT_ready, 1)

                def tile(t, p, first):
                    if not first:
                        hidden_out(t - 1, 1 - p)
                    rows_out(t + 1, 1 - p)
                    hidden(t, p)
                rows_out(0, 0)
                tile(0, 0, True)
                tile(1, 1, False)
                with dve.Fori(1, n_pairs) as i:
                    tile(i * 2, 0, False)
                    tile(i * 2 + 1, 1, False)
                hidden_out(n_pairs * 2 - 1, 1)


def experts_gelu(nc, env, w_chunks, b_up, b_down):
    with ExitStack() as cx:
        def sb(n, s, dt=F32):
            return cx.enter_context(nc.sbuf_tensor(env.name(n), s, dt))

        def sem(n):
            return env.semaphore(n)

        def pb(n, s):
            return cx.enter_context(nc.psum_tensor(env.name(n), s, F32))

        ident = env.ident
        NQ = I1 // 512
        FQ = 512 // P
        NCH = 2 * NQ
        w = [sb(f"w{q}", [P, 4, 512]) for q in range(NCH)]
        b1, b2 = sb("b1", [P, I1]), sb("b2", [P, D])
        index_now, xg = sb("index_now", [P, 1], U32), sb("xg", [P, D])
        xT = [sb(f"xT{part}", [P, DC, P], F32R) for part in ("_high", "_low")]
        WS, WS_DOWN = (0, 1, 2, 1), {1: 0, 2: 2}
        ws = [[sb(f"ws{n}{part}", [P, 4, 512], F32R) for part in ("_high", "_low")] for n in range(3)]
        x_high = sem("x_high")
        w_high, w_low = [sem(f"w_high{q}") for q in range(NQ)], [sem(f"w_low{q}") for q in range(NQ)]
        hb = [sb(f"hb{n}", [P, 512]) for n in range(2)]
        h = [sb(f"h{n}", [P, 512]) for n in range(2)]
        hT = sb("hT", [P, 2, FQ, P])
        hs = [sb(f"hs{part}", [P, 2, FQ, P], F32R) for part in ("_high", "_low")]
        y, yb = sb("y", [P, D]), sb("yb", [P, D])
        d_high, d_low = ({q: sem(f"{name}{q}") for q in WS_DOWN} for name in ("d_high", "d_low"))
        hs_high, hs_ready = sem("hs_high"), sem("hs_ready")
        px = pb("px", [P, DC, P])
        pu = [pb(f"pu{n}", [P, 512]) for n in range(2)]
        ph = [pb(f"ph{n}", [P, FQ, P]) for n in range(2)]
        pd = pb("pd", [P, D])
        w_in = [sem(f"w_in{q}") for q in range(NCH)]
        b1_in, b2_in, x_in, added = sem("b1_in"), sem("b2_in"), sem("x_in"), sem("added")
        sum_at, sum_at_ready, y_biased = sb("sum_at", [P, 1], U32), sem("sum_at_ready"), sem("y_biased")
        index_ready, passed = sem("index_ready"), sem("passed")
        x_mm, x_ready, biased, h_ready = sem("x_mm"), sem("x_ready"), sem("biased"), sem("h_ready")
        up_mm, down_mm = sem("up_mm"), sem("down_mm")
        h_mm, hT_ready, y_ready = sem("h_mm"), sem("hT_ready"), sem("y_ready")

        def last_tile_of(engine):
            return engine.value_load(env.tile_count[0:1, 1:2], min_val=MIN_TILES1 - 1, max_val=TILES1 - 1)

        def tiles_of(engine):
            return engine.value_load(env.tile_count[0:1, 0:1], min_val=MIN_TILES1, max_val=TILES1)

        def expert_of(engine, t):
            at = slice(t, t + 1) if isinstance(t, int) else bass.ds(t, 1)
            return engine.value_load(env.tile_expert[0:1, at], min_val=0, max_val=E1 - 1)

        with nc.Block() as block:
            @block.sync
            def _(sp):
                for q in range(NCH):
                    if q == NQ:
                        sp.dma_start(b1[:, :], b_up[0:1, :].broadcast_to([P, I1])).then_inc(b1_in, 16)
                    sp.dma_start(w[q][:, :, :], w_chunks[0, q]).then_inc(w_in[q], 16)
                sp.dma_start(b2[:, :], b_down[0:1, :].broadcast_to([P, D])).then_inc(b2_in, 16)
                for e in range(1, E1):
                    ended = sp.value_load(env.tile_ends[0:1, e - 1:e], min_val=0, max_val=TILES1)

                    def load(dst, src, arrived, used, value):
                        sp.wait_ge(arrived, 16 * e)
                        sp.wait_ge(used, value)
                        sp.dma_start(dst, src).then_inc(arrived, 16)
                    for q in range(NCH):
                        if q < NQ:
                            used, value = w_low[q], ended + 1
                        elif q - NQ in WS_DOWN:
                            used, value = d_low[q - NQ], ended + 1
                        else:
                            used, value = down_mm, ended * NQ + (q - NQ + 1)
                        if q == NQ:
                            load(b1[:, :], b_up[e:e + 1, :].broadcast_to([P, I1]), b1_in, biased, ended * NQ + 1)
                        load(w[q][:, :, :], w_chunks[e, q], w_in[q], used, value)
                    load(b2[:, :], b_down[e:e + 1, :].broadcast_to([P, D]), b2_in, y_ready, ended + 1)

            @block.gpsimd
            def _(pool):
                n_tiles = tiles_of(pool)

                def fetch(t):
                    at = slice(t, t + 1) if isinstance(t, int) else bass.ds(t, 1)
                    pool.tensor_copy(index_now[:, :], env.slot_token[:, at]).then_inc(index_ready, 1)
                    pool.wait_ge(index_ready, t + 1)
                    pool.sem_inc(passed, 1)
                    pool.indirect_dma_start(
                        out=xg[:, :], out_offset=None, in_=env.xn_rows[:, :],
                        in_offset=bass.IndirectOffsetOnAxis(ap=index_now[:, 0:1], axis=0)).then_inc(x_in, 16)
                def add_rows(t, very_first=False):
                    at = slice(t, t + 1) if isinstance(t, int) else bass.ds(t, 1)
                    if not very_first:
                        pool.wait_ge(added, t * 16)
                        pool.sem_inc(passed, 1)
                    pool.tensor_copy(sum_at[:, :], env.slot_token[:, at]).then_inc(sum_at_ready, 1)
                    pool.wait_ge(sum_at_ready, t + 1)
                    pool.sem_inc(passed, 1)
                    pool.wait_ge(y_ready, t + 2)
                    pool.sem_inc(passed, 1)
                    pool.indirect_dma_start(
                        out=env.moe_sum[:, :], in_=y[:, :], in_offset=None, compute_op=ALU.add,
                        out_offset=bass.IndirectOffsetOnAxis(ap=sum_at[:, 0:1], axis=0)).then_inc(added, 16)

                def fetch_next(t):
                    pool.wait_ge(x_mm, t)
                    pool.sem_inc(passed, 1)
                    fetch(t)
                fetch(0)
                fetch_next(1)
                fetch_next(2)
                add_rows(0, True)
                with pool.Fori(3, n_tiles + 1) as t:
                    fetch_next(t)
                    add_rows(t - 2)
                add_rows(last_tile_of(pool))
                pool.wait_ge(added, n_tiles * 16)
                pool.sem_inc(passed, 1)

            @block.tensor
            def _(pe):
                n_tiles = tiles_of(pe)
                pe.sem_inc(down_mm, NQ)

                def rows_turned(t):
                    pe.wait_ge(x_in, t * 16 + 16)
                    for c in range(DC):
                        last = pe.transpose(px[:, c, :], xg[:, c * P:(c + 1) * P], ident[:, :])
                    last.then_inc(x_mm, 1)

                rows_turned(0)
                with pe.Fori(0, n_tiles) as t:
                    e = expert_of(pe, t)

                    def up(q):
                        pe.wait_ge(w_low[q], t + 2)
                        if q >= 2:
                            pe.wait_ge(biased, t * NQ + q)
                        for c in range(DC):
                            for i, j in PARTS:
                                last = pe.matmul(pu[q % 2][:, :], xT[i][:, c, :], ws[WS[q]][j][:, c, :],
                                                 start=c == 0 and (i, j) == PARTS[0],
                                                 stop=c == DC - 1 and (i, j) == PARTS[-1])
                        last.then_inc(up_mm, 1)

                    def turned(q):
                        pe.wait_ge(h_ready, t * NQ + q + 1)
                        if q >= 2:
                            pe.wait_ge((hT_ready, hs_ready)[q % 2], t * 2 + 1)
                        for f in range(FQ):
                            last = pe.transpose(ph[q % 2][:, f, :], h[q % 2][:, f * P:(f + 1) * P], ident[:, :])
                        last.then_inc(h_mm, 1)

                    def down(q):
                        if q == 0:
                            pe.wait_ge(y_ready, t + 1)
                        if q in WS_DOWN:
                            pe.wait_ge(d_low[q], t + 2)
                            pe.wait_ge(hs_ready, t * 2 + q // 2 + 1)
                            parts = [(hs[i][:, q // 2], ws[WS_DOWN[q]][j]) for i, j in PARTS]
                        else:
                            pe.wait_ge(w_in[NQ + q], e * 16 + 16)
                            pe.wait_ge(hT_ready, t * 2 + q // 2 + 1)
                            parts = [(hT[:, q // 2], w[NQ + q])]
                        for f in range(FQ):
                            for n, (hidden, weight) in enumerate(parts):
                                last = pe.matmul(pd[:, :], hidden[:, f, :], weight[:, f, :], start=q + f + n == 0,
                                                 stop=(q, f, n) == (NQ - 1, FQ - 1, len(parts) - 1))
                        last.then_inc(down_mm, 1)
                    pe.wait_ge(x_ready, t + 1)
                    up(0)
                    up(1)
                    turned(0)
                    up(2)
                    turned(1)
                    down(0)
                    up(3)
                    turned(2)
                    down(1)
                    rows_turned(t + 1)
                    turned(3)
                    down(2)
                    down(3)

            @block.scalar
            def _(act):
                n_tiles = tiles_of(act)

                def split_high(t, q, e):
                    act.wait_ge(w_in[q], e * 16 + 16)
                    act.activation(ws[WS[q]][0][:, :, :], w[q][:, :, :], ACT.Copy).then_inc(w_high[q], 1)

                def split_down_high(t, q, e):
                    act.wait_ge(w_in[NQ + q], e * 16 + 16)
                    act.activation(ws[WS_DOWN[q]][0][:, :, :], w[NQ + q][:, :, :], ACT.Copy).then_inc(d_high[q], 1)

                def x_high_out(t):
                    act.wait_ge(x_mm, t + 1)
                    act.activation(xT[0][:, :, :], px[:, :, :], ACT.Copy).then_inc(x_high, 1)
                e0 = expert_of(act, 0)
                x_high_out(0)
                for q in range(3):
                    split_high(0, q, e0)
                with act.Fori(0, n_tiles) as t:
                    e, e_next = expert_of(act, t), expert_of(act, t + 1)

                    def gelu(q):
                        act.wait_ge(biased, t * NQ + q + 2)
                        if q >= 2:
                            act.wait_ge(h_mm, t * NQ + q - 1)
                        act.activation(h[q % 2][:, :], hb[q % 2][:, :], ACT.Gelu_apprx_tanh).then_inc(h_ready, 1)

                    def up_done(q):
                        act.wait_ge(up_mm, t * NQ + q + 1)

                    def down_done(q):
                        act.wait_ge(down_mm, t * NQ + (NQ + q + 1))

                    def hidden_out(q):
                        act.wait_ge(h_mm, t * NQ + q + 1)
                        dst, ready = (hs[0], hs_high) if q in WS_DOWN else (hT, hT_ready)
                        act.activation(dst[:, q // 2], ph[q % 2][:, :, :], ACT.Copy).then_inc(ready, 1)
                    gelu(0)
                    up_done(1)
                    split_high(t, 3, e)
                    gelu(1)
                    hidden_out(0)
                    up_done(0)
                    split_down_high(t, 1, e)
                    gelu(2)
                    hidden_out(1)
                    up_done(2)
                    split_down_high(t, 2, e)
                    gelu(3)
                    hidden_out(2)
                    up_done(3)
                    split_high(t + 1, 1, e_next)
                    x_high_out(t + 1)
                    hidden_out(3)
                    down_done(1)
                    split_high(t + 1, 0, e_next)
                    down_done(2)
                    split_high(t + 1, 2, e_next)

            @block.vector
            def _(dve):
                n_tiles = tiles_of(dve)
                dve.sem_inc(y_ready, 1)
                dve.sem_inc(biased, 1)

                for q in range(NQ):
                    dve.sem_inc(w_low[q], 1)
                for q in WS_DOWN:
                    dve.sem_inc(d_low[q], 1)

                def split_low(t, q):
                    dve.wait_ge(w_high[q], t + 1)
                    dve.tensor_tensor(ws[WS[q]][1][:, :, :], w[q][:, :, :], ws[WS[q]][0][:, :, :].bitcast(F32),
                                      ALU.subtract).then_inc(w_low[q], 1)

                def split_down_low(t, q):
                    parts = ws[WS_DOWN[q]]
                    dve.wait_ge(d_high[q], t + 1)
                    dve.tensor_tensor(parts[1][:, :, :], w[NQ + q][:, :, :], parts[0][:, :, :].bitcast(F32),
                                      ALU.subtract).then_inc(d_low[q], 1)

                def x_low_out(t):
                    dve.wait_ge(x_high, t + 1)
                    dve.tensor_tensor(xT[1][:, :, :], px[:, :, :], xT[0][:, :, :].bitcast(F32), ALU.subtract)\
                        .then_inc(x_ready, 1)

                x_low_out(0)
                for q in range(3):
                    split_low(0, q)

                def add_bias(t, q):
                    if q >= 2:
                        dve.wait_ge(h_ready, t * NQ + (q - 1))
                    dve.wait_ge(up_mm, t * NQ + (q + 1))
                    dve.tensor_tensor(hb[q % 2][:, :], pu[q % 2][:, :], b1[:, q * 512:(q + 1) * 512], ALU.add)\
                        .then_inc(biased, 1)

                def hidden_low(t, q):
                    dve.wait_ge(hs_high, t * 2 + (q // 2 + 1))
                    dve.tensor_tensor(hs[1][:, q // 2], ph[q % 2][:, :, :], hs[0][:, q // 2].bitcast(F32), ALU.subtract)\
                        .then_inc(hs_ready, 1)

                def tile(t, very_first=False):
                    e = expert_of(dve, t)
                    dve.wait_ge(b1_in, e * 16 + 16)
                    add_bias(t, 0)
                    add_bias(t, 1)
                    split_low(t, 3)
                    add_bias(t, 2)
                    split_down_low(t, 1)
                    hidden_low(t, 1)
                    add_bias(t, 3)
                    split_down_low(t, 2)
                    hidden_low(t, 2)
                    split_low(t + 1, 1)
                    x_low_out(t + 1)
                    split_low(t + 1, 0)
                    split_low(t + 1, 2)
                    dve.wait_ge(b2_in, e * 16 + 16)
                    dve.wait_ge(down_mm, t * NQ + 2 * NQ)
                    dve.tensor_tensor(yb[:, :], pd[:, :], b2[:, :], ALU.add).then_inc(y_biased, 1)
                    dve.wait_ge(y_biased, t + 1)
                    if not very_first:
                        dve.wait_ge(added, t * 16)
                    at = slice(t, t + 1) if isinstance(t, int) else bass.ds(t, 1)
                    dve.tensor_scalar(y[:, :], yb[:, :], env.slot_weight[:, at], None, ALU.mult).then_inc(y_ready, 1)
                tile(0, True)
                with dve.Fori(1, n_tiles) as t:
                    tile(t)


def combine(nc, env, layer):
    with ExitStack() as cx:
        moe = cx.enter_context(nc.sbuf_tensor(env.name("moe"), [S, B, D], F32))
        sums_in = [env.semaphore(f"sums_in{t}") for t in range(B)]
        acc_done, done, out_done = env.semaphore("acc_done"), env.semaphore("done"), env.semaphore("out_done")
        x, gate = env.x, env.gate[0:S, 2 + layer:3 + layer]
        with nc.Block() as block:
            @block.vector
            def _(dve):
                for t in range(B):
                    dve.scalar_tensor_tensor(out=x[:, t, :], in0=env.acc[:, t, :], scalar=gate, in1=x[:, t, :],
                                             op0=ALU.mult, op1=ALU.add).then_inc(acc_done, 1)
                for t in range(B):
                    dve.wait_ge(sums_in[t], 16)
                    dve.wait_ge(acc_done, t + 1)
                    dve.scalar_tensor_tensor(out=x[:, t, :], in0=moe[:, t, :], scalar=gate, in1=x[:, t, :],
                                             op0=ALU.mult, op1=ALU.add).then_inc(done, 1)

            @block.sync
            def _(sp):
                for t in range(B):
                    sp.dma_start(moe[:, t, :], env.moe_sum[t * S:(t + 1) * S, :]).then_inc(sums_in[t], 16)
                if layer == 1:
                    for t in range(B):
                        sp.wait_ge(done, t + 1)
                        sp.dma_start(env.out[t], x[:, t, :]).then_inc(out_done, 16)
                    sp.wait_ge(out_done, 16 * B)


def program(nc, a, out):
    env = Env()
    count = [0]

    def name(n):
        count[0] += 1
        return f"{n}_{count[0]}"
    env.name = name
    held = []

    def semaphore(n):
        held.append(nc.alloc_semaphore(name(n)))
        return held[-1]
    env.semaphore = semaphore

    def clear_semaphores():
        nc.clear_and_free_semaphores(held)
        held.clear()
        nc.all_engine_barrier()
    env.out = out
    env.ctxT, env.mask = a["ctxT"], a["mask"]
    env.xn_rows = nc.dram_tensor("xn_rows", [TOKEN_ROWS, D], F32).ap()
    env.moe_sums = [nc.dram_tensor(f"moe_sum{l}", [MOE_ROWS, D], F32).ap() for l in range(2)]
    slot_tables = [nc.dram_tensor(f"slot_table{l}", [n, 2], F32).ap()
                   for l, n in enumerate((SLOTS0 + T * K0, SLOTS1))]
    with ExitStack() as cx:
        def sb(n, s, dt=F32):
            return cx.enter_context(nc.sbuf_tensor(n, s, dt))
        env.x, env.xnT, env.ident = sb("x", [S, B, D]), sb("xnT", [P, DC, T]), sb("ident", [P, P])
        env.gate = sb("gate", [P, 4])
        env.tile_expert, env.tile_count = sb("tile_expert", [1, TILES0], I32), sb("tile_count", [1, 2], I32)
        env.tile_ends = sb("tile_ends", [1, E0], I32)
        env.slot_token, env.slot_weight = sb("slot_token", [P, SLOTS0 // P], U32), sb("slot_weight", [P, SLOTS0 // P])

        with nc.semaphore("start_in") as start_in, nc.semaphore("ident_done") as ident_done, \
                nc.semaphore("gate_done") as gate_done, nc.Block() as block:
            @block.sync
            def _(sp):
                sp.dma_start(env.x[:, :, :], a["x"].rearrange("b s d -> s b d")).then_inc(start_in, 16)
                sp.dma_start(env.gate[:, 0:2], a["g_xattn"].broadcast_to([P, 2])).then_inc(start_in, 16)
                sp.dma_start(env.gate[:, 2:4], a["g_ffn"].broadcast_to([P, 2])).then_inc(start_in, 16)
                sp.wait_ge(start_in, 48)

            @block.gpsimd
            def _(pool):
                pool.memset(env.ident[:, :], 0.0).then_inc(ident_done, 1)
                pool.wait_ge(ident_done, 1)
                pool.affine_select(out=env.ident[:, :], in_=env.ident[:, :], compare_op=ALU.not_equal, fill=1.0,
                                   base=0, pattern=[[-1, P]], channel_multiplier=1).then_inc(ident_done, 1)

            @block.scalar
            def _(act):
                act.wait_ge(start_in, 48)
                act.activation(env.gate[:, :], env.gate[:, :], ACT.Tanh).then_inc(gate_done, 1)

        def attend(layer):
            pre = f"l{layer}_"
            attention(nc, env, layer, layer == 0, *(a[pre + n] for n in ("wq", "bq", "wk", "bk", "wv", "bv", "wo", "bo")))

        attend(0)
        with nc.sbuf_tensor("acc0", [S, B, D], F32) as env.acc:
            env.slot_table, env.moe_sum = slot_tables[0], env.moe_sums[0]
            dense_and_route(nc, env, 0, E0, K0, a["l0_gate"], None, a["l0_up"], None, a["l0_down"], None)
            slot_indices(nc, env, SLOTS0 // P)
            experts_swiglu(nc, env, a["l0_eup"], a["l0_edown"])
            combine(nc, env, 0)
        clear_semaphores()
        attend(1)
        with nc.sbuf_tensor("acc1", [S, B, D], F32) as env.acc:
            env.slot_table, env.moe_sum = slot_tables[1], env.moe_sums[1]
            dense_and_route(nc, env, 1, E1, K1, a["l1_gate"], a["l1_gate_b"], a["l1_up"], a["l1_up_b"],
                            a["l1_down"], a["l1_down_b"])
            slot_indices(nc, env, SLOTS1 // P)
            experts_gelu(nc, env, a["l1_ew"], a["l1_eb1"], a["l1_eb2"])
            combine(nc, env, 1)


def lay_out(i):
    def rows(w):
        w = np.asarray(w)
        s = w.shape
        return np.ascontiguousarray(np.moveaxis(w.reshape(*s[:-2], s[-2] // P, P, s[-1]), -3, -2))

    def col(b):
        b = np.asarray(b)
        return np.ascontiguousarray(np.swapaxes(b.reshape(*b.shape[:-1], -1, P), -1, -2))

    def row(b):
        return np.ascontiguousarray(np.asarray(b).reshape(1, -1))
    i = {k: np.asarray(v) for k, v in i.items()}
    o = {"x": i["x"], "ctxT": rows(i["ctx_1024"].transpose(0, 2, 1)), "mask": i["mask_Bx1xSxS2_ik0"].reshape(B, S, SK),
         "g_xattn": row(i["g_xattn"]), "g_ffn": row(i["g_ffn"])}
    for n, m in (("wq", "w_q"), ("wk", "w_k"), ("wv", "w_v"), ("wo", "w_out")):
        o["l0_" + n] = rows(i["L0_xattn_" + m].T)
    for n, m in (("wq", "Wq"), ("wk", "Wk"), ("wv", "Wv"), ("wo", "Wo")):
        o["l1_" + n] = rows(i["L1_xattn_" + m])
    for n, m0, m1 in (("bq", "b_q", "bq"), ("bk", "b_k", "bk"), ("bv", "b_v", "bv")):
        o["l0_" + n], o["l1_" + n] = col(i["L0_xattn_" + m0]), col(i["L1_xattn_" + m1])
    o["l0_bo"], o["l1_bo"] = row(i["L0_xattn_b_out"]), row(i["L1_xattn_bo"])
    o["l0_gate"] = rows(np.concatenate([i["L0_ffn_gate_w"], i["L0_ffn_shared_gate_w"]], 1))
    o["l0_up"], o["l0_down"] = rows(i["L0_ffn_shared_gate_up_w"]), rows(i["L0_ffn_shared_down_w"])
    o["l0_eup"], o["l0_edown"] = rows(i["L0_ffn_expert_gate_up_w"]), rows(i["L0_ffn_expert_down_w"])
    o["l1_gate"], o["l1_gate_b"] = rows(i["L1_ffn_gate_w"]), row(i["L1_ffn_gate_b"])
    o["l1_up"], o["l1_up_b"] = rows(i["L1_ffn_sh_w1"]), col(i["L1_ffn_sh_b1"])
    o["l1_down"], o["l1_down_b"] = rows(i["L1_ffn_sh_w2"]), row(i["L1_ffn_sh_b2"])
    o["l1_eb1"] = i["L1_ffn_eb1"]
    w1 = rows(i["L1_ffn_ew1"]).reshape(E1, P, DC, I1 // 512, 512).transpose(0, 3, 1, 2, 4)
    w2 = rows(i["L1_ffn_ew2"]).reshape(E1, P, I1 // 512, 4, D).transpose(0, 2, 1, 3, 4)
    o["l1_ew"] = np.concatenate([w1, w2], 1)
    o["l1_eb2"] = i["L1_ffn_eb2"]
    return {k: np.ascontiguousarray(v) for k, v in o.items()}


def kernel(**inputs):
    import concourse.bacc as bacc
    from concourse.bass_utils import run_bass_kernel_spmd

    arrays = lay_out(inputs)
    nc = bacc.Bacc("TRN2", target_bir_lowering=False, num_devices=1)
    aps = {n: nc.dram_tensor("in_" + n, v.shape, mybir.dt.from_np(v.dtype), kind="ExternalInput").ap()
           for n, v in arrays.items()}
    out = nc.dram_tensor("out", (B, S, D), F32, kind="ExternalOutput").ap()
    program(nc, aps, out)
    r = run_bass_kernel_spmd(nc, [{"in_" + n: v for n, v in arrays.items()}], core_ids=[0])
    return r.results[0]["out"]
```
